# Optimizing a Trainium2 kernel written in Bass

```python
import numpy as np
import jax
import jax.numpy as jnp

def _softmax(x, axis=-1):
    return jax.nn.softmax(x, axis=axis)

def _gelu(x):
    return jax.nn.gelu(x, approximate=True)

def _silu(x):
    return jax.nn.silu(x)

def _sigmoid(x):
    return jax.nn.sigmoid(x)

def _layernorm(x, axis=-1, eps=1e-05):
    m = jnp.mean(x, axis=axis, keepdims=True)
    v = jnp.var(x, axis=axis, keepdims=True)
    return (x - m) / jnp.sqrt(v + eps)

def _scatter_add(tgt, idx, src, axis=0):
    return tgt.at[idx].add(src)

def _segment_sum(src, seg, n):
    return jax.ops.segment_sum(src, seg, n)
kernel_name = 'mk_decoder_postln_d2_seqx_r8_d11bfd'

def setup_inputs(seed: int=0):
    np.random.seed(seed)
    _w = jnp.asarray

    def _rec_inputs():
        import jax
        import jax.numpy as jnp
        _rk = jax.random.key(seed)
        x = -0.000125 + 0.9999 * jax.random.normal(jax.random.fold_in(_rk, 1), (4, 256, 256), jnp.float32)
        _lenS = 256 - jax.random.randint(jax.random.fold_in(_rk, 7), (4,), 0, max(1, 256 // 4) + 1, jnp.int32)
        _lenS2 = 256 - jax.random.randint(jax.random.fold_in(_rk, 8), (4,), 0, max(1, 256 // 4) + 1, jnp.int32)
        fside_BxS2xS2_0 = -3.05549e-07 + 0.0199987 * jax.random.normal(jax.random.fold_in(_rk, 11), (4, 256, 256), jnp.float32)
        _ctx_1024P = jax.random.normal(jax.random.fold_in(_rk, 12), (4, 16, 128), jnp.float32)
        _ctx_1024c = jax.random.dirichlet(jax.random.fold_in(_rk, 512), 0.3 * jnp.ones((16,), jnp.float32), (4, 256))
        _ctx_1024t = jnp.einsum('bsk,bkd->bsd', _ctx_1024c, _ctx_1024P)
        _ctx_1024t = _ctx_1024t * jax.lax.rsqrt(jnp.mean(jnp.square(_ctx_1024t)) + 1e-12) * 0.953939
        ctx_1024 = 6.82029e-06 + 0.0200006 * (_ctx_1024t + 0.3 * jax.random.normal(jax.random.fold_in(_rk, 612), (4, 256, 128), jnp.float32))
        return (x, fside_BxS2xS2_0, ctx_1024)
    x, fside_BxS2xS2_0, ctx_1024 = _rec_inputs()

    def _L0_attn_setup():
        import jax, jax.numpy as jnp
        import numpy as np
        B, S, D = (2, 256, 256)
        H, KVH = (16, 4)
        HD = D // H
        KVD = KVH * HD
        BASE = 10000.0
        EPS = 1.1920929e-07

        def _rms_norm(t):
            return t * jax.lax.rsqrt(jnp.mean(t * t, axis=-1, keepdims=True) + EPS)

        def _rope_tables(s, dtype):
            inv_freq = 1.0 / BASE ** (jnp.arange(0, HD, 2, dtype=jnp.float32) / HD)
            t = jnp.arange(s, dtype=jnp.float32)
            freqs = jnp.outer(t, inv_freq)
            cos = jnp.cos(freqs)[None, None].astype(dtype)
            sin = jnp.sin(freqs)[None, None].astype(dtype)
            return (cos, sin)

        def _apply_rope(t, cos, sin):
            half = t.shape[-1] // 2
            t1, t2 = (t[..., :half], t[..., half:])
            return jnp.concatenate([t1 * cos + t2 * sin, -t1 * sin + t2 * cos], axis=-1)
        key = jax.random.key(seed)
        ks = jax.random.split(key, 9)
        sd = 1.0 / np.sqrt(D)
        x = jax.random.normal(ks[0], (B, S, D), jnp.float32)
        Wq = jax.random.normal(ks[1], (D, D), jnp.float32) * sd
        bq = jnp.zeros((D,), jnp.float32)
        Wk = jax.random.normal(ks[2], (KVD, D), jnp.float32) * sd
        bk = jnp.zeros((KVD,), jnp.float32)
        Wv = jax.random.normal(ks[3], (KVD, D), jnp.float32) * sd
        bv = jnp.zeros((KVD,), jnp.float32)
        Wo = jax.random.normal(ks[4], (D, D), jnp.float32) * sd
        bo = jnp.zeros((D,), jnp.float32)
        q_gain = jnp.ones((H,), jnp.float32)
        return {'x': x, 'Wq': Wq, 'bq': bq, 'Wk': Wk, 'bk': bk, 'Wv': Wv, 'bv': bv, 'Wo': Wo, 'bo': bo, 'q_gain': q_gain}
    _L0_attn_all = _L0_attn_setup()
    _L0_attn_in = {k: v for k, v in _L0_attn_all.items() if k in ('Wq', 'bq', 'Wk', 'bk', 'Wv', 'bv', 'Wo', 'bo', 'q_gain')}
    del _L0_attn_all

    def _L0_xattn_setup():
        import jax, jax.numpy as jnp
        import numpy as np
        EPS = 1e-06
        QMAX = 127.0

        def _smooth_quant_linear(x, w):
            amax_x = jnp.max(jnp.abs(x), axis=0)
            amax_w = jnp.max(jnp.abs(w), axis=0)
            s = jnp.sqrt(jnp.maximum(amax_x, EPS) / jnp.maximum(amax_w, EPS))
            s = jnp.maximum(s, EPS)
            xs = x / s
            ws = w * s
            x_scale = jnp.maximum(jnp.max(jnp.abs(xs), axis=-1, keepdims=True), EPS) / QMAX
            w_scale = jnp.maximum(jnp.max(jnp.abs(ws), axis=-1, keepdims=True), EPS) / QMAX
            x_q = jnp.clip(jnp.round(xs / x_scale), -QMAX, QMAX)
            w_q = jnp.clip(jnp.round(ws / w_scale), -QMAX, QMAX)
            return x_q @ w_q.T * x_scale * w_scale.T

        def _expert_forward(xe, guw, dw):
            h = _smooth_quant_linear(xe, guw)
            gate, up = jnp.split(h, 2, axis=-1)
            a = jax.nn.silu(gate) * up
            return _smooth_quant_linear(a, dw)
        key = jax.random.key(seed)
        k1, k2, k3 = jax.random.split(key, 3)
        E, T, D, I = (8, 256, 256, 128)
        x = jax.random.normal(k1, (E, T, D), dtype=jnp.float32)
        gate_up_weight = jax.random.normal(k2, (E, 2 * I, D), dtype=jnp.float32) * 0.02
        down_weight = jax.random.normal(k3, (E, D, I), dtype=jnp.float32) * 0.02
        return {'x': x, 'gate_up_weight': gate_up_weight, 'down_weight': down_weight}
    _L0_xattn_all = _L0_xattn_setup()
    _L0_xattn_in = {k: v for k, v in _L0_xattn_all.items() if k in ()}
    del _L0_xattn_all

    def _L0_ffn_setup():
        import jax, jax.numpy as jnp
        import numpy as np
        EPS = 1e-08

        def _bit_quant(w):
            scale = jnp.maximum(jnp.mean(jnp.abs(w)), EPS)
            w_ternary = jnp.clip(jnp.round(w / scale), -1.0, 1.0)
            return w + jax.lax.stop_gradient(w_ternary - w)
        key = jax.random.key(seed)
        k = jax.random.split(key, 5)
        emb, dff = (256, 1024)
        B, S = (4, 256)
        x = jax.random.normal(k[0], (B, S, emb), dtype=jnp.float32)
        w1 = jax.random.normal(k[1], (dff, emb), dtype=jnp.float32) * 0.02
        b1 = jax.random.normal(k[2], (dff,), dtype=jnp.float32) * 0.02
        w2 = jax.random.normal(k[3], (emb, dff), dtype=jnp.float32) * 0.02
        b2 = jax.random.normal(k[4], (emb,), dtype=jnp.float32) * 0.02
        return {'x': x, 'w1': w1, 'b1': b1, 'w2': w2, 'b2': b2}
    _L0_ffn_all = _L0_ffn_setup()
    _L0_ffn_in = {k: v for k, v in _L0_ffn_all.items() if k in ('w1', 'b1', 'w2', 'b2')}
    del _L0_ffn_all

    def _L1_attn_setup():
        import jax, jax.numpy as jnp
        import numpy as np
        import math
        N_HEAD = 16
        WINDOW = 64
        SINK = 4

        def _sliding_window_sink_mask(T, window, sink):
            i = jnp.arange(T)[:, None]
            j = jnp.arange(T)[None, :]
            causal_band = (j <= i) & (j >= i - (window - 1))
            sink_cols = (j < sink) & (j <= i)
            return causal_band | sink_cols
        key = jax.random.key(seed)
        ks = jax.random.split(key, 6)
        B, T, C, L = (2, 256, 256, 64)
        s = 0.02
        return {'x': jax.random.normal(ks[0], (B, T, C), jnp.float32), 'Wq': jax.random.normal(ks[1], (C, C), jnp.float32) * s, 'Wkv_down': jax.random.normal(ks[2], (L, C), jnp.float32) * s, 'Wk_up': jax.random.normal(ks[3], (C, L), jnp.float32) * s, 'Wv_up': jax.random.normal(ks[4], (C, L), jnp.float32) * s, 'Wo': jax.random.normal(ks[5], (C, C), jnp.float32) * s}
    _L1_attn_all = _L1_attn_setup()
    _L1_attn_in = {k: v for k, v in _L1_attn_all.items() if k in ('Wq', 'Wkv_down', 'Wk_up', 'Wv_up', 'Wo')}
    del _L1_attn_all

    def _L1_xattn_setup():
        import jax, jax.numpy as jnp
        import numpy as np
        key = jax.random.key(seed)
        ks = jax.random.split(key, 6)
        B, L, N, C, D = (8, 64, 256, 128, 128)
        return {'teacher_logits': jax.random.normal(ks[0], (B, L, N), dtype=jnp.float32), 'teacher_features': jax.random.normal(ks[1], (B, N, C), dtype=jnp.float32), 'Wq': jax.random.normal(ks[2], (D, C), dtype=jnp.float32) * (1.0 / np.sqrt(C)), 'bq': jnp.zeros((D,), dtype=jnp.float32), 'Wk': jax.random.normal(ks[3], (D, C), dtype=jnp.float32) * (1.0 / np.sqrt(C)), 'bk': jnp.zeros((D,), dtype=jnp.float32)}
    _L1_xattn_all = _L1_xattn_setup()
    _L1_xattn_in = {k: v for k, v in _L1_xattn_all.items() if k in ('Wq', 'bq', 'Wk', 'bk')}
    del _L1_xattn_all

    def _L1_ffn_setup():
        import jax, jax.numpy as jnp
        import numpy as np
        TOP_K = 2
        key = jax.random.key(seed)
        k1, k2, k3, k4 = jax.random.split(key, 4)
        B, S, H, I, E = (2, 128, 256, 176, 8)
        hidden_states = jax.random.normal(k1, (B, S, H), dtype=jnp.float32)
        gate_w = jax.random.normal(k2, (E, H), dtype=jnp.float32) * (1.0 / np.sqrt(H))
        w1 = jax.random.normal(k3, (E, 2 * I, H), dtype=jnp.float32) * (1.0 / np.sqrt(H))
        w2 = jax.random.normal(k4, (E, H, I), dtype=jnp.float32) * (1.0 / np.sqrt(I))
        return {'hidden_states': hidden_states, 'gate_w': gate_w, 'w1': w1, 'w2': w2}
    _L1_ffn_all = _L1_ffn_setup()
    _L1_ffn_in = {k: v for k, v in _L1_ffn_all.items() if k in ('gate_w', 'w1', 'w2')}
    del _L1_ffn_all
    return {'x': x, 'fside_BxS2xS2_0': fside_BxS2xS2_0, 'ctx_1024': ctx_1024, 'L0_attn_Wq': _L0_attn_in['Wq'], 'L0_attn_bq': _L0_attn_in['bq'], 'L0_attn_Wk': _L0_attn_in['Wk'], 'L0_attn_bk': _L0_attn_in['bk'], 'L0_attn_Wv': _L0_attn_in['Wv'], 'L0_attn_bv': _L0_attn_in['bv'], 'L0_attn_Wo': _L0_attn_in['Wo'], 'L0_attn_bo': _L0_attn_in['bo'], 'L0_attn_q_gain': _L0_attn_in['q_gain'], 'L0_ffn_w1': _L0_ffn_in['w1'], 'L0_ffn_b1': _L0_ffn_in['b1'], 'L0_ffn_w2': _L0_ffn_in['w2'], 'L0_ffn_b2': _L0_ffn_in['b2'], 'L1_attn_Wq': _L1_attn_in['Wq'], 'L1_attn_Wkv_down': _L1_attn_in['Wkv_down'], 'L1_attn_Wk_up': _L1_attn_in['Wk_up'], 'L1_attn_Wv_up': _L1_attn_in['Wv_up'], 'L1_attn_Wo': _L1_attn_in['Wo'], 'L1_xattn_Wq': _L1_xattn_in['Wq'], 'L1_xattn_bq': _L1_xattn_in['bq'], 'L1_xattn_Wk': _L1_xattn_in['Wk'], 'L1_xattn_bk': _L1_xattn_in['bk'], 'L1_ffn_gate_w': _L1_ffn_in['gate_w'], 'L1_ffn_w1': _L1_ffn_in['w1'], 'L1_ffn_w2': _L1_ffn_in['w2']}

def reference(x, fside_BxS2xS2_0, ctx_1024, L0_attn_Wq, L0_attn_bq, L0_attn_Wk, L0_attn_bk, L0_attn_Wv, L0_attn_bv, L0_attn_Wo, L0_attn_bo, L0_attn_q_gain, L0_ffn_w1, L0_ffn_b1, L0_ffn_w2, L0_ffn_b2, L1_attn_Wq, L1_attn_Wkv_down, L1_attn_Wk_up, L1_attn_Wv_up, L1_attn_Wo, L1_xattn_Wq, L1_xattn_bq, L1_xattn_Wk, L1_xattn_bk, L1_ffn_gate_w, L1_ffn_w1, L1_ffn_w2):
    import jax
    import jax.numpy as jnp

    def _L0_attn_ref(x, Wq, bq, Wk, bk, Wv, bv, Wo, bo, q_gain):
        import jax, jax.numpy as jnp
        import numpy as np
        B, S, D = (2, 256, 256)
        H, KVH = (16, 4)
        HD = D // H
        KVD = KVH * HD
        BASE = 10000.0
        EPS = 1.1920929e-07

        def _rms_norm(t):
            return t * jax.lax.rsqrt(jnp.mean(t * t, axis=-1, keepdims=True) + EPS)

        def _rope_tables(s, dtype):
            inv_freq = 1.0 / BASE ** (jnp.arange(0, HD, 2, dtype=jnp.float32) / HD)
            t = jnp.arange(s, dtype=jnp.float32)
            freqs = jnp.outer(t, inv_freq)
            cos = jnp.cos(freqs)[None, None].astype(dtype)
            sin = jnp.sin(freqs)[None, None].astype(dtype)
            return (cos, sin)

        def _apply_rope(t, cos, sin):
            half = t.shape[-1] // 2
            t1, t2 = (t[..., :half], t[..., half:])
            return jnp.concatenate([t1 * cos + t2 * sin, -t1 * sin + t2 * cos], axis=-1)
        b, s, d = x.shape
        q = (jnp.einsum('bsd,ed->bse', x, Wq) + bq).reshape(b, s, H, HD).transpose(0, 2, 1, 3)
        k = (jnp.einsum('bsd,ed->bse', x, Wk) + bk).reshape(b, s, KVH, HD).transpose(0, 2, 1, 3)
        v = (jnp.einsum('bsd,ed->bse', x, Wv) + bv).reshape(b, s, KVH, HD).transpose(0, 2, 1, 3)
        q = _rms_norm(q)
        k = _rms_norm(k)
        cos, sin = _rope_tables(s, q.dtype)
        q = _apply_rope(q, cos, sin)
        k = _apply_rope(k, cos, sin)
        q = q * q_gain[None, :, None, None]
        rep = H // KVH
        k = jnp.repeat(k, rep, axis=1)
        v = jnp.repeat(v, rep, axis=1)
        scale = HD ** (-0.5)
        attn = jnp.einsum('bhqd,bhkd->bhqk', q * scale, k)
        causal = jnp.tril(jnp.ones((s, s), dtype=bool))
        attn = jnp.where(causal[None, None], attn, -jnp.inf)
        attn = jax.nn.softmax(attn, axis=-1)
        out = jnp.einsum('bhqk,bhkd->bqhd', attn, v).reshape(b, s, d)
        return jnp.einsum('bsd,ed->bse', out, Wo) + bo

    def _L0_xattn_ref(x, gate_up_weight, down_weight):
        import jax, jax.numpy as jnp
        import numpy as np
        EPS = 1e-06
        QMAX = 127.0

        def _smooth_quant_linear(x, w):
            amax_x = jnp.max(jnp.abs(x), axis=0)
            amax_w = jnp.max(jnp.abs(w), axis=0)
            s = jnp.sqrt(jnp.maximum(amax_x, EPS) / jnp.maximum(amax_w, EPS))
            s = jnp.maximum(s, EPS)
            xs = x / s
            ws = w * s
            x_scale = jnp.maximum(jnp.max(jnp.abs(xs), axis=-1, keepdims=True), EPS) / QMAX
            w_scale = jnp.maximum(jnp.max(jnp.abs(ws), axis=-1, keepdims=True), EPS) / QMAX
            x_q = jnp.clip(jnp.round(xs / x_scale), -QMAX, QMAX)
            w_q = jnp.clip(jnp.round(ws / w_scale), -QMAX, QMAX)
            return x_q @ w_q.T * x_scale * w_scale.T

        def _expert_forward(xe, guw, dw):
            h = _smooth_quant_linear(xe, guw)
            gate, up = jnp.split(h, 2, axis=-1)
            a = jax.nn.silu(gate) * up
            return _smooth_quant_linear(a, dw)
        return jax.vmap(_expert_forward)(x, gate_up_weight, down_weight)

    def _L0_ffn_ref(x, w1, b1, w2, b2):
        import jax, jax.numpy as jnp
        import numpy as np
        EPS = 1e-08

        def _bit_quant(w):
            scale = jnp.maximum(jnp.mean(jnp.abs(w)), EPS)
            w_ternary = jnp.clip(jnp.round(w / scale), -1.0, 1.0)
            return w + jax.lax.stop_gradient(w_ternary - w)
        w1q = _bit_quant(w1)
        w2q = _bit_quant(w2)
        h = jnp.einsum('bsd,fd->bsf', x, w1q) + b1
        h = jax.nn.gelu(h, approximate=False)
        return jnp.einsum('bsf,df->bsd', h, w2q) + b2

    def _L1_attn_ref(x, Wq, Wkv_down, Wk_up, Wv_up, Wo):
        import jax, jax.numpy as jnp
        import numpy as np
        import math
        N_HEAD = 16
        WINDOW = 64
        SINK = 4

        def _sliding_window_sink_mask(T, window, sink):
            i = jnp.arange(T)[:, None]
            j = jnp.arange(T)[None, :]
            causal_band = (j <= i) & (j >= i - (window - 1))
            sink_cols = (j < sink) & (j <= i)
            return causal_band | sink_cols
        B, T, C = x.shape
        H = N_HEAD
        hd = C // H
        q = (x @ Wq.T).reshape(B, T, H, hd).transpose(0, 2, 1, 3)
        latent = x @ Wkv_down.T
        k = (latent @ Wk_up.T).reshape(B, T, H, hd).transpose(0, 2, 1, 3)
        v = (latent @ Wv_up.T).reshape(B, T, H, hd).transpose(0, 2, 1, 3)
        att = jnp.einsum('bhqd,bhkd->bhqk', q, k) / math.sqrt(hd)
        mask = _sliding_window_sink_mask(T, WINDOW, SINK)
        att = jnp.where(mask[None, None], att, -jnp.inf)
        att = jax.nn.softmax(att, axis=-1)
        y = jnp.einsum('bhqk,bhkd->bhqd', att, v)
        y = y.transpose(0, 2, 1, 3).reshape(B, T, C)
        return y @ Wo.T

    def _L1_xattn_ref(teacher_logits, teacher_features, Wq, bq, Wk, bk):
        import jax, jax.numpy as jnp
        import numpy as np
        query = jnp.einsum('bnc,dc->bnd', teacher_features, Wq) + bq
        key = jnp.einsum('bnc,dc->bnd', teacher_features, Wk) + bk
        energy = jnp.einsum('bnd,bmd->bnm', query, key)
        attention = jax.nn.softmax(energy, axis=-1)
        x_m = jnp.einsum('bln,bmn->blm', teacher_logits, attention)
        return x_m

    def _L1_ffn_ref(hidden_states, gate_w, w1, w2):
        import jax, jax.numpy as jnp
        import numpy as np
        TOP_K = 2
        B, S, H = hidden_states.shape
        E = gate_w.shape[0]
        T = B * S
        x = hidden_states.reshape(T, H)
        logits = jnp.einsum('th,eh->te', x, gate_w)
        probs = jax.nn.softmax(logits, axis=-1)
        topw, sel = jax.lax.top_k(probs, TOP_K)
        topw = topw / jnp.sum(topw, axis=-1, keepdims=True)
        combine = jnp.zeros((T, E), dtype=x.dtype).at[jnp.arange(T)[:, None], sel].add(topw)
        gate_up = jnp.einsum('th,eoh->eto', x, w1)
        g, u = jnp.split(gate_up, 2, axis=-1)
        act = jax.nn.silu(g) * u
        expert_out = jnp.einsum('eti,ehi->eth', act, w2)
        out = jnp.einsum('eth,te->th', expert_out, combine)
        return out.reshape(B, S, H)
    x = _layernorm(x + _L0_attn_ref(x, L0_attn_Wq, L0_attn_bq, L0_attn_Wk, L0_attn_bk, L0_attn_Wv, L0_attn_bv, L0_attn_Wo, L0_attn_bo, L0_attn_q_gain), axis=-1)
    x = _layernorm(x + _L0_xattn_ref(x, fside_BxS2xS2_0, ctx_1024), axis=-1)
    x = _layernorm(x + _L0_ffn_ref(x, L0_ffn_w1, L0_ffn_b1, L0_ffn_w2, L0_ffn_b2), axis=-1)
    x = _layernorm(x + _L1_attn_ref(x, L1_attn_Wq, L1_attn_Wkv_down, L1_attn_Wk_up, L1_attn_Wv_up, L1_attn_Wo), axis=-1)
    x = _layernorm(x + _L1_xattn_ref(x, ctx_1024, L1_xattn_Wq, L1_xattn_bq, L1_xattn_Wk, L1_xattn_bk), axis=-1)
    x = _layernorm(x + _L1_ffn_ref(x, L1_ffn_gate_w, L1_ffn_w1, L1_ffn_w2), axis=-1)
    return x

_drawn_inputs = setup_inputs


def setup_inputs(seed=0):
    import zlib

    import numpy as np

    out = dict(_drawn_inputs(seed))
    spreads = {'L0_attn_bq': (0.0, 0.1),
     'L0_attn_bk': (0.0, 0.1),
     'L0_attn_bv': (0.0, 0.1),
     'L0_attn_bo': (0.0, 0.1),
     'L0_attn_q_gain': (1.0, 0.2),
     'L1_xattn_bq': (0.0, 0.8),
     'L1_xattn_bk': (0.0, 2.0)}
    factors = {'L0_ffn_b1': 12.733,
     'L0_ffn_b2': 48.379,
     'L1_attn_Wq': 26.867,
     'L1_attn_Wk_up': 26.939,
     'L1_xattn_Wq': 8.0,
     'L1_xattn_Wk': 8.0,
     'L1_attn_Wkv_down': 2.668}
    for name, (base, spread) in spreads.items():
        noise = np.random.default_rng([zlib.crc32(name.encode()), seed]).standard_normal(out[name].shape)
        drawn = base * np.exp(spread * noise) if base else spread * noise
        out[name] = jnp.asarray(drawn.astype(out[name].dtype))
    for name, factor in factors.items():
        out[name] = (out[name] * factor).astype(out[name].dtype)
    return out
```

```python
import concourse.bass as bass
from concourse import mybir
from contextlib import ExitStack

STAGES = 6


def post_ln_decoder_two_layers(nc: bass.Bass, t: dict, out: bass.AP):
    F32 = mybir.dt.float32
    BF16 = mybir.dt.bfloat16
    I32 = mybir.dt.int32
    ALU = mybir.AluOpType
    ACT = mybir.ActivationFunctionType
    X = mybir.AxisListType.X

    P = 128
    B, S, D = t["x"].shape
    TT = B * S // P
    DC = D // P
    H, HD = 16, 16
    KV0 = t["L0_attn_Wk"].shape[0] // HD
    KVH = [KV0, H]
    HG = 4
    NG = H // HG
    PIECES = 6
    STK = PIECES * HD
    MROW = STK
    FF = t["L0_ffn_w1"].shape[0]
    FCH = FF // P
    LAT = t["L1_attn_Wkv_down"].shape[0]
    CX = t["ctx_1024"].shape[2]
    E = t["L1_ffn_gate_w"].shape[0]
    EI = t["L1_ffn_w2"].shape[2]
    IB = P // E
    EC = EI // IB
    NEG_SCALE = float(HD) ** -0.5
    LN_EPS = 1e-5
    RMS_EPS = 1.1920929e-07
    Q_EPS = 1e-6
    MAGIC = 12582912.0
    RSQRT_SEED = 0x5F3759DF

    with ExitStack() as ctx:
        def sb(name, shape, dt=F32):
            return ctx.enter_context(nc.sbuf_tensor(name, shape, dt))

        def sem(name):
            return ctx.enter_context(nc.semaphore(name))

        PS = ctx.enter_context(nc.psum_tensor("PS", [P, 8, 512], F32))

        def bank(i, cols=512, off=0, rows=P):
            return PS[0:rows, i, off:off + cols]

        def bank16(i, cols=1024, off=0, rows=P):
            return PS[0:rows, i, :].bitcast(BF16)[:, off:off + cols]

        x = sb("x", [P, TT, D])
        xb = sb("xb", [P, TT, D])
        xT = sb("xT", [P, DC, B * S])
        ident = sb("ident", [P, P])
        ident16 = sb("ident16", [P, P], BF16)
        ones = sb("ones", [P, P])
        stat = sb("stat", [P, 2, 2, 6])
        mv = sb("mv", [P, 2, 2, 2])
        va = sb("va", [P, 2])
        rstd = sb("rstd", [P, 2, 2])
        nt = sb("nt", [P, 2])
        res = sb("res", [P, 2, 2, D])

        wqkvT = sb("wqkvT", [P, DC, D + 2 * KV0 * HD])
        woT = [sb("woT0", [P, DC, D]), sb("woT1", [P, DC, D])]
        bqkv = sb("bqkv", [P, D + 2 * KV0 * HD])
        bo = sb("bo", [P, D])
        gain = sb("gain", [P, H])
        rope = sb("rope", [P, 2, 2, HD])
        masks = sb("masks", [P, 2, 6 * P], BF16)
        wqT1 = sb("wqT1", [P, DC, D])
        wdT = sb("wdT", [P, DC, LAT])
        wupT = sb("wupT", [LAT, 2 * D])
        b1 = sb("b1", [P, FCH])
        b2 = sb("b2", [P, D])
        xwT = sb("xwT", [P, 2, CX])
        xbias = sb("xbias", [P, 2])
        ctxT = sb("ctxT", [P, B, S])
        attT = sb("attT", [P, B, 2, S])
        gwT = sb("gwT", [P, DC, E])
        order = sb("order", [P, E])

        ARENA = 25600
        arena = sb("arena", [P, ARENA])

        def carve(off, shape, dt=F32):
            n = 1
            for k in shape[1:]:
                n *= k
            words = n if dt == F32 else n // 2
            assert off + words <= ARENA, (off, shape)
            v = arena[0:shape[0], off:off + words]
            if dt != F32:
                v = v.bitcast(dt)
            names = "abcdef"[:len(shape) - 1]
            if len(shape) > 2:
                v = v.rearrange(f"p ({' '.join(names)}) -> p {' '.join(names)}",
                                **{names[i]: shape[i + 1] for i in range(len(shape) - 1)})
            return v

        Qh = carve(0, [P, B, H, S], BF16)
        Kh = carve(8192, [P, B, H, S], BF16)
        qst = carve(16384, [P, 2, 2 * H * STK], BF16)
        kst = carve(19456, [P, 2, 2 * H * STK], BF16)
        V1 = sb("V1", [P, TT, H, HD + 1])
        rem = carve(22528, [P, 2, 2 * 2 * H * HD])
        PT = sb("PT", [P, 2, 3 * 512])
        on = sb("on", [P, 2, 2, D])
        OT = sb("OT", [P, 2, DC, S])
        att_words = attT[:, :, :, :].rearrange("p a b c -> p (a b c)")
        qk = att_words[:, 0:1280].rearrange("p (a b c) -> p a b c", a=2, b=2)
        qsq = att_words[:, 1280:1920].rearrange("p (a b) -> p a b", a=2)
        qro = sb("qro", [P, 2, (H + KV0) * HD])
        qss = sb("qss", [P, 2 * (H + KV0)])
        qrs = sb("qrs", [P, 2 * (H + KV0)])
        qnt = sb("qnt", [P, 2 * (H + KV0)])
        latT = xb[0:LAT, 0:4, :].rearrange("p a b -> p (a b)")
        mx = sb("mx", [P, 2, 2, H])
        mxr = sb("mxr", [P, 2, 2, H])
        mst = sb("mst", [P, 2, 2, 3, H], BF16)
        mT = sb("mT", [3 * H, 2, S], BF16)
        rsum = sb("rsum", [P, 2, 2, HG])

        f_nat = carve(0, [P, B, 2, D])
        c_nat = carve(2048, [P, B, 2, CX])
        w1n = carve(3072, [P, FCH, D])
        w2n = carve(5120, [P, DC, FF])
        tmpw = carve(7168, [P, 2, 2048], BF16)
        w1t = carve(9216, [P, FCH, D], BF16)
        w2t = carve(10240, [P, DC, FF], BF16)
        wq1n = carve(11264, [P, DC, D])
        wo1n = carve(11776, [P, DC, D])
        wdn = carve(12288, [LAT, D])
        wkun = carve(12544, [P, 2, DC, LAT])
        xwn = carve(12800, [P, 2, CX])
        gwn = carve(13056, [E, D])
        m1n = carve(16384, [P, 2, EC, D])
        m2n = carve(22016, [P, DC, E * EI])
        mw1T = carve(0, [P, DC, 2, EC * P])
        mw2T = carve(5632, [P, EC, D])
        fT = carve(19456, [P, B, DC, S])
        xqk = carve(21760, [P, 2, B * S])
        xP = carve(23808, [P, 2, 2, S])
        wq0n = carve(0, [P, DC + 1, D])
        wo0n = carve(768, [P, DC, D])
        xmx = sb("xmx", [P, 2, 2])
        xsm = sb("xsm", [P, 2, 2])
        tsum = sb("tsum", [P, 2])
        tthr = sb("tthr", [P, 2, 2])

        amx = sb("amx", [P, 2, B * DC])
        qs = sb("qs", [P, 4, B * DC])
        xw = carve(0, [P, B, 2, DC, S])
        q32 = carve(8192, [P, 2, 4, D])
        q16 = carve(10240, [P, 2, 4, D], BF16)
        qT = carve(11264, [P, B, 2, DC, S], BF16)
        rsc = sb("rsc", [P, B, 4])
        rrq = sb("rrq", [P, B, 4])
        wbc = carve(15360, [P, 2, D])
        hh = carve(15872, [P, 2, 2, D])
        sg = carve(16896, [P, 2, 2, D // 2])
        aa = carve(17408, [P, B, 2, D // 2])
        aT = carve(18432, [P, B, S])
        xw2 = carve(0, [P, B, 2, S])
        y2 = carve(21504, [P, 2, 2, D])

        x3 = carve(0, [P, 3, DC, B * S], BF16)
        xrem = carve(3072, [P, 2, DC, S])
        hT = carve(4096, [P, FCH, B * S])
        w1T = carve(22528, [P, DC, FF], BF16)
        w2T = carve(23552, [P, FCH, D])

        gl = sb("gl", [P, TT, E])
        gp = sb("gp", [P, TT, E])
        gq = sb("gq", [P, TT, E])
        gr = sb("gr", [P, TT, E])
        oh = sb("oh", [P, 2, TT, E])
        g1 = sb("g1", [P, 6, TT])
        GB = carve(8448, [P, B * S])
        sgm = carve(9472, [P, 2, 512])
        um = carve(10496, [P, 2, 512])
        am = carve(11520, [P, 2, 512])
        combw = carve(12544, [P, TT, E, IB])

        x_loaded = sem("x_loaded")
        w_loaded = {k: sem(f"{k}_loaded") for k in
                    ("const", "l0", "f", "c", "w1", "w2", "l1", "xw", "gate", "m1", "m2")}
        bias_loaded = sem("bias_loaded")
        ones_set = sem("ones_set")
        krow_set = sem("krow_set")
        wt_done = sem("wt_transposed")
        wt_act = sem("wt_evacuated_by_act")
        wt_dve = sem("wt_evacuated_by_dve")
        v_step = sem("v_step")
        a_step = sem("a_step")
        p_step = sem("p_step")
        xtr_done = sem("x_transposed")
        xT_ready = sem("xT_ready")
        x_normed = sem("x_normed")
        out_read = sem("out_read")
        y_done = sem("y_done")
        xb_ready = sem("xb_ready")
        stored = sem("stored")
        abs_sum = sem("abs_sum")
        abs_tot = sem("abs_tot")
        thr_ready = sem("thr_ready")
        low_ready = sem("low_ready")
        tern_ready = sem("tern_ready")
        A = [{k: sem(f"l{L}_{k}") for k in
              ("proj", "proj_read", "lat", "lat_ready", "v_ready", "hi", "rem", "mid", "lo", "stk_tr",
               "sq", "ev_act", "ev_dve", "smax", "mx", "mst", "mtr", "mT", "mrow", "sT", "pT", "av", "on",
               "otr", "OT")} for L in range(2)]
        Q = {k: sem(f"q_{k}") for k in
             ("xw", "nat", "q32", "q16", "qtr", "qT", "h", "wtr", "wbc", "hh", "sg", "aa", "atr", "aT",
              "xw2", "nat2", "q32b", "q16b", "qtr2", "qT2", "wtr2", "wbc2")}
        Fs = {k: sem(f"f_{k}") for k in ("hi", "rem", "mid", "lo", "up", "gelu", "b")}
        Xs = {k: sem(f"x_{k}") for k in ("proj", "qk", "en", "mx", "exp", "norm", "tr", "attT")}
        Ms = {k: sem(f"m_{k}") for k in ("logit", "lg", "exp", "comb", "ctr", "GB", "gu", "sg", "um", "am")}

        G = []

        def group(srcs, dst, rows, cols, half, need):
            G.append((srcs, dst, rows, cols, half, need))

        for dc in range(DC):
            group([wq0n[:, r, dc * P:(dc + 1) * P] for r in range(3)], wqkvT[:, dc, :], P, 384, False, "l0")
        for w, n in ((wo0n, 0),):
            group([w[:, r, dc * P:(dc + 1) * P] for dc in range(DC) for r in range(2)],
                  woT[n][:, :, :].rearrange("p a b -> p (a b)"), P, 512, False, "l0")
        NG0 = len(G)
        for b in range(B):
            group([f_nat[:, b, r, dc * P:(dc + 1) * P] for dc in range(DC) for r in range(2)],
                  fT[:, b, :, :].rearrange("p a b -> p (a b)"), P, 512, False, "f")
        for b in range(0, B, 2):
            group([c_nat[:, b + k, r, :] for k in range(2) for r in range(2)],
                  ctxT[:, b:b + 2, :].rearrange("p a b -> p (a b)"), P, 512, False, "c")
        group([xwn[:, k, :] for k in range(2)], xwT[:, :, :].rearrange("p a b -> p (a b)"), P, 256, False, "xw")
        NGX = len(G)
        for dc in range(DC):
            group([w1t[:, f, dc * P:(dc + 1) * P] for f in range(FCH)], w1T[:, dc, :], P, 1024, True, "t1")
        for k in range(2):
            group([w2t[:, r, f * P:(f + 1) * P] for f in range(4 * k, 4 * k + 4) for r in range(2)],
                  w2T[:, 4 * k:4 * k + 4, :].rearrange("p a b -> p (a b)"), P, 1024, True, "t2")
        group([wq1n[:, r, dc * P:(dc + 1) * P] for dc in range(DC) for r in range(2)],
              wqT1[:, :, :].rearrange("p a b -> p (a b)"), P, 512, False, "l1")
        group([wo1n[:, r, dc * P:(dc + 1) * P] for dc in range(DC) for r in range(2)],
              woT[1][:, :, :].rearrange("p a b -> p (a b)"), P, 512, False, "l1")
        group([wdn[:, dc * P:(dc + 1) * P] for dc in range(DC)],
              wdT[:, :, :].rearrange("p a b -> p (a b)"), P, DC * LAT, False, "l1")
        group([wkun[:, k, r, :] for k in range(2) for r in range(2)], wupT[:, :], LAT, 512, False, "l1")
        group([gwn[:, dc * P:(dc + 1) * P] for dc in range(DC)],
              gwT[:, :, :].rearrange("p a b -> p (a b)"), P, DC * E, False, "gate")
        NGM = len(G)
        for dc in range(DC):
            for gu in range(2):
                for c0 in range(0, EC, 4):
                    n = min(4, EC - c0)
                    group([m1n[:, gu, c, dc * P:(dc + 1) * P] for c in range(c0, c0 + n)],
                          mw1T[:, dc, gu, c0 * P:(c0 + n) * P], P, n * P, False, "m1")
        for c0 in range(0, EC, 2):
            n = min(2, EC - c0)
            group([m2n[:, r, c::EC] for c in range(c0, c0 + n) for r in range(2)],
                  mw2T[:, c0:c0 + n, :].rearrange("p a b -> p (a b)"), P, n * 256, False, "m2")

        LOADS = {"l0": 16 * 4, "f": 16, "c": 16, "w1": 16, "w2": 16, "l1": 16 * 5, "xw": 32, "gate": 16,
                 "m1": 16 * 16, "m2": 32, "const": 16 * 5}

        def pe_groups(pe, lo, hi):
            for k in range(lo, hi):
                srcs, dst, rows, cols, half, need = G[k]
                if need == "t1":
                    pe.wait_ge(tern_ready, 1)
                elif need == "t2":
                    pe.wait_ge(tern_ready, 2)
                else:
                    pe.wait_ge(w_loaded[need], LOADS[need])
                if k >= 4:
                    pe.wait_ge(wt_dve if k % 2 else wt_act, (k - 4) // 2 + 1)
                w = cols // len(srcs)
                for i, s in enumerate(srcs):
                    K = s.shape[0]
                    o = (bank16 if half else bank)(k % 4, w, i * w, rows)
                    last = nc.tensor.transpose(o, s, (ident16 if half else ident)[0:K, 0:K])
                last.then_inc(wt_done, 1)

        def evac_groups(eng, copy, lo, hi, odd):
            for k in range(lo, hi):
                if k % 2 != odd:
                    continue
                srcs, dst, rows, cols, half, need = G[k]
                eng.wait_ge(wt_done, k + 1)
                copy(dst, (bank16 if half else bank)(k % 4, cols, 0, rows)).then_inc(wt_dve if odd else wt_act, 1)

        def late_loads(sp):
            w = w_loaded
            sp.wait_ge(A[0]["pT"], B * NG)
            sp.dma_start(f_nat.rearrange("p b r d -> p (b r) d"),
                         t["fside_BxS2xS2_0"].rearrange("b (r p) d -> p (b r) d", p=P)).then_inc(w["f"], 16)
            sp.dma_start(c_nat.rearrange("p b r d -> p (b r) d"),
                         t["ctx_1024"].rearrange("b (r p) d -> p (b r) d", p=P)).then_inc(w["c"], 16)
            sp.dma_start(xwn[:, 0, :], t["L1_xattn_Wq"]).then_inc(w["xw"], 16)
            sp.dma_start(xwn[:, 1, :], t["L1_xattn_Wk"]).then_inc(w["xw"], 16)
            sp.dma_start(w1n, t["L0_ffn_w1"].rearrange("(r p) d -> p r d", p=P)).then_inc(w["w1"], 16)
            sp.dma_start(w2n, t["L0_ffn_w2"].rearrange("(r p) d -> p r d", p=P)).then_inc(w["w2"], 16)
            sp.dma_start(wq1n, t["L1_attn_Wq"].rearrange("(r p) d -> p r d", p=P)).then_inc(w["l1"], 16)
            sp.dma_start(wo1n, t["L1_attn_Wo"].rearrange("(r p) d -> p r d", p=P)).then_inc(w["l1"], 16)
            sp.dma_start(wdn, t["L1_attn_Wkv_down"]).then_inc(w["l1"], 16)
            sp.dma_start(wkun[:, 0, :, :], t["L1_attn_Wk_up"].rearrange("(r p) d -> p r d", p=P)).then_inc(w["l1"], 16)
            sp.dma_start(wkun[:, 1, :, :], t["L1_attn_Wv_up"].rearrange("(r p) d -> p r d", p=P)).then_inc(w["l1"], 16)
            sp.dma_start(gwn, t["L1_ffn_gate_w"]).then_inc(w["gate"], 16)

        def expert_loads(sp):
            w = w_loaded
            sp.wait_ge(A[1]["stk_tr"], B * TG[1])
            sp.wait_ge(A[1]["lo"], TT)
            for e in range(E):
                for gu in range(2):
                    src = t["L1_ffn_w1"][e, gu * EI:(gu + 1) * EI, :].rearrange("(i c) d -> i c d", c=EC)
                    sp.dma_start(m1n[e * IB:(e + 1) * IB, gu, :, :], src).then_inc(w["m1"], 16)
            for r in range(2):
                sp.dma_start(m2n[:, r, :].rearrange("p (e i) -> p e i", e=E), t["L1_ffn_w2"][:, r * P:(r + 1) * P, :].rearrange("e h i -> h e i")).then_inc(w["m2"], 16)

        def mrow_dmas(sp, L):
            for b in range(B):
                sp.wait_ge(A[L]["mT"], b + 1)
                for k in range(3):
                    sp.dma_start(Qh[MROW + k:MROW + k + 1, b, :, :],
                                 mT[k * H:(k + 1) * H, b % 2, :]).then_inc(A[L]["mrow"], 16)


        am_read = sem("am_read")

        Q_SLOTS = {"hi": (0, 3, 1), "mid": (3, 5, 1), "lo": (5, 6, 1)}
        K_SLOTS = {"hi": (1, 6, 2), "mid": (2, 5, 2), "lo": (0, 1, 1)}

        def stack(L, u, which, part):
            nh = (2 * H if which == "q" else 2 * KVH[0]) if L == 0 else H
            buf = (qst if which == "q" else kst)[:, u % 2, 0:nh * STK].rearrange("p (h s d) -> p h s d", h=nh, s=PIECES)
            lo, hi, st = (Q_SLOTS if which == "q" else K_SLOTS)[part]
            return buf[:, :, lo:hi:st, :]

        def part_source(L, u, which):
            if L == 0:
                v = qro[:, :, :] if which == "q" else qro[:, :, :]
                a = qro[:, :, 0:D] if which == "q" else qro[:, :, D:D + KV0 * HD]
                return a.rearrange("p t (h d) -> p t h d", d=HD)
            o = 0 if which == "q" else D
            return bank(2 * (u % 2), D, o).rearrange("p (h d) -> p h d", d=HD)

        def remainder(L, u, which):
            nh = (2 * H if which == "q" else 2 * KVH[0]) if L == 0 else H
            o = 0 if which == "q" else 2 * H * HD
            return rem[:, u % 2, o:o + nh * HD].rearrange("p (h d) -> p h d", d=HD)

        def stack_views(L, u, part):
            res_ = []
            for which in "qk":
                dst = stack(L, u, which, part)
                src = remainder(L, u, which)
                n = dst.shape[2]
                res_.append((src.unsqueeze(2).to_broadcast([P, dst.shape[1], n, HD]), dst))
            return res_

        def tr_groups(L, b):
            gs = []
            for which, nh, dst in (("k", KVH[L], Kh), ("q", H, Qh)):
                for g in range(nh // HG):
                    srcs = []
                    for h in range(HG * g, HG * g + HG):
                        for half in range(2):
                            if L == 0:
                                full = 2 * nh
                                buf = (qst if which == "q" else kst)[:, b % 2, 0:full * STK].rearrange(
                                    "p (t h s) -> p t h s", t=2, h=nh)
                                srcs.append(buf[:, half, h, :])
                            else:
                                buf = (qst if which == "q" else kst)[:, half, 0:nh * STK].rearrange(
                                    "p (h s) -> p h s", h=nh)
                                srcs.append(buf[:, h, :])
                    gs.append((srcs, dst[0:STK, b, HG * g:HG * g + HG, :].rearrange("p a b -> p (a b)")))
            return gs

        TG = [KVH[L] // HG + NG for L in range(2)]


        bias_b1 = sem("b1_loaded")

        y_ready = sem("y_ready")

        def quant_transposes(pe, b):
            pe.wait_ge(Q["q16"], b + 1)
            if b >= 2:
                pe.wait_ge(Q["qT"], b - 1)
            for i in range(4):
                for c in range(DC):
                    last = nc.tensor.transpose(bank16(4 + b % 2, P, ((i // 2) * DC + c) * S + (i % 2) * P),
                                               q16[:, b % 2, i, c * P:(c + 1) * P], ident16[:, :])
            last.then_inc(Q["qtr"], 1)

        def quant_transposes2(pe, b):
            pe.wait_ge(Q["q16b"], b + 1)
            if b >= 2:
                pe.wait_ge(Q["qT2"], b - 1)
            for i in range(4):
                last = nc.tensor.transpose(bank16(4 + b % 2, P, i * P), q16[:, b % 2, i, 0:CX], ident16[:, :])
            last.then_inc(Q["qtr2"], 1)

        block = ctx.enter_context(nc.Block())

        @block.sync
        def _(sp):
            w = w_loaded
            xv = t["x"].rearrange("b (h p) d -> p (b h) d", p=P)
            sp.dma_start(ident[:, :], t["ident"]).then_inc(w["const"], 16)
            sp.dma_start(x[:, 0:2, :], xv[:, 0:2, :]).then_inc(x_loaded, 16)
            sp.dma_start(wq0n[:, 0:2, :], t["L0_attn_Wq"].rearrange("(r p) d -> p r d", p=P)).then_inc(w["l0"], 16)
            sp.dma_start(wq0n[0:64, 2, :], t["L0_attn_Wk"]).then_inc(w["l0"], 16)
            sp.dma_start(wq0n[64:128, 2, :], t["L0_attn_Wv"]).then_inc(w["l0"], 16)
            sp.dma_start(wo0n[:, :, :], t["L0_attn_Wo"].rearrange("(r p) d -> p r d", p=P)).then_inc(w["l0"], 16)
            sp.dma_start(x[:, 2:TT, :], xv[:, 2:TT, :]).then_inc(x_loaded, 16)
            mrow_dmas(sp, 0)
            if STAGES > 1:
                late_loads(sp)
            if STAGES > 3:
                expert_loads(sp)
                mrow_dmas(sp, 1)
            ov = out.rearrange("b (h p) d -> p (b h) d", p=P)
            for b in range(B):
                sp.wait_ge(x_normed, 4 * (STAGES - 1) + b + 1)
                sp.dma_start(ov[:, 2 * b:2 * b + 2, :], x[:, 2 * b:2 * b + 2, :]).then_inc(stored, 16)
            sp.wait_ge(stored, 16 * B)

        @block.gpsimd
        def _(pool):
            w = w_loaded
            count = {}

            def alone(ins, signal=p_step):
                count[signal.name] = count.get(signal.name, 0) + 1
                ins.then_inc(signal, 1)
                pool.wait_ge(signal, count[signal.name])

            alone(pool.memset(ones[:, :], 1.0), ones_set)
            alone(pool.memset(Kh[MROW:MROW + 3, :, :, :].rearrange("p a b c -> p (a b c)"), -1.0), krow_set)
            alone(pool.memset(V1[:, :, :, HD:HD + 1], 1.0), ones_set)

            def residual_bias(stage, bias):
                for b in range(B):
                    if stage == 0:
                        pool.wait_ge(x_loaded, 32)
                        if b == 0:
                            pool.wait_ge(bias_loaded, 16 * 8)
                    else:
                        pool.wait_ge(x_normed, 4 * stage + b - 4 + 1)
                    for k in range(2):
                        alone(pool.tensor_tensor(xb[:, 2 * b + k, :], x[:, 2 * b + k, :], bias[:, :], ALU.add),
                              xb_ready if k else p_step)

            def sub_magic(n, q32_, q16_, ready, done):
                for b in range(B):
                    pool.wait_ge(ready, b + 1)
                    if b >= 2:
                        pool.wait_ge(Q["qtr"] if n == 0 else Q["qtr2"], b - 1)
                    alone(pool.tensor_scalar(q16_[:, b % 2], q32_[:, b % 2], -MAGIC, None, ALU.add), done)

            def middle_part(L):
                for u in range(4 if L == 0 else 8):
                    pool.wait_ge(A[L]["rem"], u + 1)
                    (q_src, q_dst), (k_src, k_dst) = stack_views(L, u, "mid")
                    alone(pool.tensor_copy(q_dst, q_src))
                    alone(pool.tensor_copy(k_dst, k_src), A[L]["mid"])

            residual_bias(0, bo)
            middle_part(0)
            if STAGES > 1:
                for k, wn in enumerate((w1n, w2n)):
                    pool.wait_ge(thr_ready, k + 1)
                    alone(pool.tensor_scalar(tmpw[:, k, :], wn.rearrange("p a b -> p (a b)"), tthr[:, k, 1:2], None,
                                       ALU.is_lt), low_ready)
                sub_magic(0, q32, q16, Q["q32"], Q["q16"])
                for b in range(B):
                    pool.wait_ge(Q["sg"], b + 1)
                    alone(pool.tensor_tensor(aa[:, b], sg[:, b % 2], hh[:, b % 2, :, D // 2:D], ALU.mult), Q["aa"])
                sub_magic(1, q32, q16, Q["q32b"], Q["q16b"])
            if STAGES > 2:
                residual_bias(2, b2)
            if STAGES > 3:
                pool.wait_ge(x_normed, 12)
                alone(pool.memset(Kh[MROW:MROW + 3, :, :, :].rearrange("p a b c -> p (a b c)"), -1.0), krow_set)
                middle_part(1)
            if STAGES > 5:
                for n in range(2 * EC):
                    pool.wait_ge(Ms["um"], n + 1)
                    pool.wait_ge(Ms["sg"], n + 1)
                    if n >= 2:
                        pool.wait_ge(am_read, n - 1)
                    alone(pool.tensor_tensor(am[:, n % 2, :], sgm[:, n % 2, :], um[:, n % 2, :], ALU.mult), Ms["am"])


        @block.scalar
        def _(act):
            w = w_loaded
            act.dma_start(masks[:, :, :], t["masks"].bitcast(BF16)).then_inc(w["const"], 16)
            act.dma_start(rope[:, :, :, :], t["rope"]).then_inc(w["const"], 16)
            act.dma_start(order[:, :], t["order"]).then_inc(w["const"], 16)
            act.dma_start(ident16[:, :], t["ident16"].bitcast(BF16)).then_inc(w["const"], 16)
            act.dma_start(bqkv[:, 0:D], t["L0_attn_bq"].partition_broadcast(P)).then_inc(bias_loaded, 16)
            act.dma_start(bqkv[:, D:D + 64], t["L0_attn_bk"].partition_broadcast(P)).then_inc(bias_loaded, 16)
            act.dma_start(bqkv[:, D + 64:D + 128], t["L0_attn_bv"].partition_broadcast(P)).then_inc(bias_loaded, 16)
            act.dma_start(gain[:, :], t["L0_attn_q_gain"].partition_broadcast(P)).then_inc(bias_loaded, 16)
            act.dma_start(bo[:, :], t["L0_attn_bo"].partition_broadcast(P)).then_inc(bias_loaded, 16)
            act.dma_start(b2[:, :], t["L0_ffn_b2"].partition_broadcast(P)).then_inc(bias_loaded, 16)
            act.dma_start(xbias[:, 0:1], t["L1_xattn_bq"].unsqueeze(1)).then_inc(bias_loaded, 16)
            act.dma_start(xbias[:, 1:2], t["L1_xattn_bk"].unsqueeze(1)).then_inc(bias_loaded, 16)
            act.dma_start(b1[:, :], t["b1_cols"]).then_inc(bias_b1, 16)

            def copy(dst, src):
                return nc.scalar.activation(dst, src, ACT.Copy)

            def evac_xT(stage):
                for b in range(B):
                    act.wait_ge(xtr_done, 4 * stage + b + 1)
                    copy(xT[:, :, b * S:(b + 1) * S], bank(6 + b % 2).rearrange("p (c s) -> p c s", c=DC))\
                        .then_inc(xT_ready, 1)

            def attn_front(L):
                a = A[L]
                if L == 1:
                    for n in range(2):
                        act.wait_ge(a["lat"], n + 1)
                        copy(latT[:, n * 512:(n + 1) * 512], bank(4 + n, 512, 0, LAT)).then_inc(a["lat_ready"], 1)
                for b in range(B):
                    if L == 0:
                        hi_part(L, b)
                    else:
                        hi_part(L, 2 * b)
                        hi_part(L, 2 * b + 1)
                    for g in range(TG[L]):
                        n = b * TG[L] + g
                        if n % 2 == 0:
                            act.wait_ge(a["stk_tr"], n + 1)
                            copy(tr_groups(L, b)[g][1], bank16(6, 1024, 0, STK)).then_inc(a["ev_act"], 1)

            def hi_part(L, u):
                a = A[L]
                act.wait_ge(a["sq"], u + 1) if L == 0 else act.wait_ge(a["proj"], u + 1)
                if u >= 2:
                    bb = u - 2 if L == 0 else (u - 2) // 2
                    act.wait_ge(a["stk_tr"], (bb + 1) * TG[L])
                for which in "qk":
                    dst = stack(L, u, which, "hi")
                    src = part_source(L, u, which)
                    if L == 0:
                        nh = H if which == "q" else KVH[0]
                        for half in range(2):
                            last = copy(dst[:, half * nh:(half + 1) * nh],
                                        src[:, half].unsqueeze(2).to_broadcast([P, nh, 3, HD]))
                    else:
                        last = copy(dst, src.unsqueeze(2).to_broadcast([P, H, 3, HD]))
                last.then_inc(a["hi"], 1)

            def attn_back(L):
                a = A[L]
                n = 0
                for step in range(B + 1):
                    for g in range(NG):
                        if step >= 1:
                            act.wait_ge(a["sT"], n + 1)
                            if n >= 2:
                                act.wait_ge(a["av"], n - 1)
                            nc.scalar.activation(PT[:, n % 2, :], PS[:, 3:6, :].rearrange("p a b -> p (a b)"),
                                                 ACT.Exp, scale=NEG_SCALE).then_inc(a["pT"], 1)
                            n += 1
                    if step < B:
                        act.wait_ge(a["mtr"], step + 1)
                        if step >= 2:
                            act.wait_ge(a["mrow"], 48 * (step - 1))
                        copy(mT[:, step % 2, :], bank16(7, S, 0, 3 * H)).then_inc(a["mT"], 1)
                    if step >= 1:
                        act.wait_ge(a["otr"], step)
                        copy(OT[:, (step - 1) % 2, :, :].rearrange("p a b -> p (a b)"), bank(7)).then_inc(a["OT"], 1)

            act.wait_ge(w["const"], 16 * 5)
            act.wait_ge(bias_b1, 16)
            evac_groups(act, copy, 0, NG0, 0)
            evac_xT(0)
            attn_front(0)
            attn_back(0)
            if STAGES > 1:
                evac_groups(act, copy, NG0, NGX, 0)
                for n in range(2):
                    for k in range(2):
                        act.wait_ge(Xs["proj"], 2 * n + k + 1)
                        nc.scalar.activation(xqk[:, k, n * 512:(n + 1) * 512], bank(4 + k), ACT.Identity,
                                             bias=xbias[:, k:k + 1]).then_inc(Xs["qk"], 1)
                for b in range(B):
                    act.wait_ge(Xs["mx"], b + 1)
                    if b >= 2:
                        act.wait_ge(Xs["tr"], b - 1)
                    for k in range(2):
                        last = nc.scalar.activation(xP[:, b % 2, k, :], bank(6 + b % 2, S, k * S), ACT.Exp,
                                                    bias=xmx[:, b % 2, k:k + 1], accum_out=xsm[:, b % 2, k:k + 1])
                    last.then_inc(Xs["exp"], 1)
                    act.wait_ge(Xs["tr"], b + 1)
                    copy(attT[:, b, :, :].rearrange("p a b -> p (a b)"), bank(4 + b % 2)).then_inc(Xs["attT"], 1)
                evac_groups(act, copy, NGX, NGM, 0)
                evac_xT(1)
                for b in range(B):
                    act.wait_ge(Q["qtr"], b + 1)
                    copy(qT[:, b].rearrange("p a b c -> p (a b c)"), bank16(4 + b % 2)).then_inc(Q["qT"], 1)
                for b in range(B):
                    act.wait_ge(Q["wtr"], b + 1)
                    if b >= 2:
                        act.wait_ge(Q["hh"], b - 1)
                    copy(wbc[:, b % 2, :], bank(b % 2, D)).then_inc(Q["wbc"], 1)
                    act.wait_ge(Q["hh"], b + 1)
                    if b >= 2:
                        act.wait_ge(Q["aa"], b - 1)
                    nc.scalar.activation(sg[:, b % 2], hh[:, b % 2, :, 0:D // 2], ACT.Silu).then_inc(Q["sg"], 1)
                for b in range(B):
                    act.wait_ge(Q["atr"], b + 1)
                    copy(aT[:, b, :], bank(2 + b % 2, S)).then_inc(Q["aT"], 1)
                for b in range(B):
                    act.wait_ge(Q["qtr2"], b + 1)
                    copy(qT[:, b, :, 0, :], bank16(4 + b % 2, 512).rearrange("p (a b) -> p a b", a=2)).then_inc(Q["qT2"], 1)
                for b in range(B):
                    act.wait_ge(Q["wtr2"], b + 1)
                    if b >= 2:
                        act.wait_ge(y_done, b - 1)
                    copy(wbc[:, b % 2, :], bank(b % 2, D)).then_inc(Q["wbc2"], 1)
            if STAGES > 2:
                for b in range(B):
                    act.wait_ge(xtr_done, 4 * 2 + b + 1)
                    copy(xT[:, :, b * S:(b + 1) * S], bank(6 + b % 2).rearrange("p (c s) -> p c s", c=DC))\
                        .then_inc(xT_ready, 1)
                    act.wait_ge(xT_ready, 4 * 2 + b + 1)
                    copy(x3[:, 0, :, b * S:(b + 1) * S], xT[:, :, b * S:(b + 1) * S]).then_inc(Fs["hi"], 1)
                for n in range(2 * FCH):
                    blk, f = n // FCH, n % FCH
                    act.wait_ge(Fs["up"], n + 1)
                    nc.scalar.activation(hT[:, f, blk * 512:(blk + 1) * 512], bank(n % 2), ACT.Gelu,
                                         bias=b1[:, f:f + 1]).then_inc(Fs["gelu"], 1)
            if STAGES > 3:
                evac_xT(3)
                attn_front(1)
                attn_back(1)
            if STAGES > 4:
                evac_groups(act, copy, NGM, len(G), 0)
                evac_xT(4)
            if STAGES > 5:
                evac_xT(5)
                act.wait_ge(Ms["lg"], 1)
                nc.scalar.activation(gp[:, :, :], gl[:, :, :], ACT.Exp).then_inc(Ms["exp"], 1)
                for n in range(2 * EC):
                    act.wait_ge(Ms["gu"], n + 1)
                    if n >= 2:
                        act.wait_ge(Ms["am"], n - 1)
                    nc.scalar.activation(sgm[:, n % 2, :], bank(2 * (n % 2)), ACT.Silu).then_inc(Ms["sg"], 1)


        @block.vector
        def _(dve):
            v = nc.vector
            steps = [0]

            def link(ins):
                steps[0] += 1
                ins.then_inc(v_step, 1)
                dve.wait_ge(v_step, steps[0])

            def rsqrt(y, a, tmp):
                link(v.tensor_scalar(y.bitcast(I32), a.bitcast(I32), 1, None, ALU.logical_shift_right))
                link(v.tensor_scalar(y.bitcast(I32), y.bitcast(I32), -1.0, float(RSQRT_SEED), ALU.mult, ALU.add))
                for _ in range(3):
                    link(v.tensor_tensor(tmp, y, y, ALU.mult))
                    link(v.scalar_tensor_tensor(tmp, tmp, -0.5, a, ALU.mult, ALU.mult))
                    link(v.scalar_tensor_tensor(y, tmp, 1.5, y, ALU.add, ALU.mult))

            def add_norm(stage, b, y, base, read=True):
                k = b % 2
                r = res[:, k]
                v.tensor_tensor(r, y, base[:, 2 * b:2 * b + 2, :], ALU.add).then_inc(out_read, 1)
                dve.wait_ge(out_read, 4 * stage + b + 1)
                for i in range(2):
                    ins = v.bn_stats(stat[:, k, i, :], r[:, i, :])
                link(ins)
                for i in range(2):
                    ins = v.bn_aggr(mv[:, k, i, :], stat[:, k, i, :])
                link(ins)
                link(v.tensor_scalar(va[:, :], mv[:, k, :, 1], LN_EPS, None, ALU.add))
                rsqrt(rstd[:, k, :], va[:, :], nt[:, :])
                for i in range(2):
                    ins = v.tensor_scalar(x[:, 2 * b + i, :], r[:, i, :], mv[:, k, i, 0:1], rstd[:, k, i:i + 1],
                                          ALU.subtract, ALU.mult)
                ins.then_inc(x_normed, 1)

            def low_parts(L, u):
                a = A[L]
                dve.wait_ge(a["hi"], u + 1)
                for which in "qk":
                    hi = stack(L, u, which, "hi")[:, :, 0, :]
                    src = part_source(L, u, which)
                    dst = remainder(L, u, which)
                    if L == 0:
                        nh = H if which == "q" else KVH[0]
                        for half in range(2):
                            ins = v.tensor_tensor(dst[:, half * nh:(half + 1) * nh], src[:, half],
                                                  hi[:, half * nh:(half + 1) * nh], ALU.subtract)
                    else:
                        ins = v.tensor_tensor(dst, src, hi, ALU.subtract)
                ins.then_inc(a["rem"], 1)
                dve.wait_ge(a["mid"], u + 1)
                for which in "qk":
                    mid = stack(L, u, which, "mid")[:, :, 0, :]
                    ins = v.tensor_tensor(stack(L, u, which, "lo")[:, :, 0, :], remainder(L, u, which), mid, ALU.subtract)
                ins.then_inc(a["lo"], 1)

            def attn_front(L):
                a = A[L]
                for b in range(B):
                    if L == 0:
                        if b == 0:
                            dve.wait_ge(bias_loaded, 16 * 8)
                            dve.wait_ge(w_loaded["const"], 16 * 5)
                        for k in range(2):
                            tt = 2 * b + k
                            dve.wait_ge(a["proj"], tt + 1)
                            v.tensor_tensor(V1[:, tt, 0:KV0, 0:HD],
                                            bank(k, 64, D + 64).rearrange("p (h d) -> p h d", d=HD),
                                            bqkv[:, D + 64:D + 128].rearrange("p (h d) -> p h d", d=HD),
                                            ALU.add).then_inc(a["v_ready"], 1)
                            ins = v.tensor_tensor(qk[:, b % 2, k, :], bank(k, D + 64), bqkv[:, 0:D + 64], ALU.add)
                            ins.then_inc(a["proj_read"], 1)
                        dve.wait_ge(a["proj_read"], 2 * b + 2)
                        q2 = qk[:, b % 2].rearrange("p t n -> p (t n)")
                        sq = qsq[:, :, :].rearrange("p t n -> p (t n)")
                        ro = qro[:, :, :].rearrange("p t n -> p (t n)")
                        NHB = 2 * (H + KV0)
                        link(v.tensor_tensor(sq, q2, q2, ALU.mult))
                        link(v.tensor_reduce(qss[:, :], sq.rearrange("p (h d) -> p h d", d=HD), X, ALU.add))
                        link(v.tensor_scalar(qss[:, :], qss[:, :], 1.0 / HD, RMS_EPS, ALU.mult, ALU.add))
                        rsqrt(qrs[:, :], qss[:, :], qnt[:, :])
                        rq = qrs[:, :].rearrange("p (t h) -> p t h", t=2)[:, :, 0:H]
                        link(v.tensor_tensor(rq, rq, gain[:, :].unsqueeze(1).to_broadcast([P, 2, H]), ALU.mult))
                        q3 = q2.rearrange("p (h d) -> p h d", d=HD)
                        link(v.tensor_tensor(q3, q3, qrs[:, :].unsqueeze(2).to_broadcast([P, NHB, HD]), ALU.mult))
                        if b >= 1:
                            dve.wait_ge(a["lo"], b)
                        hf = HD // 2
                        for k in range(2):
                            qi = qk[:, b % 2, k, :].rearrange("p (h d) -> p h d", d=HD)
                            ri = qro[:, k, :].rearrange("p (h d) -> p h d", d=HD)
                            si = qsq[:, k, :].rearrange("p (h d) -> p h d", d=HD)
                            nh = H + KV0
                            cos = rope[:, k, 0, :].unsqueeze(1).to_broadcast([P, nh, HD])
                            s1 = rope[:, k, 1, 0:hf].unsqueeze(1).to_broadcast([P, nh, hf])
                            s2 = rope[:, k, 1, hf:HD].unsqueeze(1).to_broadcast([P, nh, hf])
                            v.tensor_tensor(ri, qi, cos, ALU.mult)
                            v.tensor_tensor(si[:, :, 0:hf], qi[:, :, hf:HD], s1, ALU.mult)
                            link(v.tensor_tensor(si[:, :, hf:HD], qi[:, :, 0:hf], s2, ALU.mult))
                        v.tensor_tensor(ro, ro, sq, ALU.add).then_inc(a["sq"], 1)
                        low_parts(L, b)
                    else:
                        for u in (2 * b, 2 * b + 1):
                            low_parts(L, u)
                            v.tensor_copy(V1[:, u, :, 0:HD],
                                          bank(2 * (u % 2) + 1, D).rearrange("p (h d) -> p h d", d=HD))\
                                .then_inc(a["v_ready"], 1)
                    for g in range(TG[L]):
                        n = b * TG[L] + g
                        if n % 2 == 1:
                            dve.wait_ge(a["stk_tr"], n + 1)
                            v.tensor_copy(tr_groups(L, b)[g][1], bank16(7, 1024, 0, STK)).then_inc(a["ev_dve"], 1)

            def attn_back(L):
                a = A[L]
                m = n = 0
                for step in range(B + 1):
                    for g in range(NG):
                        if step < B:
                            dve.wait_ge(a["smax"], m + 1)
                            k = step % 2
                            v.tensor_reduce(mx[:, k, 0, HG * g:HG * g + HG],
                                            bank(0).rearrange("p (h s) -> p h s", h=HG), X, ALU.max)
                            v.tensor_reduce(mx[:, k, 1, HG * g:HG * g + HG],
                                            PS[:, 1:3, :].rearrange("p a (h s) -> p (a h) s", h=2), X, ALU.max)\
                                .then_inc(a["mx"], 1)
                            m += 1
                        if step >= 1:
                            dve.wait_ge(a["av"], n + 1)
                            k = (step - 1) % 2
                            o = bank(6, 2 * HG * (HD + 1)).rearrange("p (t h d) -> p t h d", t=2, h=HG)
                            link(v.reciprocal(rsum[:, n % 2], o[:, :, :, HD]))
                            if step >= 3 and g == 0:
                                dve.wait_ge(a["otr"], step - 2)
                            v.tensor_tensor(on[:, k, :, HG * HD * g:HG * HD * (g + 1)]
                                            .rearrange("p t (h d) -> p t h d", h=HG), o[:, :, :, 0:HD],
                                            rsum[:, n % 2].unsqueeze(3).to_broadcast([P, 2, HG, HD]),
                                            ALU.mult).then_inc(a["on"], 1)
                            n += 1
                    if step < B:
                        k = step % 2
                        if step >= 2:
                            dve.wait_ge(a["mtr"], step - 1)
                        dve.wait_ge(a["mx"], m)
                        link(v.tensor_copy(mst[:, k, :, 0, :], mx[:, k]))
                        link(v.tensor_tensor(mxr[:, k], mx[:, k], mst[:, k, :, 0, :], ALU.subtract))
                        link(v.tensor_copy(mst[:, k, :, 1, :], mxr[:, k]))
                        v.tensor_tensor(mst[:, k, :, 2, :], mxr[:, k], mst[:, k, :, 1, :], ALU.subtract)\
                            .then_inc(a["mst"], 1)
                    if step >= 1:
                        b = step - 1
                        dve.wait_ge(y_ready, 4 * 3 * L + b + 1)
                        if L == 0:
                            dve.wait_ge(xb_ready, b + 1)
                        add_norm(3 * L, b, bank(7).rearrange("p (t d) -> p t d", t=2), xb if L == 0 else x)

            evac_groups(dve, v.tensor_copy, 0, NG0, 1)
            dve.wait_ge(ones_set, 2)
            attn_front(0)
            attn_back(0)
            if STAGES > 1:
                evac_groups(dve, v.tensor_copy, NG0, NGX, 1)
                for k, (wn, nm, wt) in enumerate(((w1n, "w1", w1t), (w2n, "w2", w2t))):
                    dve.wait_ge(w_loaded[nm], 16)
                    v.tensor_reduce(tsum[:, k:k + 1], wn.rearrange("p a b -> p (a b)"), X, ALU.add,
                                    apply_absolute_value=True).then_inc(abs_sum, 1)
                for k in range(2):
                    dve.wait_ge(abs_tot, k + 1)
                    link(v.tensor_scalar(tthr[:, k, 0:1], bank(4 + k, 1), 1.0 / (FF * D), 1e-8, ALU.mult, ALU.max))
                    link(v.tensor_scalar(tthr[:, k, 0:1], tthr[:, k, 0:1], 0.5, None, ALU.mult))
                    v.tensor_scalar(tthr[:, k, 1:2], tthr[:, k, 0:1], -1.0, None, ALU.mult).then_inc(thr_ready, 1)
                for k, (wn, wt) in enumerate(((w1n, w1t), (w2n, w2t))):
                    dve.wait_ge(low_ready, k + 1)
                    v.scalar_tensor_tensor(wt.rearrange("p a b -> p (a b)"), wn.rearrange("p a b -> p (a b)"),
                                           tthr[:, k, 0:1], tmpw[:, k, :], ALU.is_gt, ALU.subtract)\
                        .then_inc(tern_ready, 1)
                for b in range(B):
                    dve.wait_ge(Xs["en"], b + 1)
                    v.tensor_reduce(xmx[:, b % 2, :], bank(6 + b % 2).rearrange("p (t s) -> p t s", t=2), X, ALU.max,
                                    negate=True).then_inc(Xs["mx"], 1)
                    dve.wait_ge(Xs["exp"], b + 1)
                    link(v.reciprocal(xsm[:, b % 2, :], xsm[:, b % 2, :]))
                    for k in range(2):
                        ins = v.tensor_scalar(xP[:, b % 2, k, :], xP[:, b % 2, k, :], xsm[:, b % 2, k:k + 1], None, ALU.mult)
                    ins.then_inc(Xs["norm"], 1)
                evac_groups(dve, v.tensor_copy, NGX, NGM, 1)

                def smooth_scales(n, ready_x):
                    link(v.tensor_scalar(amx[:, :, 0:n], amx[:, :, 0:n], Q_EPS, None, ALU.max))
                    link(v.reciprocal(qs[:, 0, 0:n], amx[:, 1, 0:n]))
                    link(v.tensor_tensor(qs[:, 0, 0:n], amx[:, 0, 0:n], qs[:, 0, 0:n], ALU.mult))
                    rsqrt(qs[:, 1, 0:n], qs[:, 0, 0:n], qs[:, 2, 0:n])
                    link(v.tensor_tensor(qs[:, 1, 0:n], qs[:, 1, 0:n], qs[:, 0, 0:n], ALU.mult))
                    link(v.tensor_scalar(qs[:, 1, 0:n], qs[:, 1, 0:n], Q_EPS, None, ALU.max))
                    link(v.reciprocal(qs[:, 0, 0:n], qs[:, 1, 0:n]))

                def row_scales(b, nat):
                    link(v.tensor_reduce(rsc[:, b, :], nat, X, ALU.max, apply_absolute_value=True))
                    link(v.tensor_scalar(rsc[:, b, :], rsc[:, b, :], Q_EPS, 1.0 / 127.0, ALU.max, ALU.mult))
                    link(v.reciprocal(rrq[:, b, :], rsc[:, b, :]))

                dve.wait_ge(wt_act, (NGX + 1) // 2)
                dve.wait_ge(wt_dve, NGX // 2)
                v.tensor_reduce(amx[:, 1, :], fT[:, :, :, :].rearrange("p b c s -> p (b c) s"), X, ALU.max,
                                apply_absolute_value=True)
                for b in range(B):
                    dve.wait_ge(xT_ready, 4 + b + 1)
                    ins = v.tensor_reduce(amx[:, 0, b * DC:(b + 1) * DC], xT[:, :, b * S:(b + 1) * S], X, ALU.max,
                                          apply_absolute_value=True)
                link(ins)
                smooth_scales(B * DC, None)
                for b in range(B):
                    for c in range(DC):
                        j = b * DC + c
                        v.tensor_scalar(xw[:, b, 0, c, :], xT[:, c, b * S:(b + 1) * S], qs[:, 0, j:j + 1], None, ALU.mult)
                        ins = v.tensor_scalar(xw[:, b, 1, c, :], fT[:, b, c, :], qs[:, 1, j:j + 1], None, ALU.mult)
                    ins.then_inc(Q["xw"], 1)
                for b in range(B):
                    dve.wait_ge(Q["nat"], b + 1)
                    k = 2 * (b % 2)
                    nat = PS[:, k:k + 2, :].rearrange("p a (t d) -> p (a t) d", t=2)
                    row_scales(b, nat)
                    if b >= 2:
                        dve.wait_ge(Q["q16"], b - 1)
                    for i in range(4):
                        ins = v.tensor_scalar(q32[:, b % 2, i, :], nat[:, i, :], rrq[:, b, i:i + 1], MAGIC, ALU.mult, ALU.add)
                    ins.then_inc(Q["q32"], 1)
                for b in range(B):
                    dve.wait_ge(Q["h"], b + 1)
                    dve.wait_ge(Q["wbc"], b + 1)
                    if b >= 2:
                        dve.wait_ge(Q["aa"], b - 1)
                    for i in range(2):
                        ins = v.scalar_tensor_tensor(hh[:, b % 2, i, :], bank(6 + b % 2, D, i * D), rsc[:, b, i:i + 1],
                                                     wbc[:, b % 2, :], ALU.mult, ALU.mult)
                    ins.then_inc(Q["hh"], 1)
                v.tensor_reduce(amx[:, 1, 0:B], ctxT[:, :, :], X, ALU.max, apply_absolute_value=True)
                dve.wait_ge(Q["aT"], B)
                link(v.tensor_reduce(amx[:, 0, 0:B], aT, X, ALU.max, apply_absolute_value=True))
                smooth_scales(B, None)
                for b in range(B):
                    v.tensor_scalar(xw2[:, b, 0, :], aT[:, b, :], qs[:, 0, b:b + 1], None, ALU.mult)
                    v.tensor_scalar(xw2[:, b, 1, :], ctxT[:, b, :], qs[:, 1, b:b + 1], None, ALU.mult).then_inc(Q["xw2"], 1)
                for b in range(B):
                    dve.wait_ge(Q["nat2"], b + 1)
                    nat = bank(b % 2).rearrange("p (t d) -> p t d", t=4)
                    row_scales(b, nat)
                    if b >= 2:
                        dve.wait_ge(Q["q16b"], b - 1)
                    for i in range(4):
                        ins = v.tensor_scalar(q32[:, b % 2, i, 0:CX], nat[:, i, :], rrq[:, b, i:i + 1], MAGIC, ALU.mult, ALU.add)
                    ins.then_inc(Q["q32b"], 1)
                for b in range(B):
                    dve.wait_ge(y_ready, 4 * 1 + b + 1)
                    dve.wait_ge(Q["wbc2"], b + 1)
                    for i in range(2):
                        ins = v.scalar_tensor_tensor(y2[:, b % 2, i, :], bank(6 + b % 2, D, i * D), rsc[:, b, i:i + 1],
                                                     wbc[:, b % 2, :], ALU.mult, ALU.mult)
                    ins.then_inc(y_done, 1)
                    dve.wait_ge(y_done, b + 1)
                    add_norm(1, b, y2[:, b % 2], x)
            if STAGES > 2:
                for b in range(B):
                    bs = slice(b * S, (b + 1) * S)
                    dve.wait_ge(Fs["hi"], b + 1)
                    link(v.tensor_tensor(xrem[:, b % 2], xT[:, :, bs], x3[:, 0, :, bs], ALU.subtract))
                    link(v.tensor_copy(x3[:, 1, :, bs], xrem[:, b % 2]))
                    v.tensor_tensor(x3[:, 2, :, bs], xrem[:, b % 2], x3[:, 1, :, bs], ALU.subtract).then_inc(Fs["lo"], 1)
                for b in range(B):
                    dve.wait_ge(y_ready, 4 * 2 + b + 1)
                    dve.wait_ge(xb_ready, B + b + 1)
                    add_norm(2, b, bank(2 + b % 2).rearrange("p (t d) -> p t d", t=2), xb)
            if STAGES > 3:
                attn_front(1)
                attn_back(1)
            if STAGES > 4:
                evac_groups(dve, v.tensor_copy, NGM, len(G), 1)
                for b in range(B):
                    dve.wait_ge(y_ready, 4 * 4 + b + 1)
                    add_norm(4, b, bank(b % 2).rearrange("p (t d) -> p t d", t=2), x)
            if STAGES > 5:
                def bc(a):
                    return a.unsqueeze(2).to_broadcast([P, TT, E])

                ordb = order[:, :].unsqueeze(1).to_broadcast([P, TT, E])
                dve.wait_ge(Ms["logit"], 1)
                lg = bank(4, TT * E).rearrange("p (t e) -> p t e", e=E)
                link(v.tensor_reduce(g1[:, 0, :], lg, X, ALU.max))
                v.tensor_tensor(gl[:, :, :], lg, bc(g1[:, 0, :]), ALU.subtract).then_inc(Ms["lg"], 1)
                dve.wait_ge(Ms["exp"], 1)
                link(v.tensor_reduce(g1[:, 1, :], gp[:, :, :], X, ALU.add))
                link(v.reciprocal(g1[:, 1, :], g1[:, 1, :]))
                link(v.tensor_tensor(gp[:, :, :], gp[:, :, :], bc(g1[:, 1, :]), ALU.mult))
                cur = gp
                for j in range(2):
                    link(v.tensor_reduce(g1[:, 2 + j, :], cur[:, :, :], X, ALU.max))
                    link(v.tensor_tensor(gr[:, :, :], cur[:, :, :], bc(g1[:, 2 + j, :]), ALU.is_equal))
                    link(v.tensor_tensor(gr[:, :, :], gr[:, :, :], ordb, ALU.mult))
                    link(v.tensor_reduce(g1[:, 4, :], gr[:, :, :], X, ALU.max))
                    link(v.tensor_tensor(oh[:, j], gr[:, :, :], bc(g1[:, 4, :]), ALU.is_equal))
                    if j == 0:
                        link(v.scalar_tensor_tensor(gq[:, :, :].rearrange("p a b -> p (a b)"),
                                                    oh[:, 0].rearrange("p a b -> p (a b)"), -2.0,
                                                    gp[:, :, :].rearrange("p a b -> p (a b)"), ALU.mult, ALU.add))
                        cur = gq
                link(v.tensor_tensor(oh[:, 0], oh[:, 0], oh[:, 1], ALU.add))
                link(v.tensor_tensor(g1[:, 5, :], g1[:, 2, :], g1[:, 3, :], ALU.add))
                link(v.reciprocal(g1[:, 5, :], g1[:, 5, :]))
                link(v.tensor_tensor(oh[:, 0], oh[:, 0], gp[:, :, :], ALU.mult))
                link(v.tensor_tensor(gq[:, :, :], oh[:, 0], bc(g1[:, 5, :]), ALU.mult))
                v.tensor_copy(combw.rearrange("p t e i -> p (t e) i"),
                              gq[:, :, :].rearrange("p t e -> p (t e)").unsqueeze(2).to_broadcast([P, TT * E, IB]))\
                    .then_inc(Ms["comb"], 1)
                for k in range(2):
                    dve.wait_ge(Ms["ctr"], k + 1)
                    v.tensor_copy(GB[:, k * 512:(k + 1) * 512], bank(4 + k)).then_inc(Ms["GB"], 1)
                dve.wait_ge(Ms["GB"], 2)
                for n in range(2 * EC):
                    blk = n // EC
                    dve.wait_ge(Ms["gu"], n + 1)
                    if n >= 2:
                        dve.wait_ge(Ms["am"], n - 1)
                    v.tensor_tensor(um[:, n % 2, :], bank(2 * (n % 2) + 1), GB[:, blk * 512:(blk + 1) * 512],
                                    ALU.mult).then_inc(Ms["um"], 1)
                    if n % EC == EC - 1:
                        for b in (2 * blk, 2 * blk + 1):
                            dve.wait_ge(am_read, n + 1)
                            add_norm(5, b, PS[:, 4 + 2 * (b % 2):6 + 2 * (b % 2), 0:D], x)


        @block.tensor
        def _(pe):
            mm = nc.tensor.matmul

            def transpose_x(stage, free):
                for b in range(B):
                    if stage == 0:
                        pe.wait_ge(x_loaded, 16 if b == 0 else 32)
                    else:
                        pe.wait_ge(x_normed, 4 * (stage - 1) + b + 1)
                    if b == 0 and stage == 2:
                        pe.wait_ge(out_read, 4 * stage - 1)
                    if b == 1 and stage > 0:
                        pe.wait_ge(out_read, 4 * stage)
                    if b >= 2:
                        pe.wait_ge(xT_ready, 4 * stage + b - 1)
                    for c in range(DC):
                        for k in range(2):
                            last = nc.tensor.transpose(bank(6 + b % 2, P, c * S + k * P),
                                                       x[:, 2 * b + k, c * P:(c + 1) * P], ident[:, :])
                    last.then_inc(xtr_done, 1)

            def project(L):
                a = A[L]
                if L == 1:
                    pe.wait_ge(xT_ready, 4 * 3 + B)
                    for n in range(2):
                        for c in range(DC):
                            last = mm(bank(4 + n, 512, 0, LAT), wdT[:, c, :], xT[:, c, n * 512:(n + 1) * 512],
                                      start=(c == 0), stop=(c == DC - 1))
                        last.then_inc(a["lat"], 1)
                    pe.wait_ge(a["lat_ready"], 2)
                for b in range(B):
                    for k in range(2):
                        tt = 2 * b + k
                        ts = slice(tt * P, (tt + 1) * P)
                        if L == 0:
                            pe.wait_ge(xT_ready, b + 1)
                            if tt >= 2:
                                pe.wait_ge(a["proj_read"], tt - 1)
                            for c in range(DC):
                                last = mm(bank(k, 384), xT[:, c, ts], wqkvT[:, c, :], start=(c == 0), stop=(c == DC - 1))
                        else:
                            if tt >= 2:
                                pe.wait_ge(a["v_ready"], tt - 1)
                            for c in range(DC):
                                mm(bank(2 * k, D), xT[:, c, ts], wqT1[:, c, :], start=(c == 0), stop=(c == DC - 1))
                            mm(bank(2 * k, D, D), latT[:, ts], wupT[:, 0:D], start=True, stop=True)
                            last = mm(bank(2 * k + 1, D), latT[:, ts], wupT[:, D:2 * D], start=True, stop=True)
                        last.then_inc(a["proj"], 1)
                    if b >= 1:
                        stack_transposes(L, b - 1)
                stack_transposes(L, B - 1)

            def stack_transposes(L, b):
                a = A[L]
                pe.wait_ge(a["lo"], b + 1 if L == 0 else 2 * b + 2)
                for g, (srcs, dst) in enumerate(tr_groups(L, b)):
                    n = b * TG[L] + g
                    if n == 0:
                        pe.wait_ge(xT_ready, 12 * L + B)
                    if n >= 2:
                        pe.wait_ge(a["ev_dve"] if n % 2 else a["ev_act"], (n - 2) // 2 + 1)
                    for i, s_ in enumerate(srcs):
                        last = nc.tensor.transpose(bank16(6 + n % 2, P, i * P, STK), s_, ident16[:, :])
                    last.then_inc(a["stk_tr"], 1)

            def attn_back(L):
                a = A[L]
                mk = masks[:, L, :]
                nkv = KVH[L]
                NTG = B * TG[L]
                pe.wait_ge(a["ev_act"], (NTG + 1) // 2)
                pe.wait_ge(a["ev_dve"], NTG // 2)
                pe.wait_ge(krow_set, L + 1)

                def kv(h):
                    return h * nkv // H

                def max_scores(b, g, m):
                    if m >= 1:
                        pe.wait_ge(a["mx"], m)
                    mm(bank(0), ident16[:, :], mk[:, 0:P].unsqueeze(1).to_broadcast([P, HG, P]), start=True, stop=False)
                    for j in range(2):
                        mm(bank(1 + j), ident16[:, :], mk[:, P:3 * P].unsqueeze(1).to_broadcast([P, 2, S]), start=True, stop=False)
                    for i in range(HG):
                        h = HG * g + i
                        mm(bank(0, P, i * P), Qh[0:STK, b, h, 0:P], Kh[0:STK, b, kv(h), 0:P],
                           start=False, stop=(i == HG - 1))
                    for i in range(HG):
                        h = HG * g + i
                        last = mm(bank(1 + i // 2, S, (i % 2) * S), Qh[0:STK, b, h, P:S], Kh[0:STK, b, kv(h), :],
                                  start=False, stop=(i % 2 == 1))
                    last.then_inc(a["smax"], 1)

                def exp_scores(b, g, n):
                    R = STK + 3
                    if n >= 1:
                        pe.wait_ge(a["pT"], n)
                    for j in range(2):
                        mm(bank(3 + j), ident16[:, :], mk[:, 3 * P:5 * P].unsqueeze(1).to_broadcast([P, 2, S]), start=True, stop=False)
                    mm(bank(5), ident16[:, :], mk[:, 5 * P:6 * P].unsqueeze(1).to_broadcast([P, HG, P]), start=True, stop=False)
                    for i in range(HG):
                        h = HG * g + i
                        mm(bank(3 + i // 2, S, (i % 2) * S), Kh[0:R, b, kv(h), 0:P], Qh[0:R, b, h, :],
                           start=False, stop=(i % 2 == 1))
                    for i in range(HG):
                        h = HG * g + i
                        last = mm(bank(5, P, i * P), Kh[0:R, b, kv(h), P:S], Qh[0:R, b, h, P:S],
                                  start=False, stop=(i == HG - 1))
                    last.then_inc(a["sT"], 1)

                def values(b, g, n):
                    pe.wait_ge(a["pT"], n + 1)
                    if n >= 1:
                        pe.wait_ge(a["on"], n)
                    W = HD + 1
                    p0 = PT[:, n % 2, 0:1024].rearrange("p (h s) -> p h s", h=HG)
                    p1 = PT[:, n % 2, 1024:1536].rearrange("p (h s) -> p h s", h=HG)
                    for i in range(HG):
                        kh = kv(HG * g + i)
                        mm(bank(6, W, i * W), p0[:, i, 0:P], V1[:, 2 * b, kh, :], start=True, stop=True)
                        mm(bank(6, W, (HG + i) * W), p0[:, i, P:S], V1[:, 2 * b, kh, :], start=True, stop=False)
                        last = mm(bank(6, W, (HG + i) * W), p1[:, i, :], V1[:, 2 * b + 1, kh, :], start=False, stop=True)
                    last.then_inc(a["av"], 1)

                m = n = 0
                for step in range(B + 1):
                    for g in range(NG):
                        if step >= 1:
                            if g == 0:
                                pe.wait_ge(a["mrow"], 48 * step)
                            exp_scores(step - 1, g, n)
                        if step < B:
                            max_scores(step, g, m)
                            m += 1
                        if step >= 1:
                            values(step - 1, g, n)
                            n += 1
                    if step < B:
                        pe.wait_ge(a["mst"], step + 1)
                        if step >= 2:
                            pe.wait_ge(out_read, 12 * L + step - 1)
                        for k in range(2):
                            last = nc.tensor.transpose(bank16(7, P, k * P, 3 * H),
                                                       mst[:, step % 2, k].rearrange("p a b -> p (a b)"), ident16[:, :])
                        last.then_inc(a["mtr"], 1)
                    if step >= 1:
                        b = step - 1
                        pe.wait_ge(a["on"], n)
                        if step < B:
                            pe.wait_ge(a["mT"], step + 1)
                        elif b >= 1:
                            pe.wait_ge(out_read, 12 * L + b)
                        for c in range(DC):
                            for k in range(2):
                                last = nc.tensor.transpose(bank(7, P, c * S + k * P), on[:, b % 2, k, c * P:(c + 1) * P], ident[:, :])
                        last.then_inc(a["otr"], 1)
                        pe.wait_ge(a["OT"], step)
                        for k in range(2):
                            for c in range(DC):
                                last = mm(bank(7, D, k * D), OT[:, b % 2, c, k * P:(k + 1) * P], woT[L][:, c, :],
                                          start=(c == 0), stop=(c == DC - 1))
                        last.then_inc(y_ready, 1)

            pe.wait_ge(w_loaded["const"], 16 * 5)
            pe_groups(pe, 0, NG0)
            transpose_x(0, None)
            pe.wait_ge(wt_act, (NG0 + 1) // 2)
            pe.wait_ge(wt_dve, NG0 // 2)
            project(0)
            attn_back(0)
            if STAGES > 1:
                pe_groups(pe, NG0, NGX)
                pe.wait_ge(wt_act, (NGX + 1) // 2)
                pe.wait_ge(wt_dve, NGX // 2)
                for n in range(2):
                    for k in range(2):
                        if n >= 1:
                            pe.wait_ge(Xs["qk"], 2 * n + k - 1)
                        mm(bank(4 + k), xwT[:, k, :], ctxT[:, 2 * n:2 * n + 2, :].rearrange("p a b -> p (a b)"),
                           start=True, stop=True).then_inc(Xs["proj"], 1)
                pe.wait_ge(Xs["qk"], 4)
                pe.wait_ge(ones_set, 1)
                for k in range(2):
                    pe.wait_ge(abs_sum, k + 1)
                    mm(bank(4 + k, 1), ones[:, :], tsum[:, k:k + 1], start=True, stop=True).then_inc(abs_tot, 1)
                pe.wait_ge(thr_ready, 2)
                pe.wait_ge(out_read, 4)
                for b in range(B):
                    if b >= 2:
                        pe.wait_ge(Xs["exp"], b - 1)
                    for k in range(2):
                        last = mm(bank(6 + b % 2, S, k * S), xqk[:, 0, b * S + k * P:b * S + (k + 1) * P],
                                  xqk[:, 1, b * S:(b + 1) * S], start=True, stop=True)
                    last.then_inc(Xs["en"], 1)
                    pe.wait_ge(Xs["norm"], b + 1)
                    if b >= 2:
                        pe.wait_ge(Xs["attT"], b - 1)
                    for j in range(2):
                        for k in range(2):
                            last = nc.tensor.transpose(bank(4 + b % 2, P, j * S + k * P),
                                                       xP[:, b % 2, k, j * P:(j + 1) * P], ident[:, :])
                    last.then_inc(Xs["tr"], 1)
                pe_groups(pe, NGX, NGM)
                transpose_x(1, None)
                pe.wait_ge(wt_act, (NGM + 1) // 2)
                pe.wait_ge(wt_dve, NGM // 2)
                for b in range(B):
                    pe.wait_ge(Q["xw"], b + 1)
                    if b >= 2:
                        pe.wait_ge(Q["q32"], b - 1)
                    for w_ in range(2):
                        for k in range(2):
                            for c in range(DC):
                                last = nc.tensor.transpose(bank(2 * (b % 2) + w_, P, k * D + c * P),
                                                           xw[:, b, w_, c, k * P:(k + 1) * P], ident[:, :])
                    last.then_inc(Q["nat"], 1)
                    if b >= 1:
                        quant_transposes(pe, b - 1)
                quant_transposes(pe, B - 1)
                for b in range(B):
                    pe.wait_ge(Q["qT"], b + 1)
                    if b >= 2:
                        pe.wait_ge(Q["hh"], b - 1)
                    elif b == 0:
                        pe.wait_ge(xT_ready, 8)
                    if b == 0:
                        pe.wait_ge(Q["q32"], B)
                    for k in range(2):
                        for c in range(DC):
                            last = mm(bank(6 + b % 2, D, k * D), qT[:, b, 0, c, k * P:(k + 1) * P], qT[:, b, 1, c, :],
                                      start=(c == 0), stop=(c == DC - 1))
                    last.then_inc(Q["h"], 1)
                    if b >= 2:
                        pe.wait_ge(Q["wbc"], b - 1)
                    for k in range(2):
                        last = nc.tensor.transpose(bank(b % 2, P, k * P), rsc[:, b, 2 + k:3 + k].to_broadcast([P, P]), ident[:, :])
                    last.then_inc(Q["wtr"], 1)
                for b in range(B):
                    pe.wait_ge(Q["aa"], b + 1)
                    if b >= 2:
                        pe.wait_ge(Q["aT"], b - 1)
                    for k in range(2):
                        last = nc.tensor.transpose(bank(2 + b % 2, P, k * P), aa[:, b, k, :], ident[:, :])
                    last.then_inc(Q["atr"], 1)
                for b in range(B):
                    pe.wait_ge(Q["xw2"], b + 1)
                    if b >= 2:
                        pe.wait_ge(Q["q32b"], b - 1)
                    for w_ in range(2):
                        for k in range(2):
                            last = nc.tensor.transpose(bank(b % 2, P, (2 * w_ + k) * P), xw2[:, b, w_, k * P:(k + 1) * P], ident[:, :])
                    last.then_inc(Q["nat2"], 1)
                    if b >= 1:
                        quant_transposes2(pe, b - 1)
                quant_transposes2(pe, B - 1)
                for b in range(B):
                    pe.wait_ge(Q["qT2"], b + 1)
                    if b >= 2:
                        pe.wait_ge(y_done, b - 1)
                    elif b == 0:
                        pe.wait_ge(Q["q32b"], B)
                    for k in range(2):
                        last = mm(bank(6 + b % 2, D, k * D), qT[:, b, 0, 0, k * P:(k + 1) * P], qT[:, b, 1, 0, :],
                                  start=True, stop=True)
                    last.then_inc(y_ready, 1)
                    if b >= 2:
                        pe.wait_ge(Q["wbc2"], b - 1)
                    for k in range(2):
                        last = nc.tensor.transpose(bank(b % 2, P, k * P), rsc[:, b, 2 + k:3 + k].to_broadcast([P, P]), ident[:, :])
                    last.then_inc(Q["wtr2"], 1)
            if STAGES > 2:
                transpose_x(2, None)
                for blk in range(2):
                    for f in range(FCH):
                        n = blk * FCH + f
                        if f == 0:
                            pe.wait_ge(Fs["lo"], 2 * blk + 2)
                        if n >= 2:
                            pe.wait_ge(Fs["gelu"], n - 1)
                        for i in range(3):
                            for c in range(DC):
                                last = mm(bank(n % 2), w1T[:, c, f * P:(f + 1) * P], x3[:, i, c, blk * 512:(blk + 1) * 512],
                                          start=(i == 0 and c == 0), stop=(i == 2 and c == DC - 1))
                        last.then_inc(Fs["up"], 1)
                for b in range(B):
                    pe.wait_ge(Fs["gelu"], FCH * (b // 2 + 1))
                    if b >= 2:
                        pe.wait_ge(out_read, 8 + b - 1)
                    for k in range(2):
                        for f in range(FCH):
                            last = mm(bank(2 + b % 2, D, k * D), hT[:, f, (2 * b + k) * P:(2 * b + k + 1) * P], w2T[:, f, :],
                                      start=(f == 0), stop=(f == FCH - 1))
                    last.then_inc(y_ready, 1)
            if STAGES > 3:
                transpose_x(3, None)
                project(1)
                attn_back(1)
            if STAGES > 4:
                pe_groups(pe, NGM, len(G))
                transpose_x(4, None)
                pe.wait_ge(wt_act, (len(G) + 1) // 2)
                pe.wait_ge(wt_dve, len(G) // 2)
                for b in range(B):
                    pe.wait_ge(Xs["attT"], b + 1)
                    pe.wait_ge(xT_ready, 16 + b + 1)
                    if b >= 2:
                        pe.wait_ge(out_read, 16 + b - 1)
                    for k in range(2):
                        for c in range(DC):
                            last = mm(bank(b % 2, S, k * S), xT[:, c, b * S + k * P:b * S + (k + 1) * P], attT[:, b, c, :],
                                      start=(c == 0), stop=(c == DC - 1))
                    last.then_inc(y_ready, 1)
            if STAGES > 5:
                transpose_x(5, None)
                pe.wait_ge(xT_ready, 24)
                for tt in range(TT):
                    for c in range(DC):
                        last = mm(bank(4, E, tt * E), xT[:, c, tt * P:(tt + 1) * P], gwT[:, c, :],
                                  start=(c == 0), stop=(c == DC - 1))
                last.then_inc(Ms["logit"], 1)

                def up(n):
                    blk, c_ = n // EC, n % EC
                    if n == 0:
                        pe.wait_ge(out_read, 20)
                    if n >= 2:
                        pe.wait_ge(Ms["sg"], n - 1)
                        pe.wait_ge(Ms["um"], n - 1)
                    for gu in range(2):
                        for c in range(DC):
                            last = mm(bank(2 * (n % 2) + gu), mw1T[:, c, gu, c_ * P:(c_ + 1) * P],
                                      xT[:, c, blk * 512:(blk + 1) * 512], start=(c == 0), stop=(c == DC - 1))
                    last.then_inc(Ms["gu"], 1)

                def down(n):
                    blk, c_ = n // EC, n % EC
                    pe.wait_ge(Ms["am"], n + 1)
                    if c_ == 0 and blk == 0:
                        pe.wait_ge(Ms["GB"], 2)
                    if c_ == 0 and blk == 1:
                        pe.wait_ge(out_read, 22)
                    for k in range(4):
                        last = mm(bank(4 + k, D), am[:, n % 2, k * P:(k + 1) * P], mw2T[:, c_, :],
                                  start=(c_ == 0), stop=(c_ == EC - 1))
                    last.then_inc(am_read, 1)

                up(0)
                pe.wait_ge(Ms["comb"], 1)
                for k in range(2):
                    for i in range(4):
                        last = nc.tensor.transpose(bank(4 + k, P, i * P),
                                                   combw[:, 4 * k + i].rearrange("p e i -> p (e i)"), ident[:, :])
                    last.then_inc(Ms["ctr"], 1)
                for n in range(1, 2 * EC):
                    up(n)
                    down(n - 1)
                down(2 * EC - 1)


def shape_constants():
    import numpy as np

    def bf16_bits(a):
        return (np.ascontiguousarray(a, np.float32).view(np.uint32) >> 16).astype(np.uint16)

    s, hd = 256, 16
    i = np.arange(s)[:, None]
    j = np.arange(s)[None, :]
    causal = j <= i
    window = (causal & (j >= i - 63)) | ((j < 4) & causal)
    m = np.zeros((128, 2, 768), np.float32)
    for n, ok in enumerate((causal, window)):
        f = np.where(ok, 0.0, -1e30).astype(np.float32)
        m[:, n, 0:128] = f[0:128, 0:128]
        m[:, n, 128:384] = f[128:256, :]
        m[:, n, 384:640] = f[:, 0:128].T
        m[:, n, 640:768] = f[128:256, 128:256].T
    inv = 1.0 / 10000.0 ** (np.arange(0, hd, 2, dtype=np.float32) / hd)
    fr = np.outer(np.arange(s, dtype=np.float32), inv.astype(np.float32)).astype(np.float32)
    c, sn = np.cos(fr).astype(np.float32), np.sin(fr).astype(np.float32)
    r = np.stack([np.concatenate([c, c], 1), np.concatenate([sn, -sn], 1)], 1)
    r = np.ascontiguousarray(r.reshape(2, 128, 2, hd).transpose(1, 0, 2, 3))
    return {
        "ident": np.eye(128, dtype=np.float32),
        "ident16": bf16_bits(np.eye(128)),
        "masks": bf16_bits(m),
        "rope": r,
        "order": np.tile(np.arange(8, 0, -1, dtype=np.float32), (128, 1)),
    }


def kernel(**inputs):
    import numpy as np
    import concourse.bacc as bacc
    from concourse import mybir as mb
    from concourse.bass_utils import run_bass_kernel_spmd

    nc = bacc.Bacc("TRN2", target_bir_lowering=False, num_devices=1)
    arrays, args = {}, {}
    named = {k: np.asarray(v) for k, v in inputs.items()}
    named["b1_cols"] = np.ascontiguousarray(named.pop("L0_ffn_b1").reshape(8, 128).T)
    named.update(shape_constants())
    for name, a in named.items():
        a = np.ascontiguousarray(a)
        arrays[f"in_{name}"] = a
        args[name] = nc.dram_tensor(f"in_{name}", a.shape, mb.dt.from_np(a.dtype), kind="ExternalInput").ap()
    out = nc.dram_tensor("out_0", (4, 256, 256), mb.dt.float32, kind="ExternalOutput").ap()
    post_ln_decoder_two_layers(nc, args, out)
    r = run_bass_kernel_spmd(nc, [arrays], core_ids=[0])
    return r.results[0]["out_0"]
```

```python
import concourse.bass as bass
from concourse import mybir
from contextlib import ExitStack

STAGES = 6


def post_ln_decoder_two_layers(nc: bass.Bass, t: dict, out: bass.AP):
    F32 = mybir.dt.float32
    BF16 = mybir.dt.bfloat16
    I32 = mybir.dt.int32
    ALU = mybir.AluOpType
    ACT = mybir.ActivationFunctionType
    X = mybir.AxisListType.X

    P = 128
    B, S, D = t["x"].shape
    TT = B * S // P
    DC = D // P
    H, HD = 16, 16
    KV0 = t["L0_attn_Wk"].shape[0] // HD
    KVH = [KV0, H]
    HG = 4
    NG = H // HG
    PIECES = 6
    STK = PIECES * HD
    MROW = STK
    VW = 2 * HD
    FF = t["L0_ffn_w1"].shape[0]
    FCH = FF // P
    LAT = t["L1_attn_Wkv_down"].shape[0]
    CX = t["ctx_1024"].shape[2]
    E = t["L1_ffn_gate_w"].shape[0]
    EI = t["L1_ffn_w2"].shape[2]
    IB = P // E
    EC = EI // IB
    NEG_SCALE = float(HD) ** -0.5
    LN_EPS = 1e-5
    RMS_EPS = 1.1920929e-07
    Q_EPS = 1e-6
    MAGIC = 12582912.0
    RSQRT_SEED = 0x5F3759DF

    with ExitStack() as ctx:
        def sb(name, shape, dt=F32):
            return ctx.enter_context(nc.sbuf_tensor(name, shape, dt))

        def sem(name):
            return ctx.enter_context(nc.semaphore(name))

        PS = ctx.enter_context(nc.psum_tensor("PS", [P, 8, 512], F32))

        def bank(i, cols=512, off=0, rows=P):
            return PS[0:rows, i, off:off + cols]

        def bank16(i, cols=1024, off=0, rows=P):
            return PS[0:rows, i, :].bitcast(BF16)[:, off:off + cols]

        x = sb("x", [P, TT, D])
        xb = sb("xb", [P, TT, D])
        xT = sb("xT", [P, DC, B * S])
        ident = sb("ident", [P, P])
        ident16 = sb("ident16", [P, P], BF16)
        ones = sb("ones", [P, P])
        stat = sb("stat", [P, 4, 6])
        mv = sb("mv", [P, 4, 2])
        va = sb("va", [P, 4])
        rstd = sb("rstd", [P, 4])
        nt = sb("nt", [P, 4])
        res = sb("res", [P, 2, 2, D])

        wqkvT = sb("wqkvT", [P, DC, D + 2 * KV0 * HD])
        woT = [sb("woT0", [P, DC, D]), sb("woT1", [P, DC, D])]
        bqkv = sb("bqkv", [P, D + 2 * KV0 * HD])
        bo = sb("bo", [P, D])
        gain = sb("gain", [P, H])
        rope = sb("rope", [P, 2, 2, HD])
        masks = sb("masks", [P, 2, 6 * P], BF16)
        wqT1 = sb("wqT1", [P, DC, D])
        wdT = sb("wdT", [P, DC, LAT])
        wupT = sb("wupT", [LAT, 2 * D])
        b1 = sb("b1", [P, FCH])
        b2 = sb("b2", [P, D])
        xwT = sb("xwT", [P, 2, CX])
        xbias = sb("xbias", [P, 2])
        ctxT = sb("ctxT", [P, B, S])
        attT = sb("attT", [P, B, 2, S])
        gwT = sb("gwT", [P, DC, E])
        order = sb("order", [P, E])

        ARENA = 25600
        arena = sb("arena", [P, ARENA])

        def carve(off, shape, dt=F32):
            n = 1
            for k in shape[1:]:
                n *= k
            words = n if dt == F32 else n // 2
            assert off + words <= ARENA, (off, shape)
            v = arena[0:shape[0], off:off + words]
            if dt != F32:
                v = v.bitcast(dt)
            names = "abcdef"[:len(shape) - 1]
            if len(shape) > 2:
                v = v.rearrange(f"p ({' '.join(names)}) -> p {' '.join(names)}",
                                **{names[i]: shape[i + 1] for i in range(len(shape) - 1)})
            return v

        Qh = carve(0, [P, B, H, S], BF16)
        Kh = carve(8192, [P, B, H, S], BF16)
        qst = carve(16384, [P, 2, 2 * H * STK], BF16)
        kst = carve(19456, [P, 2, 2 * H * STK], BF16)
        Kh0 = carve(8192, [P, B, KV0, S], BF16)
        kst0 = carve(19456, [P, 2, 2 * KV0 * STK], BF16)
        V1 = sb("V1", [P, TT, H, VW])
        rem = carve(22528, [P, 2, 2 * 2 * H * HD])
        PT = sb("PT", [P, 2, 3 * 512])
        on = sb("on", [P, 2, 2, D])
        OT = sb("OT", [P, 2, DC, S])
        att_words = attT[:, :, :, :].rearrange("p a b c -> p (a b c)")
        qk = att_words[:, 0:1280].rearrange("p (a b c) -> p a b c", a=2, b=2)
        qsq = att_words[:, 1280:1920].rearrange("p (a b) -> p a b", a=2)
        qro = sb("qro", [P, 2, (H + KV0) * HD])
        qss = sb("qss", [P, 2 * (H + KV0)])
        qrs = sb("qrs", [P, 2 * (H + KV0)])
        qnt = sb("qnt", [P, 2 * (H + KV0)])
        latT = xb[0:LAT, 0:4, :].rearrange("p a b -> p (a b)")
        mx = sb("mx", [P, 2, 2, H])
        mxr = sb("mxr", [P, 2, 2, H])
        mst = sb("mst", [P, 2, 2, 3, H], BF16)
        mT = sb("mT", [3 * H, 2, S], BF16)
        rsum = sb("rsum", [P, 2, 2, HG])
        OS = sb("OS", [P, 2, S])

        f_nat = carve(10240, [P, B, 2, D])
        c_nat = carve(12288, [P, B, 2, CX])
        w1n = carve(13312, [P, FCH, D])
        w1t = carve(15360, [P, FCH, D], BF16)
        w2n = carve(20224, [P, DC, FF])
        w2t = carve(13312, [P, DC, FF], BF16)
        tmpw = carve(24576, [P, 2048], BF16)
        wq1n = carve(16384, [P, DC, D])
        wo1n = carve(16896, [P, DC, D])
        wdn = carve(17408, [LAT, D])
        wkun = carve(17664, [P, 2, DC, LAT])
        xwn = carve(17920, [P, 2, CX])
        gwn = carve(18176, [E, D])
        m1n = carve(16384, [P, 2, EC, D])
        m2n = carve(22016, [P, DC, E * EI])
        mw1T = [carve(0, [P, 2, EC * P]), carve(8192, [P, 2, EC * P])]
        mw2T = carve(2816, [P, EC, D])
        fT = carve(19456, [P, B, DC, S])
        xqk = carve(0, [P, 2, B * S])
        xP = carve(2048, [P, 2, 2, S])
        wq0n = carve(0, [P, DC + 1, D])
        wo0n = carve(768, [P, DC, D])
        xmx = sb("xmx", [P, 2, 2])
        xsm = sb("xsm", [P, 2, 2])
        tsum = sb("tsum", [P, 2])
        tthr = sb("tthr", [P, 2, 2])

        amx = sb("amx", [P, 2, B * DC])
        qs = sb("qs", [P, 4, B * DC])
        xw = carve(0, [P, B, 2, DC, S])
        q32 = carve(8192, [P, 2, 4, D])
        q16 = carve(10240, [P, 2, 4, D], BF16)
        qT = carve(11264, [P, B, 2, DC, S], BF16)
        rsc = sb("rsc", [P, B, 4])
        rrq = sb("rrq", [P, B, 4])
        wbc = carve(15360, [P, 2, D])
        hh = carve(15872, [P, 2, 2, D])
        sg = carve(16896, [P, 2, 2, D // 2])
        aa = carve(17408, [P, B, 2, D // 2])
        aT = carve(18432, [P, B, S])
        xw2 = carve(0, [P, B, 2, S])
        y2 = carve(21504, [P, 2, 2, D])

        x3 = carve(0, [P, 3, DC, B * S], BF16)
        xrem = carve(3072, [P, 2, DC, S])
        hT = carve(4096, [P, FCH, B * S])
        w1T = carve(22528, [P, DC, FF], BF16)
        w2T = carve(23552, [P, FCH, D])

        gl = sb("gl", [P, TT, E])
        gp = sb("gp", [P, TT, E])
        gq = sb("gq", [P, TT, E])
        gr = sb("gr", [P, TT, E])
        oh = sb("oh", [P, 2, TT, E])
        g1 = sb("g1", [P, 6, TT])
        GB = carve(16384, [P, B * S])
        sgm = carve(17408, [P, 2, 512])
        um = carve(18432, [P, 2, 512])
        am = carve(19456, [P, 2, 512])
        combw = carve(20480, [P, TT, E, IB])

        x_loaded = sem("x_batch0_loaded")
        x_rest_loaded = sem("x_rest_loaded")
        w_loaded = {k: sem(f"{k}_loaded") for k in
                    ("ident", "const", "l0", "f", "c", "w1", "w2", "l1", "xw", "gate", "m1", "m2")}
        bias_loaded = sem("bias_loaded")
        ones_set = sem("ones_set")
        krow_set = sem("krow_set")
        wt_done = sem("wt_transposed")
        wt_act = sem("wt_evacuated_by_act")
        wt_dve = sem("wt_evacuated_by_dve")
        v_step = sem("v_step")
        a_step = sem("a_step")
        p_step = sem("p_step")
        xtr_done = sem("x_transposed")
        xT_ready = sem("xT_ready")
        x_normed = sem("x_normed")
        out_read = sem("out_read")
        y_done = sem("y_done")
        xb_ready = sem("xb_ready")
        stored = sem("stored")
        abs_sum = sem("abs_sum")
        abs_tot = sem("abs_tot")
        thr_ready = sem("thr_ready")
        low_ready = sem("low_ready")
        tern_ready = sem("tern_ready")
        A = [{k: sem(f"l{L}_{k}") for k in
              ("proj", "proj_read", "lat", "lat_ready", "v_ready", "hi", "rem", "mid", "lo", "stk_tr",
               "sq", "ev_act", "ev_dve", "smax", "mx", "mst", "mtr", "mT", "mrow", "sT", "pT", "av", "os", "ot2", "on",
               "otr", "OT")} for L in range(2)]
        Q = {k: sem(f"q_{k}") for k in
             ("xw", "nat", "q32", "q16", "qtr", "qT", "h", "wtr", "wbc", "hh", "sg", "aa", "atr", "aT",
              "xw2", "nat2", "q32b", "q16b", "qtr2", "qT2", "wtr2", "wbc2")}
        Fs = {k: sem(f"f_{k}") for k in ("hi", "rem", "mid", "lo", "up", "gelu", "b")}
        Xs = {k: sem(f"x_{k}") for k in ("proj", "qk", "en", "mx", "exp", "norm", "tr", "attT")}
        Ms = {k: sem(f"m_{k}") for k in ("logit", "lg", "exp", "comb", "ctr", "GB", "gu", "sg", "um", "am")}

        G = []

        def group(srcs, dst, rows, cols, half, need):
            G.append((srcs, dst, rows, cols, half, need))

        for dc in range(DC):
            group([wq0n[:, r, dc * P:(dc + 1) * P] for r in range(3)], wqkvT[:, dc, :], P, 384, False, "l0")
        for w, n in ((wo0n, 0),):
            group([w[:, r, dc * P:(dc + 1) * P] for dc in range(DC) for r in range(2)],
                  woT[n][:, :, :].rearrange("p a b -> p (a b)"), P, 512, False, "l0")
        NG0 = len(G)
        for b in range(0, B, 2):
            group([c_nat[:, b + k, r, :] for k in range(2) for r in range(2)],
                  ctxT[:, b:b + 2, :].rearrange("p a b -> p (a b)"), P, 512, False, "c")
        group([xwn[:, k, :] for k in range(2)], xwT[:, :, :].rearrange("p a b -> p (a b)"), P, 256, False, "xw")
        group([wq1n[:, r, dc * P:(dc + 1) * P] for dc in range(DC) for r in range(2)],
              wqT1[:, :, :].rearrange("p a b -> p (a b)"), P, 512, False, "l1")
        group([wo1n[:, r, dc * P:(dc + 1) * P] for dc in range(DC) for r in range(2)],
              woT[1][:, :, :].rearrange("p a b -> p (a b)"), P, 512, False, "l1")
        group([wdn[:, dc * P:(dc + 1) * P] for dc in range(DC)],
              wdT[:, :, :].rearrange("p a b -> p (a b)"), P, DC * LAT, False, "l1")
        group([wkun[:, k, r, :] for k in range(2) for r in range(2)], wupT[:, :], LAT, 512, False, "l1")
        group([gwn[:, dc * P:(dc + 1) * P] for dc in range(DC)],
              gwT[:, :, :].rearrange("p a b -> p (a b)"), P, DC * E, False, "gate")
        for dc in range(DC):
            group([w1t[:, f, dc * P:(dc + 1) * P] for f in range(FCH)], w1T[:, dc, :], P, 1024, True, "t1")
        for k in range(2):
            group([w2t[:, r, f * P:(f + 1) * P] for f in range(4 * k, 4 * k + 4) for r in range(2)],
                  w2T[:, 4 * k:4 * k + 4, :].rearrange("p a b -> p (a b)"), P, 1024, True, "t2")
        for b in range(B):
            group([f_nat[:, b, r, dc * P:(dc + 1) * P] for dc in range(DC) for r in range(2)],
                  fT[:, b, :, :].rearrange("p a b -> p (a b)"), P, 512, False, "f")
        NGM = len(G)
        for dc in range(DC):
            for gu in range(2):
                for c0 in range(0, EC, 4):
                    n = min(4, EC - c0)
                    group([m1n[:, gu, c, dc * P:(dc + 1) * P] for c in range(c0, c0 + n)],
                          mw1T[dc][:, gu, c0 * P:(c0 + n) * P], P, n * P, False, "m1")
        NG2 = len(G)
        for c0 in range(0, EC, 2):
            n = min(2, EC - c0)
            group([m2n[:, r, c::EC] for c in range(c0, c0 + n) for r in range(2)],
                  mw2T[:, c0:c0 + n, :].rearrange("p a b -> p (a b)"), P, n * 256, False, "m2")

        LOADS = {"l0": 16 * 4, "f": 16, "c": 16, "w1": 16, "w2": 16, "l1": 16 * 5, "xw": 32, "gate": 16,
                 "m1": 16 * 16, "m2": 32, "const": 16 * 4, "ident": 16}

        BESIDE = set(range(NG0, NGM)) | set(range(NGM, NG2))
        PLAN = []
        for k in range(len(G)):
            bank_ = (k % 2) if k in BESIDE else (k % 4)
            eng_ = "dve" if k in BESIDE or k % 2 else "act"
            before = [j for j in range(k) if PLAN[j][0] == bank_]
            PLAN.append((bank_, eng_, 1 + sum(p[1] == eng_ for p in PLAN), before[-1] if before else None))

        def copied_out(eng, upto):
            for name, s_ in (("act", wt_act), ("dve", wt_dve)):
                n = sum(p[1] == name for p in PLAN[:upto])
                if n:
                    eng.wait_ge(s_, n)

        def pe_groups(pe, lo, hi):
            for k in range(lo, hi):
                srcs, dst, rows, cols, half, need = G[k]
                if need in ("t1", "t2"):
                    pe.wait_ge(tern_ready, int(need[1]))
                else:
                    pe.wait_ge(w_loaded[need], LOADS[need])
                bk, _, _, prev = PLAN[k]
                if prev is not None:
                    pe.wait_ge(wt_act if PLAN[prev][1] == "act" else wt_dve, PLAN[prev][2])
                w = cols // len(srcs)
                for i, s in enumerate(srcs):
                    K = s.shape[0]
                    o = (bank16 if half else bank)(bk, w, i * w, rows)
                    last = nc.tensor.transpose(o, s, (ident16 if half else ident)[0:K, 0:K])
                last.then_inc(wt_done, 1)

        def evac_groups(eng, copy, lo, hi, name):
            for k in range(lo, hi):
                srcs, dst, rows, cols, half, need = G[k]
                if PLAN[k][1] == name:
                    eng.wait_ge(wt_done, k + 1)
                    copy(dst, (bank16 if half else bank)(PLAN[k][0], cols, 0, rows))\
                        .then_inc(wt_act if name == "act" else wt_dve, 1)

        LAG = 2
        STEPS = B + LAG

        def score_set(m):
            return 3 * (m % 2) if m < LAG * NG else 0

        def beside(L, step, g):
            lo, hi = (NG0, NGM) if L == 0 else (NGM, NG2)
            slot = (step - B) * NG + g
            if slot < 0:
                return 0, 0
            per = -(-(hi - lo) // (LAG * NG))
            a_ = min(lo + slot * per, hi)
            return a_, min(a_ + per, hi)

        def early_loads(sp):
            w = w_loaded
            sp.dma_start(w1n, t["L0_ffn_w1"].rearrange("(r p) d -> p r d", p=P)).then_inc(w["w1"], 16)
            sp.dma_start(w2n, t["L0_ffn_w2"].rearrange("(r p) d -> p r d", p=P)).then_inc(w["w2"], 16)
            sp.dma_start(c_nat.rearrange("p b r d -> p (b r) d"),
                         t["ctx_1024"].rearrange("b (r p) d -> p (b r) d", p=P)).then_inc(w["c"], 16)
            sp.dma_start(f_nat.rearrange("p b r d -> p (b r) d"),
                         t["fside_BxS2xS2_0"].rearrange("b (r p) d -> p (b r) d", p=P)).then_inc(w["f"], 16)

        def late_loads(sp):
            w = w_loaded
            sp.wait_ge(A[0]["stk_tr"], B * TG[0])
            sp.dma_start(xwn[:, 0, :], t["L1_xattn_Wq"]).then_inc(w["xw"], 16)
            sp.dma_start(xwn[:, 1, :], t["L1_xattn_Wk"]).then_inc(w["xw"], 16)
            sp.dma_start(wq1n, t["L1_attn_Wq"].rearrange("(r p) d -> p r d", p=P)).then_inc(w["l1"], 16)
            sp.dma_start(wo1n, t["L1_attn_Wo"].rearrange("(r p) d -> p r d", p=P)).then_inc(w["l1"], 16)
            sp.dma_start(wdn, t["L1_attn_Wkv_down"]).then_inc(w["l1"], 16)
            sp.dma_start(wkun[:, 0, :, :], t["L1_attn_Wk_up"].rearrange("(r p) d -> p r d", p=P)).then_inc(w["l1"], 16)
            sp.dma_start(wkun[:, 1, :, :], t["L1_attn_Wv_up"].rearrange("(r p) d -> p r d", p=P)).then_inc(w["l1"], 16)
            sp.dma_start(gwn, t["L1_ffn_gate_w"]).then_inc(w["gate"], 16)

        def expert_loads(sp):
            w = w_loaded
            sp.wait_ge(A[1]["stk_tr"], B * TG[1])
            sp.wait_ge(A[1]["lo"], TT)
            for e in range(E):
                for gu in range(2):
                    src = t["L1_ffn_w1"][e, gu * EI:(gu + 1) * EI, :].rearrange("(i c) d -> i c d", c=EC)
                    sp.dma_start(m1n[e * IB:(e + 1) * IB, gu, :, :], src).then_inc(w["m1"], 16)
            for r in range(2):
                sp.dma_start(m2n[:, r, :].rearrange("p (e i) -> p e i", e=E), t["L1_ffn_w2"][:, r * P:(r + 1) * P, :].rearrange("e h i -> h e i")).then_inc(w["m2"], 16)

        def mrow_dmas(sp, L):
            for b in range(B):
                sp.wait_ge(A[L]["mT"], b + 1)
                for k in range(3):
                    sp.dma_start(Qh[MROW + k:MROW + k + 1, b, :, :],
                                 mT[k * H:(k + 1) * H, b % 2, :]).then_inc(A[L]["mrow"], 16)


        am_read = sem("am_read")

        Q_SLOTS = {"hi": (0, 3, 1), "mid": (3, 5, 1), "lo": (5, 6, 1)}
        K_SLOTS = {"hi": (1, 6, 2), "mid": (2, 5, 2), "lo": (0, 1, 1)}

        def stack_buffer(L, slot, which):
            buf = qst if which == "q" else (kst0 if L == 0 else kst)
            return buf[:, slot % 2, :]

        def stack(L, u, which, part):
            nh = H if which == "q" else KVH[L]
            if L == 0:
                rows = stack_buffer(0, u, which)[:, 0:2 * nh * STK]
                nh = 2 * nh
            else:
                rows = stack_buffer(1, u // 2, which)[:, (u % 2) * nh * STK:(u % 2 + 1) * nh * STK]
            buf = rows.rearrange("p (h s d) -> p h s d", h=nh, s=PIECES)
            lo, hi, st = (Q_SLOTS if which == "q" else K_SLOTS)[part]
            return buf[:, :, lo:hi:st, :]

        def part_source(L, u, which):
            if L == 0:
                a = qro[:, :, 0:D] if which == "q" else qro[:, :, D:D + KV0 * HD]
                return a.rearrange("p t (h d) -> p t h d", d=HD)
            o = 0 if which == "q" else D
            return bank(2 * (u % 2), D, o).rearrange("p (h d) -> p h d", d=HD)

        def remainder(L, u, which):
            nh = (2 * H if which == "q" else 2 * KVH[0]) if L == 0 else H
            o = 0 if which == "q" else 2 * H * HD
            return rem[:, u % 2, o:o + nh * HD].rearrange("p (h d) -> p h d", d=HD)

        def stack_views(L, u, part):
            res_ = []
            for which in "qk":
                dst = stack(L, u, which, part)
                src = remainder(L, u, which)
                n = dst.shape[2]
                res_.append((src.unsqueeze(2).to_broadcast([P, dst.shape[1], n, HD]), dst))
            return res_

        def tr_groups(L, b):
            gs = []
            for which, nh, dst in (("k", KVH[L], Kh0 if L == 0 else Kh), ("q", H, Qh)):
                buf = stack_buffer(L, b, which)[:, 0:2 * nh * STK].rearrange("p (t h s) -> p t h s", t=2, h=nh)
                for g in range(nh // HG):
                    srcs = [buf[:, half, h, :] for h in range(HG * g, HG * g + HG) for half in range(2)]
                    gs.append((srcs, dst[0:STK, b, HG * g:HG * g + HG, :].rearrange("p a b -> p (a b)")))
            return gs

        TG = [KVH[L] // HG + NG for L in range(2)]

        def stack_evac(L, n):
            if L == 0:
                return "act", n + 1
            if n % 4 == 0:
                return "act", n // 4 + 1
            return "dve", n - n // 4


        bias_b1 = sem("b1_loaded")

        y_ready = sem("y_ready")

        def quant_transposes(pe, b):
            pe.wait_ge(Q["q16"], b + 1)
            if b >= 2:
                pe.wait_ge(Q["qT"], b - 1)
            for i in range(4):
                for c in range(DC):
                    last = nc.tensor.transpose(bank16(4 + b % 2, P, ((i // 2) * DC + c) * S + (i % 2) * P),
                                               q16[:, b % 2, i, c * P:(c + 1) * P], ident16[:, :])
            last.then_inc(Q["qtr"], 1)

        def quant_transposes2(pe, b):
            pe.wait_ge(Q["q16b"], b + 1)
            if b >= 2:
                pe.wait_ge(Q["qT2"], b - 1)
            for i in range(4):
                last = nc.tensor.transpose(bank16(4 + b % 2, P, i * P), q16[:, b % 2, i, 0:CX], ident16[:, :])
            last.then_inc(Q["qtr2"], 1)

        block = ctx.enter_context(nc.Block())

        @block.sync
        def _(sp):
            w = w_loaded
            xv = t["x"].rearrange("b (h p) d -> p (b h) d", p=P)
            sp.dma_start(ident[:, :], t["ident"]).then_inc(w["ident"], 16)
            sp.dma_start(wq0n[:, 0:2, :], t["L0_attn_Wq"].rearrange("(r p) d -> p r d", p=P)).then_inc(w["l0"], 16)
            sp.dma_start(wq0n[0:64, 2, :], t["L0_attn_Wk"]).then_inc(w["l0"], 16)
            sp.dma_start(wq0n[64:128, 2, :], t["L0_attn_Wv"]).then_inc(w["l0"], 16)
            sp.dma_start(wo0n[:, :, :], t["L0_attn_Wo"].rearrange("(r p) d -> p r d", p=P)).then_inc(w["l0"], 16)
            sp.dma_start(x[:, 0:2, :], xv[:, 0:2, :]).then_inc(x_loaded, 16)
            sp.dma_start(x[:, 2:TT, :], xv[:, 2:TT, :]).then_inc(x_rest_loaded, 16)
            early_loads(sp)
            late_loads(sp)
            mrow_dmas(sp, 0)
            if STAGES > 3:
                expert_loads(sp)
                mrow_dmas(sp, 1)
            ov = out.rearrange("b (h p) d -> p (b h) d", p=P)
            for b in range(B):
                sp.wait_ge(x_normed, 4 * (STAGES - 1) + b + 1)
                sp.dma_start(ov[:, 2 * b:2 * b + 2, :], x[:, 2 * b:2 * b + 2, :]).then_inc(stored, 16)
            sp.wait_ge(stored, 16 * B)
        @block.gpsimd
        def _(pool):
            w = w_loaded
            count = {}

            def alone(ins, signal=p_step):
                count[signal.name] = count.get(signal.name, 0) + 1
                ins.then_inc(signal, 1)
                pool.wait_ge(signal, count[signal.name])

            alone(pool.memset(ones[:, :], 1.0), ones_set)
            alone(pool.memset(V1[:, :, :, HD:VW], 1.0), ones_set)
            alone(pool.memset(Kh0[MROW:MROW + 3, :, :, :].rearrange("p a b c -> p (a b c)"), -1.0), krow_set)

            def residual_bias(stage, bias):
                for b in range(B):
                    if stage == 0:
                        pool.wait_ge(x_rest_loaded if b else x_loaded, 16)
                        if b == 0:
                            pool.wait_ge(bias_loaded, 16 * 8)
                    else:
                        pool.wait_ge(x_normed, 4 * stage + b - 4 + 1)
                    for k in range(2):
                        alone(pool.tensor_tensor(xb[:, 2 * b + k, :], x[:, 2 * b + k, :], bias[:, :], ALU.add),
                              xb_ready if k else p_step)

            def sub_magic(n, q32_, q16_, ready, done):
                for b in range(B):
                    pool.wait_ge(ready, b + 1)
                    if b >= 2:
                        pool.wait_ge(Q["qtr"] if n == 0 else Q["qtr2"], b - 1)
                    alone(pool.tensor_scalar(q16_[:, b % 2], q32_[:, b % 2], -MAGIC, None, ALU.add), done)

            residual_bias(0, bo)
            for k, (wn, wt) in enumerate(((w1n, w1t), (w2n, w2t))):
                pool.wait_ge(thr_ready, k + 1)
                if k == 1:
                    pool.wait_ge(tern_ready, 1)
                alone(pool.tensor_scalar(tmpw, wn.rearrange("p a b -> p (a b)"), tthr[:, k, 1:2], None, ALU.is_lt),
                      low_ready)
            if STAGES > 1:
                sub_magic(0, q32, q16, Q["q32"], Q["q16"])
                for b in range(B):
                    pool.wait_ge(Q["sg"], b + 1)
                    alone(pool.tensor_tensor(aa[:, b], sg[:, b % 2], hh[:, b % 2, :, D // 2:D], ALU.mult), Q["aa"])
                sub_magic(1, q32, q16, Q["q32b"], Q["q16b"])
            if STAGES > 2:
                residual_bias(2, b2)
            if STAGES > 3:
                pool.wait_ge(x_normed, 12)
                alone(pool.memset(Kh[MROW:MROW + 3, :, :, :].rearrange("p a b c -> p (a b c)"), -1.0), krow_set)
            if STAGES > 5:
                for n in range(2 * EC):
                    pool.wait_ge(Ms["um"], n + 1)
                    pool.wait_ge(Ms["sg"], n + 1)
                    if n >= 2:
                        pool.wait_ge(am_read, n - 1)
                    alone(pool.tensor_tensor(am[:, n % 2, :], sgm[:, n % 2, :], um[:, n % 2, :], ALU.mult), Ms["am"])


        @block.scalar
        def _(act):
            w = w_loaded
            act.dma_start(masks[:, :, :], t["masks"].bitcast(BF16)).then_inc(w["const"], 16)
            act.dma_start(rope[:, :, :, :], t["rope"]).then_inc(w["const"], 16)
            act.dma_start(order[:, :], t["order"]).then_inc(w["const"], 16)
            act.dma_start(ident16[:, :], t["ident16"].bitcast(BF16)).then_inc(w["const"], 16)
            act.dma_start(bqkv[:, 0:D], t["L0_attn_bq"].partition_broadcast(P)).then_inc(bias_loaded, 16)
            act.dma_start(bqkv[:, D:D + 64], t["L0_attn_bk"].partition_broadcast(P)).then_inc(bias_loaded, 16)
            act.dma_start(bqkv[:, D + 64:D + 128], t["L0_attn_bv"].partition_broadcast(P)).then_inc(bias_loaded, 16)
            act.dma_start(gain[:, :], t["L0_attn_q_gain"].partition_broadcast(P)).then_inc(bias_loaded, 16)
            act.dma_start(bo[:, :], t["L0_attn_bo"].partition_broadcast(P)).then_inc(bias_loaded, 16)
            act.dma_start(b2[:, :], t["L0_ffn_b2"].partition_broadcast(P)).then_inc(bias_loaded, 16)
            act.dma_start(xbias[:, 0:1], t["L1_xattn_bq"].unsqueeze(1)).then_inc(bias_loaded, 16)
            act.dma_start(xbias[:, 1:2], t["L1_xattn_bk"].unsqueeze(1)).then_inc(bias_loaded, 16)
            act.dma_start(b1[:, :], t["b1_cols"]).then_inc(bias_b1, 16)

            def copy(dst, src):
                return nc.scalar.activation(dst, src, ACT.Copy)

            def evac_xT(stage):
                for b in range(B):
                    act.wait_ge(xtr_done, 4 * stage + b + 1)
                    copy(xT[:, :, b * S:(b + 1) * S], bank(6 + b % 2).rearrange("p (c s) -> p c s", c=DC))\
                        .then_inc(xT_ready, 1)

            def abs_sums():
                for k, (wn, nm) in enumerate(((w1n, "w1"), (w2n, "w2"))):
                    act.wait_ge(w[nm], 16)
                    if k == 1:
                        act.wait_ge(abs_sum, 1)
                    nc.scalar.activation(tmpw, wn.rearrange("p a b -> p (a b)"), ACT.Abs,
                                         accum_out=tsum[:, k:k + 1]).then_inc(abs_sum, 1)

            def attn_front(L):
                a = A[L]
                if L == 1:
                    for n in range(2):
                        act.wait_ge(a["lat"], n + 1)
                        copy(latT[:, n * 512:(n + 1) * 512], bank(4 + n, 512, 0, LAT)).then_inc(a["lat_ready"], 1)
                for b in range(B):
                    units = (b,) if L == 0 else (2 * b, 2 * b + 1)
                    for u in units:
                        hi_part(L, u)
                    if L == 1 and b >= 1:
                        evac_stacks(L, b - 1)
                    for u in units:
                        mid_part(L, u)
                    if L == 0:
                        evac_stacks(L, b)
                    if L == 0 and b == 1:
                        abs_sums()
                if L == 1:
                    evac_stacks(L, B - 1)

            def evac_stacks(L, b):
                a = A[L]
                for g in range(TG[L]):
                    n = b * TG[L] + g
                    if stack_evac(L, n)[0] == "act":
                        act.wait_ge(a["stk_tr"], n + 1)
                        copy(tr_groups(L, b)[g][1], bank16(4 + n % 4, 1024, 0, STK)).then_inc(a["ev_act"], 1)

            def mid_part(L, u):
                a = A[L]
                act.wait_ge(a["rem"], u + 1)
                for src, dst in stack_views(L, u, "mid"):
                    last = copy(dst, src)
                last.then_inc(a["mid"], 1)

            def hi_part(L, u):
                a = A[L]
                act.wait_ge(a["sq"], u + 1) if L == 0 else act.wait_ge(a["proj"], u + 1)
                b = u if L == 0 else u // 2
                if b >= 2:
                    act.wait_ge(a["stk_tr"], (b - 1) * TG[L])
                for which in "qk":
                    dst = stack(L, u, which, "hi")
                    src = part_source(L, u, which)
                    if L == 0:
                        nh = H if which == "q" else KVH[0]
                        for half in range(2):
                            last = copy(dst[:, half * nh:(half + 1) * nh],
                                        src[:, half].unsqueeze(2).to_broadcast([P, nh, 3, HD]))
                    else:
                        last = copy(dst, src.unsqueeze(2).to_broadcast([P, H, 3, HD]))
                last.then_inc(a["hi"], 1)

            def copy_outputs(L, j):
                a = A[L]
                act.wait_ge(a["av"], j + 1)
                if j >= 2:
                    act.wait_ge(a["ot2"], j - 1)
                copy(OS[:, j % 2, :], bank(6, S)).then_inc(a["os"], 1)

            def copy_OT(L, b):
                a = A[L]
                act.wait_ge(a["otr"], b + 1)
                copy(OT[:, b % 2, :, :].rearrange("p a b -> p (a b)"), bank(7)).then_inc(a["OT"], 1)

            def attn_back(L):
                a = A[L]
                for step in range(STEPS):
                    for g in range(NG):
                        n = (step - LAG) * NG + g
                        if n >= 0:
                            act.wait_ge(a["sT"], n + 1)
                            if n >= 2:
                                act.wait_ge(a["av"], n - 1)
                            nc.scalar.activation(PT[:, n % 2, :], PS[:, 3:6, :].rearrange("p a b -> p (a b)"),
                                                 ACT.Exp, scale=NEG_SCALE).then_inc(a["pT"], 1)
                        if n >= 1:
                            copy_outputs(L, n - 1)
                        if g == 0 and 1 <= step <= B:
                            act.wait_ge(a["mtr"], step)
                            if step >= 3:
                                act.wait_ge(a["mrow"], 48 * (step - 2))
                            copy(mT[:, (step - 1) % 2, :], bank16(7, S, 0, 3 * H)).then_inc(a["mT"], 1)
                        if g == 1 and step > LAG:
                            copy_OT(L, step - LAG - 1)
                copy_outputs(L, B * NG - 1)
                copy_OT(L, B - 1)

            evac_groups(act, copy, 0, NG0, "act")
            evac_xT(0)
            attn_front(0)
            attn_back(0)
            if STAGES > 1:
                for n in range(2):
                    for k in range(2):
                        act.wait_ge(bias_loaded, 16 * 8)
                        act.wait_ge(Xs["proj"], 2 * n + k + 1)
                        nc.scalar.activation(xqk[:, k, n * 512:(n + 1) * 512], bank(4 + k), ACT.Identity,
                                             bias=xbias[:, k:k + 1]).then_inc(Xs["qk"], 1)
                for b in range(B):
                    act.wait_ge(Xs["mx"], b + 1)
                    if b >= 2:
                        act.wait_ge(Xs["tr"], b - 1)
                    for k in range(2):
                        last = nc.scalar.activation(xP[:, b % 2, k, :], bank(6 + b % 2, S, k * S), ACT.Exp,
                                                    bias=xmx[:, b % 2, k:k + 1], accum_out=xsm[:, b % 2, k:k + 1])
                    last.then_inc(Xs["exp"], 1)
                    act.wait_ge(Xs["tr"], b + 1)
                    copy(attT[:, b, :, :].rearrange("p a b -> p (a b)"), bank(4 + b % 2)).then_inc(Xs["attT"], 1)
                evac_xT(1)
                for b in range(B):
                    act.wait_ge(Q["qtr"], b + 1)
                    copy(qT[:, b].rearrange("p a b c -> p (a b c)"), bank16(4 + b % 2)).then_inc(Q["qT"], 1)
                for b in range(B):
                    act.wait_ge(Q["wtr"], b + 1)
                    if b >= 2:
                        act.wait_ge(Q["hh"], b - 1)
                    copy(wbc[:, b % 2, :], bank(b % 2, D)).then_inc(Q["wbc"], 1)
                    act.wait_ge(Q["hh"], b + 1)
                    if b >= 2:
                        act.wait_ge(Q["aa"], b - 1)
                    nc.scalar.activation(sg[:, b % 2], hh[:, b % 2, :, 0:D // 2], ACT.Silu).then_inc(Q["sg"], 1)
                for b in range(B):
                    act.wait_ge(Q["atr"], b + 1)
                    copy(aT[:, b, :], bank(2 + b % 2, S)).then_inc(Q["aT"], 1)
                for b in range(B):
                    act.wait_ge(Q["qtr2"], b + 1)
                    copy(qT[:, b, :, 0, :], bank16(4 + b % 2, 512).rearrange("p (a b) -> p a b", a=2)).then_inc(Q["qT2"], 1)
                for b in range(B):
                    act.wait_ge(Q["wtr2"], b + 1)
                    if b >= 2:
                        act.wait_ge(y_done, b - 1)
                    copy(wbc[:, b % 2, :], bank(b % 2, D)).then_inc(Q["wbc2"], 1)
            if STAGES > 2:
                act.wait_ge(bias_b1, 16)
                for b in range(B):
                    act.wait_ge(xtr_done, 4 * 2 + b + 1)
                    copy(xT[:, :, b * S:(b + 1) * S], bank(6 + b % 2).rearrange("p (c s) -> p c s", c=DC))\
                        .then_inc(xT_ready, 1)
                    act.wait_ge(xT_ready, 4 * 2 + b + 1)
                    copy(x3[:, 0, :, b * S:(b + 1) * S], xT[:, :, b * S:(b + 1) * S]).then_inc(Fs["hi"], 1)
                for n in range(2 * FCH):
                    blk, f = n // FCH, n % FCH
                    act.wait_ge(Fs["up"], n + 1)
                    nc.scalar.activation(hT[:, f, blk * 512:(blk + 1) * 512], bank(n % 2), ACT.Gelu,
                                         bias=b1[:, f:f + 1]).then_inc(Fs["gelu"], 1)
            if STAGES > 3:
                evac_xT(3)
                attn_front(1)
                attn_back(1)
            if STAGES > 4:
                evac_groups(act, copy, NG2, len(G), "act")
                evac_xT(4)
            if STAGES > 5:
                evac_xT(5)
                act.wait_ge(Ms["lg"], 1)
                nc.scalar.activation(gp[:, :, :], gl[:, :, :], ACT.Exp).then_inc(Ms["exp"], 1)
                for n in range(2 * EC):
                    act.wait_ge(Ms["gu"], n + 1)
                    if n >= 2:
                        act.wait_ge(Ms["am"], n - 1)
                    nc.scalar.activation(sgm[:, n % 2, :], bank(2 * (n % 2)), ACT.Silu).then_inc(Ms["sg"], 1)


        @block.vector
        def _(dve):
            v = nc.vector
            steps = [0]

            def link(ins):
                steps[0] += 1
                ins.then_inc(v_step, 1)
                dve.wait_ge(v_step, steps[0])

            def rsqrt(y, a, tmp):
                link(v.tensor_scalar(y.bitcast(I32), a.bitcast(I32), 1, None, ALU.logical_shift_right))
                link(v.tensor_scalar(y.bitcast(I32), y.bitcast(I32), -1.0, float(RSQRT_SEED), ALU.mult, ALU.add))
                for _ in range(3):
                    link(v.tensor_tensor(tmp, y, y, ALU.mult))
                    link(v.scalar_tensor_tensor(tmp, tmp, -0.5, a, ALU.mult, ALU.mult))
                    link(v.scalar_tensor_tensor(y, tmp, 1.5, y, ALU.add, ALU.mult))

            def add_residual(stage, b, y, base):
                if b % 2 == 0 and 4 * stage + b:
                    dve.wait_ge(x_normed, 4 * stage + b)
                v.tensor_tensor(res[:, b % 2], y, base[:, 2 * b:2 * b + 2, :], ALU.add).then_inc(out_read, 1)

            def norm_pair(stage, b):
                dve.wait_ge(out_read, 4 * stage + b + 2)
                for i in range(4):
                    ins = v.bn_stats(stat[:, i, :], res[:, i // 2, i % 2, :])
                link(ins)
                for i in range(4):
                    ins = v.bn_aggr(mv[:, i, :], stat[:, i, :])
                link(ins)
                link(v.tensor_scalar(va[:, :], mv[:, :, 1], LN_EPS, None, ALU.add))
                rsqrt(rstd[:, :], va[:, :], nt[:, :])
                for i in range(4):
                    ins = v.tensor_scalar(x[:, 2 * b + i, :], res[:, i // 2, i % 2, :], mv[:, i, 0:1], rstd[:, i:i + 1],
                                          ALU.subtract, ALU.mult)
                    if i % 2:
                        ins.then_inc(x_normed, 1)

            def rem_part(L, u):
                a = A[L]
                if u >= 2:
                    dve.wait_ge(a["lo"], u - 1)
                dve.wait_ge(a["hi"], u + 1)
                for which in "qk":
                    hi = stack(L, u, which, "hi")[:, :, 0, :]
                    src = part_source(L, u, which)
                    dst = remainder(L, u, which)
                    if L == 0:
                        nh = H if which == "q" else KVH[0]
                        for half in range(2):
                            ins = v.tensor_tensor(dst[:, half * nh:(half + 1) * nh], src[:, half],
                                                  hi[:, half * nh:(half + 1) * nh], ALU.subtract)
                    else:
                        ins = v.tensor_tensor(dst, src, hi, ALU.subtract)
                ins.then_inc(a["rem"], 1)

            def lo_part(L, u):
                a = A[L]
                dve.wait_ge(a["mid"], u + 1)
                for which in "qk":
                    mid = stack(L, u, which, "mid")[:, :, 0, :]
                    ins = v.tensor_tensor(stack(L, u, which, "lo")[:, :, 0, :], remainder(L, u, which), mid, ALU.subtract)
                ins.then_inc(a["lo"], 1)

            def evac_stacks(b):
                a = A[1]
                for g in range(TG[1]):
                    n = b * TG[1] + g
                    if stack_evac(1, n)[0] == "dve":
                        dve.wait_ge(a["stk_tr"], n + 1)
                        v.tensor_copy(tr_groups(1, b)[g][1], bank16(4 + n % 4, 1024, 0, STK)).then_inc(a["ev_dve"], 1)

            def thresholds():
                for k in range(2):
                    dve.wait_ge(abs_tot, k + 1)
                    link(v.tensor_scalar(tthr[:, k, 0:1], bank(2 + k, 1), 1.0 / (FF * D), 1e-8, ALU.mult, ALU.max))
                    link(v.tensor_scalar(tthr[:, k, 0:1], tthr[:, k, 0:1], 0.5, None, ALU.mult))
                    v.tensor_scalar(tthr[:, k, 1:2], tthr[:, k, 0:1], -1.0, None, ALU.mult).then_inc(thr_ready, 1)

            def ternary(k):
                wn, wt = ((w1n, w1t), (w2n, w2t))[k]
                dve.wait_ge(low_ready, k + 1)
                v.scalar_tensor_tensor(wt.rearrange("p a b -> p (a b)"), wn.rearrange("p a b -> p (a b)"),
                                       tthr[:, k, 0:1], tmpw, ALU.is_gt, ALU.subtract).then_inc(tern_ready, 1)

            def read_projections(b):
                a = A[0]
                for k in range(2):
                    tt = 2 * b + k
                    dve.wait_ge(a["proj"], tt + 1)
                    v.tensor_tensor(V1[:, tt, 0:KV0, 0:HD],
                                    bank(k, 64, D + 64).rearrange("p (h d) -> p h d", d=HD),
                                    bqkv[:, D + 64:D + 128].rearrange("p (h d) -> p h d", d=HD),
                                    ALU.add).then_inc(a["v_ready"], 1)
                    v.tensor_tensor(qk[:, b % 2, k, :], bank(k, D + 64), bqkv[:, 0:D + 64], ALU.add)\
                        .then_inc(a["proj_read"], 1)

            def attn_front(L):
                a = A[L]
                for b in range(B):
                    if L == 0:
                        if b == 0:
                            dve.wait_ge(bias_loaded, 16 * 8)
                            dve.wait_ge(w_loaded["const"], LOADS["const"])
                            read_projections(0)
                        dve.wait_ge(a["proj_read"], 2 * b + 2)
                        q2 = qk[:, b % 2].rearrange("p t n -> p (t n)")
                        sq = qsq[:, :, :].rearrange("p t n -> p (t n)")
                        ro = qro[:, :, :].rearrange("p t n -> p (t n)")
                        NHB = 2 * (H + KV0)
                        link(v.tensor_tensor(sq, q2, q2, ALU.mult))
                        link(v.tensor_reduce(qss[:, :], sq.rearrange("p (h d) -> p h d", d=HD), X, ALU.add))
                        link(v.tensor_scalar(qss[:, :], qss[:, :], 1.0 / HD, RMS_EPS, ALU.mult, ALU.add))
                        rsqrt(qrs[:, :], qss[:, :], qnt[:, :])
                        rq = qrs[:, :].rearrange("p (t h) -> p t h", t=2)[:, :, 0:H]
                        link(v.tensor_tensor(rq, rq, gain[:, :].unsqueeze(1).to_broadcast([P, 2, H]), ALU.mult))
                        q3 = q2.rearrange("p (h d) -> p h d", d=HD)
                        link(v.tensor_tensor(q3, q3, qrs[:, :].unsqueeze(2).to_broadcast([P, NHB, HD]), ALU.mult))
                        if b >= 1:
                            dve.wait_ge(a["lo"], b)
                        hf = HD // 2
                        for k in range(2):
                            qi = qk[:, b % 2, k, :].rearrange("p (h d) -> p h d", d=HD)
                            ri = qro[:, k, :].rearrange("p (h d) -> p h d", d=HD)
                            si = qsq[:, k, :].rearrange("p (h d) -> p h d", d=HD)
                            nh = H + KV0
                            cos = rope[:, k, 0, :].unsqueeze(1).to_broadcast([P, nh, HD])
                            s1 = rope[:, k, 1, 0:hf].unsqueeze(1).to_broadcast([P, nh, hf])
                            s2 = rope[:, k, 1, hf:HD].unsqueeze(1).to_broadcast([P, nh, hf])
                            v.tensor_tensor(ri, qi, cos, ALU.mult)
                            v.tensor_tensor(si[:, :, 0:hf], qi[:, :, hf:HD], s1, ALU.mult)
                            link(v.tensor_tensor(si[:, :, hf:HD], qi[:, :, 0:hf], s2, ALU.mult))
                        v.tensor_tensor(ro, ro, sq, ALU.add).then_inc(a["sq"], 1)
                        rem_part(L, b)
                        if b == 2:
                            thresholds()
                        if b + 1 < B:
                            read_projections(b + 1)
                        lo_part(L, b)
                    else:
                        for u in (2 * b, 2 * b + 1):
                            rem_part(L, u)
                            v.tensor_copy(V1[:, u, :, 0:HD],
                                          bank(2 * (u % 2) + 1, D).rearrange("p (h d) -> p h d", d=HD))\
                                .then_inc(a["v_ready"], 1)
                        if b >= 1:
                            evac_stacks(b - 1)
                        for u in (2 * b, 2 * b + 1):
                            lo_part(L, u)
                if L == 1:
                    evac_stacks(B - 1)

            def row_maxima(L, b, g, m):
                a = A[L]
                set_ = score_set(m)
                dve.wait_ge(a["smax"], 2 * m + 1)
                v.tensor_reduce(mx[:, b % 2, 0, HG * g:HG * g + HG],
                                bank(set_).rearrange("p (h s) -> p h s", h=HG), X, ALU.max).then_inc(a["mx"], 1)
                dve.wait_ge(a["smax"], 2 * m + 2)
                v.tensor_reduce(mx[:, b % 2, 1, HG * g:HG * g + HG],
                                PS[:, set_ + 1:set_ + 3, :].rearrange("p a (h s) -> p (a h) s", h=2), X, ALU.max)\
                    .then_inc(a["mx"], 1)

            def divide_outputs(L, j):
                a = A[L]
                b, g = j // NG, j % NG
                dve.wait_ge(a["ot2"], j + 1)
                o = bank(6, S, S).rearrange("p (t h d) -> p t h d", t=2, h=HG)
                link(v.reciprocal(rsum[:, j % 2], o[:, :, :, HD]))
                if b >= 2 and g == 0:
                    dve.wait_ge(a["otr"], b - 1)
                v.tensor_tensor(on[:, b % 2, :, HG * HD * g:HG * HD * (g + 1)]
                                .rearrange("p t (h d) -> p t h d", h=HG), o[:, :, :, 0:HD],
                                rsum[:, j % 2].unsqueeze(3).to_broadcast([P, 2, HG, HD]),
                                ALU.mult).then_inc(a["on"], 1)

            def attention_residual(L, b):
                dve.wait_ge(y_ready, 4 * 3 * L + b + 1)
                if L == 0:
                    dve.wait_ge(xb_ready, b + 1)
                add_residual(3 * L, b, bank(7).rearrange("p (t d) -> p t d", t=2), xb if L == 0 else x)

            def attn_back(L):
                a = A[L]
                for step in range(STEPS):
                    for g in range(NG):
                        n = (step - LAG) * NG + g
                        if step < B:
                            row_maxima(L, step, g, step * NG + g)
                            if g == NG - 1:
                                k = step % 2
                                if step >= 2:
                                    dve.wait_ge(a["mtr"], step - 1)
                                dve.wait_ge(a["mx"], 2 * NG * (step + 1))
                                link(v.tensor_copy(mst[:, k, :, 0, :], mx[:, k]))
                                link(v.tensor_tensor(mxr[:, k], mx[:, k], mst[:, k, :, 0, :], ALU.subtract))
                                link(v.tensor_copy(mst[:, k, :, 1, :], mxr[:, k]))
                                v.tensor_tensor(mst[:, k, :, 2, :], mxr[:, k], mst[:, k, :, 1, :], ALU.subtract)\
                                    .then_inc(a["mst"], 1)
                        evac_groups(dve, v.tensor_copy, *beside(L, step, g), "dve")
                        if g == 2 and step > LAG:
                            attention_residual(L, step - LAG - 1)
                        if n >= 1:
                            divide_outputs(L, n - 1)
                        if L == 0 and step in (1, 2) and g == 2:
                            ternary(step - 1)
                        if g == 2 and step == LAG + 2:
                            norm_pair(3 * L, 0)
                divide_outputs(L, B * NG - 1)
                attention_residual(L, B - 1)
                norm_pair(3 * L, 2)

            evac_groups(dve, v.tensor_copy, 0, NG0, "dve")
            dve.wait_ge(ones_set, 2)
            attn_front(0)
            attn_back(0)
            if STAGES > 1:
                for b in range(B):
                    dve.wait_ge(Xs["en"], b + 1)
                    v.tensor_reduce(xmx[:, b % 2, :], bank(6 + b % 2).rearrange("p (t s) -> p t s", t=2), X, ALU.max,
                                    negate=True).then_inc(Xs["mx"], 1)
                    dve.wait_ge(Xs["exp"], b + 1)
                    link(v.reciprocal(xsm[:, b % 2, :], xsm[:, b % 2, :]))
                    for k in range(2):
                        ins = v.tensor_scalar(xP[:, b % 2, k, :], xP[:, b % 2, k, :], xsm[:, b % 2, k:k + 1], None, ALU.mult)
                    ins.then_inc(Xs["norm"], 1)

                def smooth_scales(n, ready_x):
                    link(v.tensor_scalar(amx[:, :, 0:n], amx[:, :, 0:n], Q_EPS, None, ALU.max))
                    link(v.reciprocal(qs[:, 0, 0:n], amx[:, 1, 0:n]))
                    link(v.tensor_tensor(qs[:, 0, 0:n], amx[:, 0, 0:n], qs[:, 0, 0:n], ALU.mult))
                    rsqrt(qs[:, 1, 0:n], qs[:, 0, 0:n], qs[:, 2, 0:n])
                    link(v.tensor_tensor(qs[:, 1, 0:n], qs[:, 1, 0:n], qs[:, 0, 0:n], ALU.mult))
                    link(v.tensor_scalar(qs[:, 1, 0:n], qs[:, 1, 0:n], Q_EPS, None, ALU.max))
                    link(v.reciprocal(qs[:, 0, 0:n], qs[:, 1, 0:n]))

                def row_scales(b, nat):
                    link(v.tensor_reduce(rsc[:, b, :], nat, X, ALU.max, apply_absolute_value=True))
                    link(v.tensor_scalar(rsc[:, b, :], rsc[:, b, :], Q_EPS, 1.0 / 127.0, ALU.max, ALU.mult))
                    link(v.reciprocal(rrq[:, b, :], rsc[:, b, :]))

                copied_out(dve, NGM)
                dve.wait_ge(Xs["tr"], B)
                v.tensor_reduce(amx[:, 1, :], fT[:, :, :, :].rearrange("p b c s -> p (b c) s"), X, ALU.max,
                                apply_absolute_value=True)
                for b in range(B):
                    dve.wait_ge(xT_ready, 4 + b + 1)
                    ins = v.tensor_reduce(amx[:, 0, b * DC:(b + 1) * DC], xT[:, :, b * S:(b + 1) * S], X, ALU.max,
                                          apply_absolute_value=True)
                link(ins)
                smooth_scales(B * DC, None)
                for b in range(B):
                    for c in range(DC):
                        j = b * DC + c
                        v.tensor_scalar(xw[:, b, 0, c, :], xT[:, c, b * S:(b + 1) * S], qs[:, 0, j:j + 1], None, ALU.mult)
                        ins = v.tensor_scalar(xw[:, b, 1, c, :], fT[:, b, c, :], qs[:, 1, j:j + 1], None, ALU.mult)
                    ins.then_inc(Q["xw"], 1)
                for b in range(B):
                    dve.wait_ge(Q["nat"], b + 1)
                    k = 2 * (b % 2)
                    nat = PS[:, k:k + 2, :].rearrange("p a (t d) -> p (a t) d", t=2)
                    row_scales(b, nat)
                    if b >= 2:
                        dve.wait_ge(Q["q16"], b - 1)
                    for i in range(4):
                        ins = v.tensor_scalar(q32[:, b % 2, i, :], nat[:, i, :], rrq[:, b, i:i + 1], MAGIC, ALU.mult, ALU.add)
                    ins.then_inc(Q["q32"], 1)
                for b in range(B):
                    dve.wait_ge(Q["h"], b + 1)
                    dve.wait_ge(Q["wbc"], b + 1)
                    if b >= 2:
                        dve.wait_ge(Q["aa"], b - 1)
                    for i in range(2):
                        ins = v.scalar_tensor_tensor(hh[:, b % 2, i, :], bank(6 + b % 2, D, i * D), rsc[:, b, i:i + 1],
                                                     wbc[:, b % 2, :], ALU.mult, ALU.mult)
                    ins.then_inc(Q["hh"], 1)
                v.tensor_reduce(amx[:, 1, 0:B], ctxT[:, :, :], X, ALU.max, apply_absolute_value=True)
                dve.wait_ge(Q["aT"], B)
                link(v.tensor_reduce(amx[:, 0, 0:B], aT, X, ALU.max, apply_absolute_value=True))
                smooth_scales(B, None)
                for b in range(B):
                    v.tensor_scalar(xw2[:, b, 0, :], aT[:, b, :], qs[:, 0, b:b + 1], None, ALU.mult)
                    v.tensor_scalar(xw2[:, b, 1, :], ctxT[:, b, :], qs[:, 1, b:b + 1], None, ALU.mult).then_inc(Q["xw2"], 1)
                for b in range(B):
                    dve.wait_ge(Q["nat2"], b + 1)
                    nat = bank(b % 2).rearrange("p (t d) -> p t d", t=4)
                    row_scales(b, nat)
                    if b >= 2:
                        dve.wait_ge(Q["q16b"], b - 1)
                    for i in range(4):
                        ins = v.tensor_scalar(q32[:, b % 2, i, 0:CX], nat[:, i, :], rrq[:, b, i:i + 1], MAGIC, ALU.mult, ALU.add)
                    ins.then_inc(Q["q32b"], 1)
                for b in range(B):
                    dve.wait_ge(y_ready, 4 * 1 + b + 1)
                    dve.wait_ge(Q["wbc2"], b + 1)
                    for i in range(2):
                        ins = v.scalar_tensor_tensor(y2[:, b % 2, i, :], bank(6 + b % 2, D, i * D), rsc[:, b, i:i + 1],
                                                     wbc[:, b % 2, :], ALU.mult, ALU.mult)
                    ins.then_inc(y_done, 1)
                    dve.wait_ge(y_done, b + 1)
                    add_residual(1, b, y2[:, b % 2], x)
                    if b % 2:
                        norm_pair(1, b - 1)
            if STAGES > 2:
                for b in range(B):
                    bs = slice(b * S, (b + 1) * S)
                    dve.wait_ge(Fs["hi"], b + 1)
                    link(v.tensor_tensor(xrem[:, b % 2], xT[:, :, bs], x3[:, 0, :, bs], ALU.subtract))
                    link(v.tensor_copy(x3[:, 1, :, bs], xrem[:, b % 2]))
                    v.tensor_tensor(x3[:, 2, :, bs], xrem[:, b % 2], x3[:, 1, :, bs], ALU.subtract).then_inc(Fs["lo"], 1)
                for b in range(B):
                    dve.wait_ge(y_ready, 4 * 2 + b + 1)
                    dve.wait_ge(xb_ready, B + b + 1)
                    add_residual(2, b, bank(2 + b % 2).rearrange("p (t d) -> p t d", t=2), xb)
                    if b % 2:
                        norm_pair(2, b - 1)
            if STAGES > 3:
                attn_front(1)
                attn_back(1)
            if STAGES > 4:
                evac_groups(dve, v.tensor_copy, NG2, len(G), "dve")
                for b in range(B):
                    dve.wait_ge(y_ready, 4 * 4 + b + 1)
                    add_residual(4, b, bank(b % 2).rearrange("p (t d) -> p t d", t=2), x)
                    if b % 2:
                        norm_pair(4, b - 1)
            if STAGES > 5:
                def bc(a):
                    return a.unsqueeze(2).to_broadcast([P, TT, E])

                ordb = order[:, :].unsqueeze(1).to_broadcast([P, TT, E])
                dve.wait_ge(Ms["logit"], 1)
                lg = bank(4, TT * E).rearrange("p (t e) -> p t e", e=E)
                link(v.tensor_reduce(g1[:, 0, :], lg, X, ALU.max))
                v.tensor_tensor(gl[:, :, :], lg, bc(g1[:, 0, :]), ALU.subtract).then_inc(Ms["lg"], 1)
                dve.wait_ge(Ms["exp"], 1)
                link(v.tensor_reduce(g1[:, 1, :], gp[:, :, :], X, ALU.add))
                link(v.reciprocal(g1[:, 1, :], g1[:, 1, :]))
                link(v.tensor_tensor(gp[:, :, :], gp[:, :, :], bc(g1[:, 1, :]), ALU.mult))
                cur = gp
                for j in range(2):
                    link(v.tensor_reduce(g1[:, 2 + j, :], cur[:, :, :], X, ALU.max))
                    link(v.tensor_tensor(gr[:, :, :], cur[:, :, :], bc(g1[:, 2 + j, :]), ALU.is_equal))
                    link(v.tensor_tensor(gr[:, :, :], gr[:, :, :], ordb, ALU.mult))
                    link(v.tensor_reduce(g1[:, 4, :], gr[:, :, :], X, ALU.max))
                    link(v.tensor_tensor(oh[:, j], gr[:, :, :], bc(g1[:, 4, :]), ALU.is_equal))
                    if j == 0:
                        link(v.scalar_tensor_tensor(gq[:, :, :].rearrange("p a b -> p (a b)"),
                                                    oh[:, 0].rearrange("p a b -> p (a b)"), -2.0,
                                                    gp[:, :, :].rearrange("p a b -> p (a b)"), ALU.mult, ALU.add))
                        cur = gq
                link(v.tensor_tensor(oh[:, 0], oh[:, 0], oh[:, 1], ALU.add))
                link(v.tensor_tensor(g1[:, 5, :], g1[:, 2, :], g1[:, 3, :], ALU.add))
                link(v.reciprocal(g1[:, 5, :], g1[:, 5, :]))
                link(v.tensor_tensor(oh[:, 0], oh[:, 0], gp[:, :, :], ALU.mult))
                link(v.tensor_tensor(gq[:, :, :], oh[:, 0], bc(g1[:, 5, :]), ALU.mult))
                v.tensor_copy(combw.rearrange("p t e i -> p (t e) i"),
                              gq[:, :, :].rearrange("p t e -> p (t e)").unsqueeze(2).to_broadcast([P, TT * E, IB]))\
                    .then_inc(Ms["comb"], 1)
                for k in range(2):
                    dve.wait_ge(Ms["ctr"], k + 1)
                    v.tensor_copy(GB[:, k * 512:(k + 1) * 512], bank(4 + k)).then_inc(Ms["GB"], 1)
                dve.wait_ge(Ms["GB"], 2)
                for n in range(2 * EC):
                    blk = n // EC
                    dve.wait_ge(Ms["gu"], n + 1)
                    if n >= 2:
                        dve.wait_ge(Ms["am"], n - 1)
                    v.tensor_tensor(um[:, n % 2, :], bank(2 * (n % 2) + 1), GB[:, blk * 512:(blk + 1) * 512],
                                    ALU.mult).then_inc(Ms["um"], 1)
                    if n % EC == EC - 1:
                        for b in (2 * blk, 2 * blk + 1):
                            dve.wait_ge(am_read, n + 1)
                            add_residual(5, b, PS[:, 4 + 2 * (b % 2):6 + 2 * (b % 2), 0:D], x)
                        norm_pair(5, 2 * blk)


        @block.tensor
        def _(pe):
            mm = nc.tensor.matmul

            def transpose_x(stage, free):
                for b in range(B):
                    if stage == 0:
                        pe.wait_ge(x_rest_loaded if b else x_loaded, 16)
                    else:
                        pe.wait_ge(x_normed, 4 * (stage - 1) + b + 1)
                    if b == 0 and stage == 2:
                        pe.wait_ge(out_read, 4 * stage - 1)
                    if b == 1 and stage > 0:
                        pe.wait_ge(out_read, 4 * stage)
                    if b >= 2:
                        pe.wait_ge(xT_ready, 4 * stage + b - 1)
                    for c in range(DC):
                        for k in range(2):
                            last = nc.tensor.transpose(bank(6 + b % 2, P, c * S + k * P),
                                                       x[:, 2 * b + k, c * P:(c + 1) * P], ident[:, :])
                    last.then_inc(xtr_done, 1)

            def project(L):
                a = A[L]
                if L == 1:
                    pe.wait_ge(xT_ready, 4 * 3 + B)
                    for n in range(2):
                        for c in range(DC):
                            last = mm(bank(4 + n, 512, 0, LAT), wdT[:, c, :], xT[:, c, n * 512:(n + 1) * 512],
                                      start=(c == 0), stop=(c == DC - 1))
                        last.then_inc(a["lat"], 1)
                    pe.wait_ge(a["lat_ready"], 2)
                for b in range(B):
                    for k in range(2):
                        tt = 2 * b + k
                        ts = slice(tt * P, (tt + 1) * P)
                        if L == 0:
                            pe.wait_ge(xT_ready, b + 1)
                            if tt >= 2:
                                pe.wait_ge(a["proj_read"], tt - 1)
                            for c in range(DC):
                                last = mm(bank(k, 384), xT[:, c, ts], wqkvT[:, c, :], start=(c == 0), stop=(c == DC - 1))
                        else:
                            if tt >= 2:
                                pe.wait_ge(a["v_ready"], tt - 1)
                            for c in range(DC):
                                mm(bank(2 * k, D), xT[:, c, ts], wqT1[:, c, :], start=(c == 0), stop=(c == DC - 1))
                            mm(bank(2 * k, D, D), latT[:, ts], wupT[:, 0:D], start=True, stop=True)
                            last = mm(bank(2 * k + 1, D), latT[:, ts], wupT[:, D:2 * D], start=True, stop=True)
                        last.then_inc(a["proj"], 1)
                    if b >= 1:
                        stack_transposes(L, b - 1)
                    if L == 0 and b == 2:
                        pe.wait_ge(ones_set, 1)
                        for k in range(2):
                            pe.wait_ge(abs_sum, k + 1)
                            mm(bank(2 + k, 1), ones[:, :], tsum[:, k:k + 1], start=True, stop=True).then_inc(abs_tot, 1)
                stack_transposes(L, B - 1)

            def stack_transposes(L, b):
                a = A[L]
                pe.wait_ge(a["lo"], b + 1 if L == 0 else 2 * b + 2)
                for g, (srcs, dst) in enumerate(tr_groups(L, b)):
                    n = b * TG[L] + g
                    if n == 0:
                        pe.wait_ge(xT_ready, 12 * L + B)
                    if n >= 4:
                        who, count = stack_evac(L, n - 4)
                        pe.wait_ge(a["ev_" + who], count)
                    for i, s_ in enumerate(srcs):
                        last = nc.tensor.transpose(bank16(4 + n % 4, P, i * P, STK), s_, ident16[:, :])
                    last.then_inc(a["stk_tr"], 1)

            def attn_back(L):
                a = A[L]
                mk = masks[:, L, :]
                nkv = KVH[L]
                K_ = Kh0 if L == 0 else Kh
                causal = L == 0
                last_n = B * TG[L] - 1
                for n in range(last_n - 3, last_n + 1):
                    who, count = stack_evac(L, n)
                    pe.wait_ge(a["ev_" + who], count)
                pe.wait_ge(krow_set, L + 1)

                def kv(h):
                    return h * nkv // H

                def mask(out_, cols, n_heads, start):
                    mm(out_, ident16[:, :], mk[:, cols].unsqueeze(1).to_broadcast([P, n_heads, cols.stop - cols.start]),
                       start=start, stop=not start)

                def two_heads(bk):
                    return bank(bk).rearrange("p (h s) -> p h s", h=2)

                def max_scores(b, g, m):
                    set_ = score_set(m)
                    if m >= 2 * NG:
                        pe.wait_ge(a["mx"], 2 * m - 1)
                    elif m >= 2:
                        pe.wait_ge(a["mx"], 2 * (m - 1))
                    mask(bank(set_), slice(0, P), HG, True)
                    for i in range(HG):
                        h = HG * g + i
                        last = mm(bank(set_, P, i * P), Qh[0:STK, b, h, 0:P], K_[0:STK, b, kv(h), 0:P],
                                  start=False, stop=(i == HG - 1))
                    last.then_inc(a["smax"], 1)
                    if m >= 2 * NG:
                        pe.wait_ge(a["mx"], 2 * m)
                    for j in range(2):
                        bk = set_ + 1 + j
                        if not causal:
                            mask(bank(bk), slice(P, 3 * P), 2, True)
                        for i in range(2):
                            h = HG * g + 2 * j + i
                            last = mm(bank(bk, S, i * S), Qh[0:STK, b, h, P:S], K_[0:STK, b, kv(h), :],
                                      start=(causal and i == 0), stop=(not causal and i == 1))
                        if causal:
                            last = mm(two_heads(bk)[:, :, P:S], ident16[:, :],
                                      mk[:, 2 * P:3 * P].unsqueeze(1).to_broadcast([P, 2, P]), start=False, stop=True)
                    last.then_inc(a["smax"], 1)

                def exp_scores(b, g, n):
                    R = STK + 3
                    if n >= 1:
                        pe.wait_ge(a["pT"], n)
                    else:
                        pe.wait_ge(a["mx"], 4 * NG)
                    for j in range(2):
                        bk = 3 + j
                        if not causal:
                            mask(bank(bk), slice(3 * P, 5 * P), 2, True)
                        for i in range(2):
                            h = HG * g + 2 * j + i
                            mm(bank(bk, S, i * S), K_[0:R, b, kv(h), 0:P], Qh[0:R, b, h, :],
                               start=(causal and i == 0), stop=(not causal and i == 1))
                        if causal:
                            mm(two_heads(bk)[:, :, 0:P], ident16[:, :],
                               mk[:, 3 * P:4 * P].unsqueeze(1).to_broadcast([P, 2, P]), start=False, stop=True)
                    mask(bank(5), slice(5 * P, 6 * P), HG, True)
                    for i in range(HG):
                        h = HG * g + i
                        last = mm(bank(5, P, i * P), K_[0:R, b, kv(h), P:S], Qh[0:R, b, h, P:S],
                                  start=False, stop=(i == HG - 1))
                    last.then_inc(a["sT"], 1)

                def values(j):
                    b, g = j // NG, j % NG
                    pe.wait_ge(a["pT"], j + 1)
                    if j >= 1:
                        pe.wait_ge(a["on"], j)
                    p0 = PT[:, j % 2, 0:1024].rearrange("p (h s) -> p h s", h=HG)
                    p1 = PT[:, j % 2, 1024:1536].rearrange("p (h s) -> p h s", h=HG)
                    for i in range(HG):
                        mm(PS[VW * i:VW * (i + 1), 6, 0:S], V1[:, 2 * b, kv(HG * g + i), :], p0[:, i, :],
                           start=True, stop=False)
                    for i in range(HG):
                        last = mm(PS[VW * i:VW * (i + 1), 6, P:S], V1[:, 2 * b + 1, kv(HG * g + i), :], p1[:, i, :],
                                  start=False, stop=True)
                    last.then_inc(a["av"], 1)

                def output_rows(j):
                    pe.wait_ge(a["os"], j + 1)
                    for k in range(2):
                        last = nc.tensor.transpose(bank(6, P, S + k * P), OS[:, j % 2, k * P:(k + 1) * P], ident[:, :])
                    last.then_inc(a["ot2"], 1)

                def transpose_maxima(b):
                    pe.wait_ge(a["mst"], b + 1)
                    if b >= LAG + 1:
                        pe.wait_ge(out_read, 12 * L + b - LAG)
                    elif b >= 1:
                        pe.wait_ge(a["mT"], b)
                    for k in range(2):
                        last = nc.tensor.transpose(bank16(7, P, k * P, 3 * H),
                                                   mst[:, b % 2, k].rearrange("p a b -> p (a b)"), ident16[:, :])
                    last.then_inc(a["mtr"], 1)

                def transpose_outputs(b):
                    pe.wait_ge(a["on"], NG * (b + 1))
                    if b + LAG + 1 <= B:
                        pe.wait_ge(a["mT"], b + LAG + 1)
                    elif b >= 1:
                        pe.wait_ge(out_read, 12 * L + b)
                    for c in range(DC):
                        for k in range(2):
                            last = nc.tensor.transpose(bank(7, P, c * S + k * P), on[:, b % 2, k, c * P:(c + 1) * P], ident[:, :])
                    last.then_inc(a["otr"], 1)

                def project_outputs(b):
                    pe.wait_ge(a["OT"], b + 1)
                    for k in range(2):
                        for c in range(DC):
                            last = mm(bank(7, D, k * D), OT[:, b % 2, c, k * P:(k + 1) * P], woT[L][:, c, :],
                                      start=(c == 0), stop=(c == DC - 1))
                    last.then_inc(y_ready, 1)

                for step in range(STEPS):
                    for g in range(NG):
                        n = (step - LAG) * NG + g
                        if n >= 0:
                            if g == 0:
                                pe.wait_ge(a["mrow"], 48 * (step - LAG + 1))
                            exp_scores(step - LAG, g, n)
                        if n >= 1:
                            values(n - 1)
                        if step < B:
                            max_scores(step, g, step * NG + g)
                        lo, hi = beside(L, step, g)
                        if hi > lo and step == B and g == 0:
                            pe.wait_ge(a["mx"], 2 * B * NG)
                        pe_groups(pe, lo, hi)
                        if g == 0 and 1 <= step <= B:
                            transpose_maxima(step - 1)
                        if g == 1 and step > LAG:
                            transpose_outputs(step - LAG - 1)
                        if g == 2 and step > LAG:
                            project_outputs(step - LAG - 1)
                        if n >= 1:
                            output_rows(n - 1)
                values(B * NG - 1)
                output_rows(B * NG - 1)
                transpose_outputs(B - 1)
                project_outputs(B - 1)

            pe.wait_ge(w_loaded["ident"], LOADS["ident"])
            pe_groups(pe, 0, NG0)
            transpose_x(0, None)
            copied_out(pe, NG0)
            pe.wait_ge(w_loaded["const"], LOADS["const"])
            project(0)
            attn_back(0)
            if STAGES > 1:
                copied_out(pe, NGM)
                for n in range(2):
                    for k in range(2):
                        if n >= 1:
                            pe.wait_ge(Xs["qk"], 2 * n + k - 1)
                        mm(bank(4 + k), xwT[:, k, :], ctxT[:, 2 * n:2 * n + 2, :].rearrange("p a b -> p (a b)"),
                           start=True, stop=True).then_inc(Xs["proj"], 1)
                pe.wait_ge(Xs["qk"], 4)
                pe.wait_ge(out_read, 4)
                for b in range(B):
                    if b >= 2:
                        pe.wait_ge(Xs["exp"], b - 1)
                    for k in range(2):
                        last = mm(bank(6 + b % 2, S, k * S), xqk[:, 0, b * S + k * P:b * S + (k + 1) * P],
                                  xqk[:, 1, b * S:(b + 1) * S], start=True, stop=True)
                    last.then_inc(Xs["en"], 1)
                    pe.wait_ge(Xs["norm"], b + 1)
                    if b >= 2:
                        pe.wait_ge(Xs["attT"], b - 1)
                    for j in range(2):
                        for k in range(2):
                            last = nc.tensor.transpose(bank(4 + b % 2, P, j * S + k * P),
                                                       xP[:, b % 2, k, j * P:(j + 1) * P], ident[:, :])
                    last.then_inc(Xs["tr"], 1)
                transpose_x(1, None)
                for b in range(B):
                    pe.wait_ge(Q["xw"], b + 1)
                    if b >= 2:
                        pe.wait_ge(Q["q32"], b - 1)
                    for w_ in range(2):
                        for k in range(2):
                            for c in range(DC):
                                last = nc.tensor.transpose(bank(2 * (b % 2) + w_, P, k * D + c * P),
                                                           xw[:, b, w_, c, k * P:(k + 1) * P], ident[:, :])
                    last.then_inc(Q["nat"], 1)
                    if b >= 1:
                        quant_transposes(pe, b - 1)
                quant_transposes(pe, B - 1)
                for b in range(B):
                    pe.wait_ge(Q["qT"], b + 1)
                    if b >= 2:
                        pe.wait_ge(Q["hh"], b - 1)
                    elif b == 0:
                        pe.wait_ge(xT_ready, 8)
                    if b == 0:
                        pe.wait_ge(Q["q32"], B)
                    for k in range(2):
                        for c in range(DC):
                            last = mm(bank(6 + b % 2, D, k * D), qT[:, b, 0, c, k * P:(k + 1) * P], qT[:, b, 1, c, :],
                                      start=(c == 0), stop=(c == DC - 1))
                    last.then_inc(Q["h"], 1)
                    if b >= 2:
                        pe.wait_ge(Q["wbc"], b - 1)
                    for k in range(2):
                        last = nc.tensor.transpose(bank(b % 2, P, k * P), rsc[:, b, 2 + k:3 + k].to_broadcast([P, P]), ident[:, :])
                    last.then_inc(Q["wtr"], 1)
                for b in range(B):
                    pe.wait_ge(Q["aa"], b + 1)
                    if b >= 2:
                        pe.wait_ge(Q["aT"], b - 1)
                    for k in range(2):
                        last = nc.tensor.transpose(bank(2 + b % 2, P, k * P), aa[:, b, k, :], ident[:, :])
                    last.then_inc(Q["atr"], 1)
                for b in range(B):
                    pe.wait_ge(Q["xw2"], b + 1)
                    if b >= 2:
                        pe.wait_ge(Q["q32b"], b - 1)
                    for w_ in range(2):
                        for k in range(2):
                            last = nc.tensor.transpose(bank(b % 2, P, (2 * w_ + k) * P), xw2[:, b, w_, k * P:(k + 1) * P], ident[:, :])
                    last.then_inc(Q["nat2"], 1)
                    if b >= 1:
                        quant_transposes2(pe, b - 1)
                quant_transposes2(pe, B - 1)
                for b in range(B):
                    pe.wait_ge(Q["qT2"], b + 1)
                    if b >= 2:
                        pe.wait_ge(y_done, b - 1)
                    elif b == 0:
                        pe.wait_ge(Q["q32b"], B)
                    for k in range(2):
                        last = mm(bank(6 + b % 2, D, k * D), qT[:, b, 0, 0, k * P:(k + 1) * P], qT[:, b, 1, 0, :],
                                  start=True, stop=True)
                    last.then_inc(y_ready, 1)
                    if b >= 2:
                        pe.wait_ge(Q["wbc2"], b - 1)
                    for k in range(2):
                        last = nc.tensor.transpose(bank(b % 2, P, k * P), rsc[:, b, 2 + k:3 + k].to_broadcast([P, P]), ident[:, :])
                    last.then_inc(Q["wtr2"], 1)
            if STAGES > 2:
                transpose_x(2, None)
                for blk in range(2):
                    for f in range(FCH):
                        n = blk * FCH + f
                        if f == 0:
                            pe.wait_ge(Fs["lo"], 2 * blk + 2)
                        if n >= 2:
                            pe.wait_ge(Fs["gelu"], n - 1)
                        for i in range(3):
                            for c in range(DC):
                                last = mm(bank(n % 2), w1T[:, c, f * P:(f + 1) * P], x3[:, i, c, blk * 512:(blk + 1) * 512],
                                          start=(i == 0 and c == 0), stop=(i == 2 and c == DC - 1))
                        last.then_inc(Fs["up"], 1)
                for b in range(B):
                    pe.wait_ge(Fs["gelu"], FCH * (b // 2 + 1))
                    if b >= 2:
                        pe.wait_ge(out_read, 8 + b - 1)
                    for k in range(2):
                        for f in range(FCH):
                            last = mm(bank(2 + b % 2, D, k * D), hT[:, f, (2 * b + k) * P:(2 * b + k + 1) * P], w2T[:, f, :],
                                      start=(f == 0), stop=(f == FCH - 1))
                    last.then_inc(y_ready, 1)
            if STAGES > 3:
                transpose_x(3, None)
                project(1)
                attn_back(1)
            if STAGES > 4:
                pe_groups(pe, NG2, len(G))
                transpose_x(4, None)
                copied_out(pe, len(G))
                for b in range(B):
                    pe.wait_ge(Xs["attT"], b + 1)
                    pe.wait_ge(xT_ready, 16 + b + 1)
                    if b >= 2:
                        pe.wait_ge(out_read, 16 + b - 1)
                    for k in range(2):
                        for c in range(DC):
                            last = mm(bank(b % 2, S, k * S), xT[:, c, b * S + k * P:b * S + (k + 1) * P], attT[:, b, c, :],
                                      start=(c == 0), stop=(c == DC - 1))
                    last.then_inc(y_ready, 1)
            if STAGES > 5:
                transpose_x(5, None)
                pe.wait_ge(xT_ready, 24)
                for tt in range(TT):
                    for c in range(DC):
                        last = mm(bank(4, E, tt * E), xT[:, c, tt * P:(tt + 1) * P], gwT[:, c, :],
                                  start=(c == 0), stop=(c == DC - 1))
                last.then_inc(Ms["logit"], 1)

                def up(n):
                    blk, c_ = n // EC, n % EC
                    if n == 0:
                        pe.wait_ge(out_read, 20)
                    if n >= 2:
                        pe.wait_ge(Ms["sg"], n - 1)
                        pe.wait_ge(Ms["um"], n - 1)
                    for gu in range(2):
                        for c in range(DC):
                            last = mm(bank(2 * (n % 2) + gu), mw1T[c][:, gu, c_ * P:(c_ + 1) * P],
                                      xT[:, c, blk * 512:(blk + 1) * 512], start=(c == 0), stop=(c == DC - 1))
                    last.then_inc(Ms["gu"], 1)

                def down(n):
                    blk, c_ = n // EC, n % EC
                    pe.wait_ge(Ms["am"], n + 1)
                    if c_ == 0 and blk == 0:
                        pe.wait_ge(Ms["GB"], 2)
                    if c_ == 0 and blk == 1:
                        pe.wait_ge(out_read, 22)
                    for k in range(4):
                        last = mm(bank(4 + k, D), am[:, n % 2, k * P:(k + 1) * P], mw2T[:, c_, :],
                                  start=(c_ == 0), stop=(c_ == EC - 1))
                    last.then_inc(am_read, 1)

                up(0)
                pe.wait_ge(Ms["comb"], 1)
                for k in range(2):
                    for i in range(4):
                        last = nc.tensor.transpose(bank(4 + k, P, i * P),
                                                   combw[:, 4 * k + i].rearrange("p e i -> p (e i)"), ident[:, :])
                    last.then_inc(Ms["ctr"], 1)
                for n in range(1, 2 * EC):
                    up(n)
                    down(n - 1)
                down(2 * EC - 1)


def shape_constants():
    import numpy as np

    def bf16_bits(a):
        return (np.ascontiguousarray(a, np.float32).view(np.uint32) >> 16).astype(np.uint16)

    s, hd = 256, 16
    i = np.arange(s)[:, None]
    j = np.arange(s)[None, :]
    causal = j <= i
    window = (causal & (j >= i - 63)) | ((j < 4) & causal)
    m = np.zeros((128, 2, 768), np.float32)
    for n, ok in enumerate((causal, window)):
        f = np.where(ok, 0.0, -1e30).astype(np.float32)
        m[:, n, 0:128] = f[0:128, 0:128]
        m[:, n, 128:384] = f[128:256, :]
        m[:, n, 384:640] = f[:, 0:128].T
        m[:, n, 640:768] = f[128:256, 128:256].T
    inv = 1.0 / 10000.0 ** (np.arange(0, hd, 2, dtype=np.float32) / hd)
    fr = np.outer(np.arange(s, dtype=np.float32), inv.astype(np.float32)).astype(np.float32)
    c, sn = np.cos(fr).astype(np.float32), np.sin(fr).astype(np.float32)
    r = np.stack([np.concatenate([c, c], 1), np.concatenate([sn, -sn], 1)], 1)
    r = np.ascontiguousarray(r.reshape(2, 128, 2, hd).transpose(1, 0, 2, 3))
    return {
        "ident": np.eye(128, dtype=np.float32),
        "ident16": bf16_bits(np.eye(128)),
        "masks": bf16_bits(m),
        "rope": r,
        "order": np.tile(np.arange(8, 0, -1, dtype=np.float32), (128, 1)),
    }


def kernel(**inputs):
    import numpy as np
    import concourse.bacc as bacc
    from concourse import mybir as mb
    from concourse.bass_utils import run_bass_kernel_spmd

    nc = bacc.Bacc("TRN2", target_bir_lowering=False, num_devices=1)
    arrays, args = {}, {}
    named = {k: np.asarray(v) for k, v in inputs.items()}
    named["b1_cols"] = np.ascontiguousarray(named.pop("L0_ffn_b1").reshape(8, 128).T)
    named.update(shape_constants())
    for name, a in named.items():
        a = np.ascontiguousarray(a)
        arrays[f"in_{name}"] = a
        args[name] = nc.dram_tensor(f"in_{name}", a.shape, mb.dt.from_np(a.dtype), kind="ExternalInput").ap()
    out = nc.dram_tensor("out_0", (4, 256, 256), mb.dt.float32, kind="ExternalOutput").ap()
    post_ln_decoder_two_layers(nc, args, out)
    r = run_bass_kernel_spmd(nc, [arrays], core_ids=[0])
    return r.results[0]["out_0"]
```

```python
import concourse.bass as bass
from concourse import mybir
from contextlib import ExitStack


def post_ln_decoder_two_layers(nc: bass.Bass, t: dict, out: bass.AP):
    F32 = mybir.dt.float32
    BF16 = mybir.dt.bfloat16
    F32R = mybir.dt.float32r
    I32 = mybir.dt.int32
    ALU = mybir.AluOpType
    ACT = mybir.ActivationFunctionType
    X = mybir.AxisListType.X

    P = 128
    B, S, D = t["x"].shape
    TT = B * S // P
    DC = D // P
    H, HD = 16, 16
    KV0 = t["L0_attn_Wk"].shape[0] // HD
    KVH = [KV0, H]
    HG = 4
    NG = H // HG
    PIECES = 6
    STK = PIECES * HD
    MROW = STK
    VW = 2 * HD
    FF = t["L0_ffn_w1"].shape[0]
    FCH = FF // P
    LAT = t["L1_attn_Wkv_down"].shape[0]
    CX = t["ctx_1024"].shape[2]
    E = t["L1_ffn_gate_w"].shape[0]
    EI = t["L1_ffn_w2"].shape[2]
    IB = P // E
    EC = EI // IB
    NEG_SCALE = float(HD) ** -0.5
    LN_EPS = 1e-5
    RMS_EPS = 1.1920929e-07
    Q_EPS = 1e-6
    MAGIC = 12582912.0
    RSQRT_SEED = 0x5F3759DF

    with ExitStack() as ctx:
        def sb(name, shape, dt=F32):
            return ctx.enter_context(nc.sbuf_tensor(name, shape, dt))

        def sem(name):
            return ctx.enter_context(nc.semaphore(name))

        PS = ctx.enter_context(nc.psum_tensor("PS", [P, 8, 512], F32))

        def bank(i, cols=512, off=0, rows=P):
            return PS[0:rows, i, off:off + cols]

        def bank16(i, cols=1024, off=0, rows=P):
            return PS[0:rows, i, :].bitcast(BF16)[:, off:off + cols]

        x = sb("x", [P, TT, D])
        xb = sb("xb", [P, TT, D])
        xT = sb("xT", [P, DC, B * S])
        ident = sb("ident", [P, P])
        ident16 = sb("ident16", [P, P], BF16)
        ones = sb("ones", [P, P])
        unround = sb("unround", [P, 1])
        stat = sb("stat", [P, 4, 6])
        mv = sb("mv", [P, 4, 2])
        va = sb("va", [P, 4])
        rstd = sb("rstd", [P, 4])
        nt = sb("nt", [P, 4])
        res = sb("res", [P, 2, 2, D])

        wqkvT = sb("wqkvT", [P, DC, D + 2 * KV0 * HD])
        woT = [sb("woT0", [P, DC, D]), sb("woT1", [P, DC, D])]
        bqkv = sb("bqkv", [P, D + 2 * KV0 * HD])
        bo = sb("bo", [P, D])
        gain = sb("gain", [P, H])
        rope = sb("rope", [P, 2, 2, HD])
        masks = sb("masks", [P, 2, 6 * P], BF16)
        wqT1 = sb("wqT1", [P, DC, D])
        wdT = sb("wdT", [P, DC, LAT])
        wupT = sb("wupT", [LAT, 2 * D])
        b1 = sb("b1", [P, FCH])
        b2 = sb("b2", [P, D])
        xwT = sb("xwT", [P, 2, CX])
        xbias = sb("xbias", [P, 2])
        ctxT = sb("ctxT", [P, B, S])
        attT = sb("attT", [P, B, 2, S])
        gwT = sb("gwT", [P, DC, E])
        order = sb("order", [P, E])

        V1 = sb("V1", [P, TT, H, VW])
        PT = sb("PT", [P, 2, 3 * 512])
        on = sb("on", [P, 2, 2, D])
        OT = sb("OT", [P, 2, DC, S])
        qss = sb("qss", [P, 4 * (H + KV0)])
        qrs = sb("qrs", [P, 4 * (H + KV0)])
        qnt = sb("qnt", [P, 4 * (H + KV0)])
        mx = sb("mx", [P, 2, 2, H])
        mxr = sb("mxr", [P, 2, 2, H])
        mst = sb("mst", [P, 2, 2, 3, H], BF16)
        mT = sb("mT", [3 * H, 2, S], BF16)
        rsum = sb("rsum", [P, 2, 2, HG])
        OS = sb("OS", [P, 2, S])
        xmx = sb("xmx", [P, B, 2])
        xsm = sb("xsm", [P, B, 2])
        tsum = sb("tsum", [P, 2])
        tthr = sb("tthr", [P, 2, 2])
        amx = sb("amx", [P, 2, B * DC])
        qs = sb("qs", [P, 4, B * DC])
        rsc = sb("rsc", [P, B, 4])
        rrq = sb("rrq", [P, B, 4])
        gl = sb("gl", [P, TT, E])
        gp = sb("gp", [P, TT, E])
        gq = sb("gq", [P, TT, E])
        gr = sb("gr", [P, TT, E])
        oh = sb("oh", [P, 2, TT, E])
        g1 = sb("g1", [P, 6, TT])

        ARENA = 25600
        with nc.sbuf_tensor("arena", [P, ARENA], F32) as arena:
            pass
        arena_r = ctx.enter_context(nc.sbuf_tensor("arena_r", [P, ARENA], F32R))

        def carve(off, shape, dt=F32):
            n = 1
            for k in shape[1:]:
                n *= k
            words = n if dt == F32 else n // 2
            assert off + words <= ARENA, (off, shape)
            v = arena[0:shape[0], off:off + words]
            if dt != F32:
                v = v.bitcast(dt)
            names = "abcdef"[:len(shape) - 1]
            if len(shape) > 2:
                v = v.rearrange(f"p ({' '.join(names)}) -> p {' '.join(names)}",
                                **{names[i]: shape[i + 1] for i in range(len(shape) - 1)})
            return v

        def carve_parts(off, shape):
            n = 1
            for k in shape[1:]:
                n *= k
            assert off + n <= ARENA, (off, shape)
            names = "abcdef"[:len(shape) - 1]
            return arena_r[0:shape[0], off:off + n].rearrange(
                f"p ({' '.join(names)}) -> p {' '.join(names)}", **{names[i]: shape[i + 1] for i in range(len(shape) - 1)})

        def words_of(a, off, shape):
            n = 1
            for k in shape[1:]:
                n *= k
            names = "abcdef"[:len(shape) - 1]
            return a[:, off:off + n].rearrange(
                f"p ({' '.join(names)}) -> p {' '.join(names)}", **{names[i]: shape[i + 1] for i in range(len(shape) - 1)})

        V1_words = V1[:, :, :, :].rearrange("p a b c -> p (a b c)")
        PT_words = PT[:, :, :].rearrange("p a b -> p (a b)")
        xb_words = xb[:, :, :].rearrange("p a b -> p (a b)")

        Qh = carve(0, [P, B, H, S], BF16)
        Kh = carve(8192, [P, B, H, S], BF16)
        qst = carve(16384, [P, 2, 2 * H * STK], BF16)
        kst = carve(19456, [P, 2, 2 * H * STK], BF16)
        Kh0 = carve(8192, [P, B, KV0, S], BF16)
        kst0 = carve(19456, [P, 2, 2 * KV0 * STK], BF16)
        res4 = [words_of(xb_words, 0, [P, 2, 2, D]), words_of(V1_words, 3072, [P, 2, 2, D])]
        rem = carve(22528, [P, 2, 2 * 2 * H * HD])
        att_words = attT[:, :, :, :].rearrange("p a b c -> p (a b c)")
        qk = att_words[:, 0:1280].rearrange("p (a b c) -> p a b c", a=2, b=2)
        HEADS0 = H + KV0
        qsq = PT[:, 0, 0:4 * HEADS0 * HD].rearrange("p (a t n) -> p a t n", a=2, t=2)
        qro = PT[:, 1, 0:4 * HEADS0 * HD].rearrange("p (a t n) -> p a t n", a=2, t=2)
        latT = xb[0:LAT, 0:4, :].rearrange("p a b -> p (a b)")

        f_nat = carve(10240, [P, B, 2, D])
        c_nat = carve(12288, [P, B, 2, CX])
        w1n = carve(13312, [P, FCH, D])
        w1t = carve(15360, [P, FCH, D], BF16)
        w2n = carve(20224, [P, DC, FF])
        w2t = carve(13312, [P, DC, FF], BF16)
        tmpw = carve(24576, [P, 2048], BF16)
        absw = carve(1024, [P, 2048], BF16)
        wq1n = carve(16384, [P, DC, D])
        wo1n = carve(16896, [P, DC, D])
        wdn = carve(17408, [LAT, D])
        wkun = carve(17664, [P, 2, DC, LAT])
        xwn = carve(17920, [P, 2, CX])
        gwn = carve(18176, [E, D])
        m1n = carve(16384, [P, 2, EC, D])
        m2n = carve(22016, [P, DC, E * EI])
        mw1H = [carve_parts(0, [P, 2, EC * P]), carve_parts(2816, [P, 2, EC * P])]
        mw1L = [carve_parts(8192, [P, 2, EC * P]), carve_parts(11008, [P, 2, EC * P])]
        mw2H = carve_parts(16384, [P, EC, D])
        mw2L = carve_parts(19200, [P, EC, D])
        mw2f = words_of(PT_words, 0, [P, EC, D])
        fT = carve(19456, [P, B, DC, S])
        xqk = carve(0, [P, 2, B * S])
        xP = words_of(xb_words, 0, [P, B, 2, S])
        wq0n = carve(0, [P, DC + 1, D])
        wo0n = carve(24576, [P, DC, D])

        xw = carve(0, [P, B, 2, DC, S])
        q32 = carve(8192, [P, 2, 4, D])
        q16 = carve(10240, [P, 2, 4, D], BF16)
        qT = carve(11264, [P, B, 2, DC, S], BF16)
        wbc = carve(15360, [P, 2, D])
        hh = carve(15872, [P, 2, 2, D])
        sg = carve(16896, [P, 2, 2, D // 2])
        aa = carve(17408, [P, B, 2, D // 2])
        aT = carve(18432, [P, B, S])
        xw2 = carve(0, [P, B, 2, S])
        y2 = words_of(PT_words, 0, [P, 2, 2, D])

        w1T = carve_parts(21504, [P, DC, FF])
        w2T = carve_parts(23552, [P, FCH, D])
        h32 = carve(4096, [P, 2, 512])
        hP = carve_parts(5120, [P, 3, 2, 512])
        xH = {2: carve_parts(0, [P, DC, B * S]), 5: carve_parts(5632, [P, DC, B * S])}
        xL = {2: carve_parts(2048, [P, DC, B * S]), 5: carve_parts(13824, [P, DC, B * S])}

        GB = xb_words[:, 0:B * S]
        combw = words_of(xb_words, 1024, [P, TT, E, IB])
        sgm = words_of(V1_words, 0, [P, 2, 512])
        um = words_of(V1_words, 1024, [P, 2, 512])
        am = words_of(V1_words, 2048, [P, 2, 512])
        amP = carve_parts(22016, [P, 3, 2, 512])

        x_loaded = sem("x_batch0_loaded")
        x_rest_loaded = sem("x_rest_loaded")
        w_loaded = {k: sem(f"{k}_loaded") for k in
                    ("ident", "const", "tables", "l0", "wo0", "f", "c", "w1", "w2", "l1", "xw", "gate", "m1", "m2")}
        qkv_bias_loaded = sem("qkv_bias_loaded")
        bias_loaded = sem("bias_loaded")
        ones_set = sem("ones_set")
        krow_set = sem("krow_set")
        wt_done = sem("wt_transposed")
        wt_act = sem("wt_evacuated_by_act")
        wt_dve = sem("wt_evacuated_by_dve")
        v_step = sem("v_step")
        a_step = sem("a_step")
        p_step = sem("p_step")
        xtr_done = sem("x_transposed")
        xT_ready = sem("xT_ready")
        x_normed = sem("x_normed")
        out_read = sem("out_read")
        context_ready = sem("context_ready")
        context_read = sem("context_read")
        y_done = sem("y_done")
        xb_ready = sem("xb_ready")
        stored = sem("stored")
        abs_sum = sem("abs_sum")
        abs_tot = sem("abs_tot")
        thr_ready = sem("thr_ready")
        low_ready = sem("low_ready")
        tern_ready = sem("tern_ready")
        A = [{k: sem(f"l{L}_{k}") for k in
              ("proj", "proj_read", "lat", "lat_ready", "v_ready", "hi", "rem", "mid", "lo", "squared", "stk_tr",
               "sq", "ev_act", "ev_dve", "smax", "mx", "mst", "mtr", "mT", "mrow", "sT", "pT", "av", "os", "ot2", "on",
               "otr", "OT")} for L in range(2)]
        Q = {k: sem(f"q_{k}") for k in
             ("xw", "nat", "q32", "q16", "qtr", "qT", "h", "wtr", "wbc", "hh", "sg", "aa", "atr", "aT",
              "xw2", "nat2", "q32b", "q16b", "qtr2", "qT2", "wtr2", "wbc2")}
        Fs = {k: sem(f"f_{k}") for k in ("up", "gelu", "parts", "down")}
        Xs = {k: sem(f"x_{k}") for k in ("proj", "qk", "en", "mx", "exp", "norm", "tr", "attT")}
        Ms = {k: sem(f"m_{k}") for k in ("logit", "lg", "exp", "comb", "ctr", "GB", "gu", "sg", "um", "am", "high", "parts")}
        x_low = sem("x_low_part")
        x_low0 = sem("x_low_part_of_pair0")
        mw2_low = sem("mw2_low_part")

        G = []

        def group(srcs, dst, rows, cols, half, need):
            G.append((srcs, dst, rows, cols, half, need))

        for dc in range(DC):
            group([wq0n[:, r, dc * P:(dc + 1) * P] for r in range(3)], wqkvT[:, dc, :], P, 384, False, "l0")
        group([wo0n[:, r, dc * P:(dc + 1) * P] for dc in range(DC) for r in range(2)],
              woT[0][:, :, :].rearrange("p a b -> p (a b)"), P, 512, False, "wo0")
        NG0 = len(G)
        for b in range(0, B, 2):
            group([c_nat[:, b + k, r, :] for k in range(2) for r in range(2)],
                  ctxT[:, b:b + 2, :].rearrange("p a b -> p (a b)"), P, 512, False, "c")
        group([xwn[:, k, :] for k in range(2)], xwT[:, :, :].rearrange("p a b -> p (a b)"), P, 256, False, "xw")
        group([wq1n[:, r, dc * P:(dc + 1) * P] for dc in range(DC) for r in range(2)],
              wqT1[:, :, :].rearrange("p a b -> p (a b)"), P, 512, False, "l1")
        group([wo1n[:, r, dc * P:(dc + 1) * P] for dc in range(DC) for r in range(2)],
              woT[1][:, :, :].rearrange("p a b -> p (a b)"), P, 512, False, "l1")
        group([wdn[:, dc * P:(dc + 1) * P] for dc in range(DC)],
              wdT[:, :, :].rearrange("p a b -> p (a b)"), P, DC * LAT, False, "l1")
        group([wkun[:, k, r, :] for k in range(2) for r in range(2)], wupT[:, :], LAT, 512, False, "l1")
        group([gwn[:, dc * P:(dc + 1) * P] for dc in range(DC)],
              gwT[:, :, :].rearrange("p a b -> p (a b)"), P, DC * E, False, "gate")
        for dc in range(DC):
            group([w1t[:, f, dc * P:(dc + 1) * P] for f in range(FCH)], w1T[:, dc, :], P, 1024, True, "t1")
        for k in range(2):
            group([w2t[:, r, f * P:(f + 1) * P] for f in range(4 * k, 4 * k + 4) for r in range(2)],
                  w2T[:, 4 * k:4 * k + 4, :].rearrange("p a b -> p (a b)"), P, 1024, True, "t2")
        for b in range(B):
            group([f_nat[:, b, r, dc * P:(dc + 1) * P] for dc in range(DC) for r in range(2)],
                  fT[:, b, :, :].rearrange("p a b -> p (a b)"), P, 512, False, "f")
        NGM = len(G)
        for dc in range(DC):
            for gu in range(2):
                for c0 in range(0, EC, 4):
                    n = min(4, EC - c0)
                    group([m1n[:, gu, c, dc * P:(dc + 1) * P] for c in range(c0, c0 + n)],
                          [m[dc][:, gu, c0 * P:(c0 + n) * P] for m in (mw1H, mw1L)], P, n * P, False, "m1")
        NG2 = len(G)
        for c0 in range(0, EC, 2):
            n = min(2, EC - c0)
            group([m2n[:, r, c::EC] for c in range(c0, c0 + n) for r in range(2)],
                  [m[:, c0:c0 + n, :].rearrange("p a b -> p (a b)") for m in (mw2H, mw2L, mw2f)], P, n * 256, False, "m2")

        LOADS = {"l0": 16 * 3, "wo0": 16, "f": 16, "c": 16, "w1": 16, "w2": 16, "l1": 16 * 5, "xw": 32, "gate": 16,
                 "m1": 16 * 16, "m2": 32, "const": 16 * 2, "tables": 16 * 2, "ident": 16}

        BESIDE = range(NG0, NG2)
        PLAN = []
        for k in range(len(G)):
            bank_ = k % 2 if k in BESIDE else 2 + k % 2 if k >= NG2 else k % 4
            eng_ = "act" if k >= NG2 else "dve" if k in BESIDE or k % 2 else "act"
            before = [j for j in range(k) if PLAN[j][0] == bank_]
            PLAN.append((bank_, eng_, 1 + sum(p[1] == eng_ for p in PLAN), before[-1] if before else None))

        def copied_out(eng, upto):
            for name, s_ in (("act", wt_act), ("dve", wt_dve)):
                n = sum(p[1] == name for p in PLAN[:upto])
                if n:
                    eng.wait_ge(s_, n)

        def pe_groups(pe, lo, hi):
            for k in range(lo, hi):
                srcs, dst, rows, cols, half, need = G[k]
                if need in ("t1", "t2"):
                    pe.wait_ge(tern_ready, int(need[1]))
                else:
                    pe.wait_ge(w_loaded[need], LOADS[need])
                bk, _, _, prev = PLAN[k]
                if prev is not None:
                    pe.wait_ge(wt_act if PLAN[prev][1] == "act" else wt_dve, PLAN[prev][2])
                w = cols // len(srcs)
                for i, s in enumerate(srcs):
                    K = s.shape[0]
                    o = (bank16 if half else bank)(bk, w, i * w, rows)
                    last = nc.tensor.transpose(o, s, (ident16 if half else ident)[0:K, 0:K])
                last.then_inc(wt_done, 1)

        def evac_groups(eng, copy, lo, hi, name):
            for k in range(lo, hi):
                srcs, dst, rows, cols, half, need = G[k]
                if PLAN[k][1] == name:
                    eng.wait_ge(wt_done, k + 1)
                    src = (bank16 if half else bank)(PLAN[k][0], cols, 0, rows)
                    if need == "m2":
                        copy(dst[0], src)
                        dst = dst[2]
                    copy(dst, src).then_inc(wt_act if name == "act" else wt_dve, 1)

        LAG = 2
        STEPS = B + LAG

        NORM_ORDER = [(st, b) for st in range(3) for b in range(B)] + \
            [(3, 0), (3, 1), (4, 0), (4, 1), (3, 2), (3, 3), (4, 2), (4, 3)] + [(5, b) for b in range(B)]
        XT_ORDER = [(st, b) for st in range(4) for b in range(B)] + \
            [(4, 0), (4, 1), (5, 0), (5, 1), (4, 2), (4, 3), (5, 2), (5, 3)]

        def normed(stage, b):
            return NORM_ORDER.index((stage, b)) + 1

        def turned(stage, b):
            return XT_ORDER.index((stage, b)) + 1

        AT_LOGITS, AT_COMBINE = 6, 10
        AT_XT = 5

        def xT_bank(stage, b):
            if stage == 1 and b == 1:
                return 3
            return b if stage == 4 and b < 2 else 6 + b % 2

        def latent_bank(n):
            return 5 if n else 3

        def score_set(m):
            return 3 * (1 - m % 2) if m < LAG * NG else 0

        def output_bank(j):
            return 2 if j % 2 == 0 and j >= LAG * NG else 6

        def beside(L, step, g):
            lo, hi = (NG0, NGM) if L == 0 else (NGM, NG2)
            slot = (step - B) * NG + g
            if slot < 0:
                return 0, 0
            return lo + (hi - lo) * slot // (LAG * NG), lo + (hi - lo) * (slot + 1) // (LAG * NG)

        def early_loads(sp):
            w = w_loaded
            sp.dma_start(w1n, t["L0_ffn_w1"].rearrange("(r p) d -> p r d", p=P)).then_inc(w["w1"], 16)
            sp.dma_start(w2n, t["L0_ffn_w2"].rearrange("(r p) d -> p r d", p=P)).then_inc(w["w2"], 16)
            sp.dma_start(c_nat.rearrange("p b r d -> p (b r) d"),
                         t["ctx_1024"].rearrange("b (r p) d -> p (b r) d", p=P)).then_inc(w["c"], 16)
            sp.dma_start(f_nat.rearrange("p b r d -> p (b r) d"),
                         t["fside_BxS2xS2_0"].rearrange("b (r p) d -> p (b r) d", p=P)).then_inc(w["f"], 16)

        def late_loads(sp):
            w = w_loaded
            sp.wait_ge(A[0]["stk_tr"], B * TG[0])
            sp.dma_start(xwn[:, 0, :], t["L1_xattn_Wq"]).then_inc(w["xw"], 16)
            sp.dma_start(xwn[:, 1, :], t["L1_xattn_Wk"]).then_inc(w["xw"], 16)
            sp.dma_start(wq1n, t["L1_attn_Wq"].rearrange("(r p) d -> p r d", p=P)).then_inc(w["l1"], 16)
            sp.dma_start(wo1n, t["L1_attn_Wo"].rearrange("(r p) d -> p r d", p=P)).then_inc(w["l1"], 16)
            sp.dma_start(wdn, t["L1_attn_Wkv_down"]).then_inc(w["l1"], 16)
            sp.dma_start(wkun[:, 0, :, :], t["L1_attn_Wk_up"].rearrange("(r p) d -> p r d", p=P)).then_inc(w["l1"], 16)
            sp.dma_start(wkun[:, 1, :, :], t["L1_attn_Wv_up"].rearrange("(r p) d -> p r d", p=P)).then_inc(w["l1"], 16)
            sp.dma_start(gwn, t["L1_ffn_gate_w"]).then_inc(w["gate"], 16)

        def expert_loads(sp):
            w = w_loaded
            sp.wait_ge(A[1]["stk_tr"], B * TG[1])
            sp.wait_ge(A[1]["lo"], TT)
            for e in range(E):
                for gu in range(2):
                    src = t["L1_ffn_w1"][e, gu * EI:(gu + 1) * EI, :].rearrange("(i c) d -> i c d", c=EC)
                    sp.dma_start(m1n[e * IB:(e + 1) * IB, gu, :, :], src).then_inc(w["m1"], 16)
            for r in range(2):
                sp.dma_start(m2n[:, r, :].rearrange("p (e i) -> p e i", e=E), t["L1_ffn_w2"][:, r * P:(r + 1) * P, :].rearrange("e h i -> h e i")).then_inc(w["m2"], 16)

        def mrow_dmas(sp, L):
            for b in range(B):
                sp.wait_ge(A[L]["mT"], b + 1)
                for k in range(3):
                    sp.dma_start(Qh[MROW + k:MROW + k + 1, b, :, :],
                                 mT[k * H:(k + 1) * H, b % 2, :]).then_inc(A[L]["mrow"], 16)

        am_read = sem("am_read")
        last_outputs = sem("last_outputs")

        Q_SLOTS = {"hi": (0, 3, 1), "mid": (3, 5, 1), "lo": (5, 6, 1)}
        K_SLOTS = {"hi": (1, 6, 2), "mid": (2, 5, 2), "lo": (0, 1, 1)}

        def stack_buffer(L, slot, which):
            buf = qst if which == "q" else (kst0 if L == 0 else kst)
            return buf[:, slot % 2, :]

        def stack(L, u, which, part):
            nh = H if which == "q" else KVH[L]
            if L == 0:
                rows = stack_buffer(0, u, which)[:, 0:2 * nh * STK]
                nh = 2 * nh
            else:
                rows = stack_buffer(1, u // 2, which)[:, (u % 2) * nh * STK:(u % 2 + 1) * nh * STK]
            buf = rows.rearrange("p (h s d) -> p h s d", h=nh, s=PIECES)
            lo, hi, st = (Q_SLOTS if which == "q" else K_SLOTS)[part]
            return buf[:, :, lo:hi:st, :]

        def part_source(L, u, which):
            if L == 0:
                a = qro[:, u % 2, :, 0:D] if which == "q" else qro[:, u % 2, :, D:D + KV0 * HD]
                return a.rearrange("p t (h d) -> p t h d", d=HD)
            o = 0 if which == "q" else D
            return bank(2 * (u % 2), D, o).rearrange("p (h d) -> p h d", d=HD)

        def remainder(L, u, which):
            nh = (2 * H if which == "q" else 2 * KVH[0]) if L == 0 else H
            o = 0 if which == "q" else 2 * H * HD
            return rem[:, u % 2, o:o + nh * HD].rearrange("p (h d) -> p h d", d=HD)

        def stack_views(L, u, part):
            res_ = []
            for which in "qk":
                dst = stack(L, u, which, part)
                src = remainder(L, u, which)
                n = dst.shape[2]
                res_.append((src.unsqueeze(2).to_broadcast([P, dst.shape[1], n, HD]), dst))
            return res_

        def tr_groups(L, b):
            gs = []
            for which, nh, dst in (("k", KVH[L], Kh0 if L == 0 else Kh), ("q", H, Qh)):
                buf = stack_buffer(L, b, which)[:, 0:2 * nh * STK].rearrange("p (t h s) -> p t h s", t=2, h=nh)
                for g in range(nh // HG):
                    srcs = [buf[:, half, h, :] for h in range(HG * g, HG * g + HG) for half in range(2)]
                    gs.append((srcs, dst[0:STK, b, HG * g:HG * g + HG, :].rearrange("p a b -> p (a b)")))
            return gs

        TG = [KVH[L] // HG + NG for L in range(2)]

        def stack_evac(L, n):
            if L == 0:
                who = ["dve" if k >= 2 * TG[0] and k % 2 else "act" for k in range(n + 1)]
            else:
                who = ["dve" if k % 4 else "act" for k in range(n + 1)]
            return who[-1], who.count(who[-1])

        bias_b1 = sem("b1_loaded")
        y_ready = sem("y_ready")

        def quant_transposes(pe, b):
            pe.wait_ge(Q["q16"], b + 1)
            if b >= 2:
                pe.wait_ge(Q["qT"], b - 1)
            for i in range(4):
                for c in range(DC):
                    last = nc.tensor.transpose(bank16(4 + b % 2, P, ((i // 2) * DC + c) * S + (i % 2) * P),
                                               q16[:, b % 2, i, c * P:(c + 1) * P], ident16[:, :])
            last.then_inc(Q["qtr"], 1)

        def quant_transposes2(pe, b):
            if b == 0:
                pe.wait_ge(Xs["attT"], B)
            pe.wait_ge(Q["q16b"], b + 1)
            if b >= 2:
                pe.wait_ge(Q["qT2"], b - 1)
            for i in range(4):
                last = nc.tensor.transpose(bank16(4 + b % 2, P, i * P), q16[:, b % 2, i, 0:CX], ident16[:, :])
            last.then_inc(Q["qtr2"], 1)

        block = ctx.enter_context(nc.Block())

        @block.sync
        def _(sp):
            w = w_loaded
            xv = t["x"].rearrange("b (h p) d -> p (b h) d", p=P)
            sp.dma_start(ident[:, :], t["ident"]).then_inc(w["ident"], 16)
            sp.dma_start(x[:, 0:2, :], xv[:, 0:2, :]).then_inc(x_loaded, 16)
            sp.dma_start(wq0n[:, 0:2, :], t["L0_attn_Wq"].rearrange("(r p) d -> p r d", p=P)).then_inc(w["l0"], 16)
            sp.dma_start(wq0n[0:64, 2, :], t["L0_attn_Wk"]).then_inc(w["l0"], 16)
            sp.dma_start(wq0n[64:128, 2, :], t["L0_attn_Wv"]).then_inc(w["l0"], 16)
            sp.dma_start(x[:, 2:TT, :], xv[:, 2:TT, :]).then_inc(x_rest_loaded, 16)
            sp.dma_start(wo0n[:, :, :], t["L0_attn_Wo"].rearrange("(r p) d -> p r d", p=P)).then_inc(w["wo0"], 16)
            sp.dma_start(masks[:, :, :], t["masks"].bitcast(BF16)).then_inc(w["tables"], 16)
            sp.dma_start(order[:, :], t["order"]).then_inc(w["tables"], 16)
            sp.dma_start(bo[:, :], t["L0_attn_bo"].partition_broadcast(P)).then_inc(bias_loaded, 16)
            sp.dma_start(b2[:, :], t["L0_ffn_b2"].partition_broadcast(P)).then_inc(bias_loaded, 16)
            sp.dma_start(xbias[:, 0:1], t["L1_xattn_bq"].unsqueeze(1)).then_inc(bias_loaded, 16)
            sp.dma_start(xbias[:, 1:2], t["L1_xattn_bk"].unsqueeze(1)).then_inc(bias_loaded, 16)
            sp.dma_start(b1[:, :], t["b1_cols"]).then_inc(bias_b1, 16)
            early_loads(sp)
            late_loads(sp)
            mrow_dmas(sp, 0)
            expert_loads(sp)
            mrow_dmas(sp, 1)
            ov = out.rearrange("b (h p) d -> p (b h) d", p=P)
            for b in range(B):
                sp.wait_ge(x_normed, normed(5, b))
                sp.dma_start(ov[:, 2 * b:2 * b + 2, :], x[:, 2 * b:2 * b + 2, :]).then_inc(stored, 16)
            sp.wait_ge(stored, 16 * B)

        @block.gpsimd
        def _(pool):
            w = w_loaded
            count = {}

            def alone(ins, signal=p_step):
                count[signal.name] = count.get(signal.name, 0) + 1
                ins.then_inc(signal, 1)
                pool.wait_ge(signal, count[signal.name])

            alone(pool.memset(ones[:, :], 1.0), ones_set)
            alone(pool.memset(unround[:, :], -MAGIC), ones_set)
            alone(pool.memset(V1[:, :, :, HD:VW], 1.0), ones_set)
            alone(pool.memset(Kh0[MROW:MROW + 3, :, :, :].rearrange("p a b c -> p (a b c)"), -1.0), krow_set)

            def residual_bias(stage, bias):
                if stage == 2:
                    pool.wait_ge(Xs["tr"], B)
                for b in range(B):
                    if stage == 0:
                        pool.wait_ge(x_rest_loaded if b else x_loaded, 16)
                        if b == 0:
                            pool.wait_ge(bias_loaded, 16 * 4)
                    else:
                        pool.wait_ge(x_normed, 4 * stage + b - 4 + 1)
                    for k in range(2):
                        alone(pool.tensor_tensor(xb[:, 2 * b + k, :], x[:, 2 * b + k, :], bias[:, :], ALU.add),
                              xb_ready if k else p_step)

            residual_bias(0, bo)
            for k, (wn, wt) in enumerate(((w1n, w1t), (w2n, w2t))):
                pool.wait_ge(thr_ready, k + 1)
                if k == 1:
                    pool.wait_ge(tern_ready, 1)
                alone(pool.tensor_scalar(tmpw, wn.rearrange("p a b -> p (a b)"), tthr[:, k, 1:2], None, ALU.is_lt),
                      low_ready)
            for b in range(B):
                pool.wait_ge(Q["sg"], b + 1)
                alone(pool.tensor_tensor(aa[:, b], sg[:, b % 2], hh[:, b % 2, :, D // 2:D], ALU.mult), Q["aa"])
            residual_bias(2, b2)
            pool.wait_ge(x_normed, 12)
            alone(pool.memset(Kh[MROW:MROW + 3, :, :, :].rearrange("p a b c -> p (a b c)"), -1.0), krow_set)
            for b in range(2):
                bs = slice(b * S, (b + 1) * S)
                pool.wait_ge(xT_ready, turned(5, b))
                alone(pool.tensor_tensor(xL[5][:, :, bs], xT[:, :, bs], xH[5][:, :, bs].bitcast(F32), ALU.subtract),
                      x_low0)
            for k in range(NG2, len(G)):
                pool.wait_ge(wt_act, PLAN[k][2])
                high, low, full = G[k][1]
                alone(pool.tensor_tensor(low, full, high.bitcast(F32), ALU.subtract), mw2_low)

        @block.scalar
        def _(act):
            w = w_loaded
            act.dma_start(bqkv[:, 0:D], t["L0_attn_bq"].partition_broadcast(P)).then_inc(qkv_bias_loaded, 16)
            act.dma_start(bqkv[:, D:D + 64], t["L0_attn_bk"].partition_broadcast(P)).then_inc(qkv_bias_loaded, 16)
            act.dma_start(bqkv[:, D + 64:D + 128], t["L0_attn_bv"].partition_broadcast(P)).then_inc(qkv_bias_loaded, 16)
            act.dma_start(gain[:, :], t["L0_attn_q_gain"].partition_broadcast(P)).then_inc(qkv_bias_loaded, 16)
            act.dma_start(rope[:, :, :, :], t["rope"]).then_inc(w["const"], 16)
            act.dma_start(ident16[:, :], t["ident16"].bitcast(BF16)).then_inc(w["const"], 16)

            def copy(dst, src):
                return nc.scalar.activation(dst, src, ACT.Copy)

            def evac_xT(stage, lo=0, hi=B):
                for b in range(lo, hi):
                    act.wait_ge(xtr_done, turned(stage, b))
                    if stage in xH:
                        copy(xH[stage][:, :, b * S:(b + 1) * S], bank(xT_bank(stage, b)).rearrange("p (c s) -> p c s", c=DC))
                    copy(xT[:, :, b * S:(b + 1) * S], bank(xT_bank(stage, b)).rearrange("p (c s) -> p c s", c=DC))\
                        .then_inc(xT_ready, 1)

            def abs_sums():
                for k, (wn, nm) in enumerate(((w1n, "w1"), (w2n, "w2"))):
                    act.wait_ge(w[nm], 16)
                    if k == 1:
                        act.wait_ge(abs_sum, 1)
                    nc.scalar.activation(absw, wn.rearrange("p a b -> p (a b)"), ACT.Abs,
                                         accum_out=tsum[:, k:k + 1]).then_inc(abs_sum, 1)

            def attn_front(L):
                a = A[L]
                def latents(n):
                    act.wait_ge(a["lat"], n + 1)
                    copy(latT[:, n * 512:(n + 1) * 512], bank(latent_bank(n), 512, 0, LAT)).then_inc(a["lat_ready"], 1)

                if L == 1:
                    latents(0)
                def squares(b):
                    act.wait_ge(a["proj_read"], 2 * b + 2)
                    nc.scalar.activation(qsq[:, b % 2], qk[:, b % 2], ACT.Square).then_inc(a["squared"], 1)

                if L == 0:
                    squares(0)
                    squares(1)
                    abs_sums()
                    for b in (0, 2):
                        hi_part(L, b)
                        hi_part(L, b + 1)
                        mid_part(L, b)
                        mid_part(L, b + 1)
                        if b == 0:
                            squares(2)
                            squares(3)
                        evac_stacks(L, b)
                        evac_stacks(L, b + 1)
                        if b == 0:
                            evac_groups(act, copy, NG0 - 1, NG0, "act")
                    return
                for b in range(B):
                    for u in (2 * b, 2 * b + 1):
                        hi_part(L, u)
                    if b > 0:
                        evac_stacks(L, b - 1)
                    for u in (2 * b, 2 * b + 1):
                        mid_part(L, u)
                    if b == 0:
                        evac_xT(3, 2, 4)
                        latents(1)
                evac_stacks(L, B - 1)

            def evac_stacks(L, b):
                a = A[L]
                for g in range(TG[L]):
                    n = b * TG[L] + g
                    if stack_evac(L, n)[0] == "act":
                        act.wait_ge(a["stk_tr"], n + 1)
                        copy(tr_groups(L, b)[g][1], bank16(4 + n % 4, 1024, 0, STK)).then_inc(a["ev_act"], 1)

            def mid_part(L, u):
                a = A[L]
                act.wait_ge(a["rem"], u + 1)
                for src, dst in stack_views(L, u, "mid"):
                    last = copy(dst, src)
                last.then_inc(a["mid"], 1)

            def hi_part(L, u):
                a = A[L]
                act.wait_ge(a["sq"], u + 1) if L == 0 else act.wait_ge(a["proj"], u + 1)
                b = u if L == 0 else u // 2
                if b >= 2:
                    act.wait_ge(a["stk_tr"], (b - 1) * TG[L])
                for which in "qk":
                    dst = stack(L, u, which, "hi")
                    src = part_source(L, u, which)
                    if L == 0:
                        nh = H if which == "q" else KVH[0]
                        for half in range(2):
                            last = copy(dst[:, half * nh:(half + 1) * nh],
                                        src[:, half].unsqueeze(2).to_broadcast([P, nh, 3, HD]))
                    else:
                        last = copy(dst, src.unsqueeze(2).to_broadcast([P, H, 3, HD]))
                last.then_inc(a["hi"], 1)

            def copy_outputs(L, j):
                a = A[L]
                act.wait_ge(a["av"], j + 1)
                if j >= 2:
                    act.wait_ge(a["ot2"], j - 1)
                copy(OS[:, j % 2, :], bank(output_bank(j), S)).then_inc(a["os"], 1)

            def copy_OT(L, b):
                a = A[L]
                act.wait_ge(a["otr"], b + 1)
                copy(OT[:, b % 2, :, :].rearrange("p a b -> p (a b)"), bank(7)).then_inc(a["OT"], 1)

            def attn_back(L):
                a = A[L]
                for step in range(STEPS):
                    for g in range(NG):
                        n = (step - LAG) * NG + g
                        if n >= 1:
                            copy_outputs(L, n - 1)
                        if n >= 0:
                            act.wait_ge(a["sT"], n + 1)
                            if n >= 2:
                                act.wait_ge(a["av"], n - 1)
                            nc.scalar.activation(PT[:, n % 2, :], PS[:, 3:6, :].rearrange("p a b -> p (a b)"),
                                                 ACT.Exp, scale=NEG_SCALE).then_inc(a["pT"], 1)
                        if g == 0 and 1 <= step <= B:
                            act.wait_ge(a["mtr"], step)
                            if step >= 3:
                                act.wait_ge(a["mrow"], 48 * (step - 2))
                            copy(mT[:, (step - 1) % 2, :], bank16(7, S, 0, 3 * H)).then_inc(a["mT"], 1)
                        if g == 1 and step > LAG:
                            copy_OT(L, step - LAG - 1)
                if L == 1:
                    evac_xT(4, 0, 2)
                copy_outputs(L, B * NG - 1)
                copy_OT(L, B - 1)
                if L == 0:
                    evac_xT(1, 0, 2)

            evac_groups(act, copy, 0, NG0 - 1, "act")
            evac_xT(0)
            attn_front(0)
            attn_back(0)
            for n in range(2):
                for k in range(2):
                    act.wait_ge(bias_loaded, 16 * 4)
                    act.wait_ge(Xs["proj"], 2 * n + k + 1)
                    nc.scalar.activation(xqk[:, k, n * 512:(n + 1) * 512], bank(4 + k), ACT.Identity,
                                         bias=xbias[:, k:k + 1]).then_inc(Xs["qk"], 1)
            evac_xT(1, 2, 4)
            for b in range(B):
                act.wait_ge(Xs["mx"], b + 1)
                for k in range(2):
                    last = nc.scalar.activation(xP[:, b, k, :], bank(b, S, k * S), ACT.Exp,
                                                bias=xmx[:, b, k:k + 1], accum_out=xsm[:, b, k:k + 1])
                last.then_inc(Xs["exp"], 1)
            act.wait_ge(ones_set, 2)
            def integers(b):
                act.wait_ge(Q["q32"], b + 1)
                nc.scalar.activation(q16[:, b % 2], q32[:, b % 2], ACT.Identity, bias=unround[:, 0:1])\
                    .then_inc(Q["q16"], 1)

            def copy_qT(b):
                act.wait_ge(Q["qtr"], b + 1)
                copy(qT[:, b].rearrange("p a b c -> p (a b c)"), bank16(4 + b % 2)).then_inc(Q["qT"], 1)

            def copy_row_scales(b):
                act.wait_ge(Q["wtr"], b + 1)
                if b >= 2:
                    act.wait_ge(Q["hh"], b - 1)
                copy(wbc[:, b % 2, :], bank(b % 2, D)).then_inc(Q["wbc"], 1)

            def silu(b):
                act.wait_ge(Q["hh"], b + 1)
                if b >= 2:
                    act.wait_ge(Q["aa"], b - 1)
                nc.scalar.activation(sg[:, b % 2], hh[:, b % 2, :, 0:D // 2], ACT.Silu).then_inc(Q["sg"], 1)

            for b in range(2):
                integers(b)
                copy_qT(b)
            integers(2)
            copy_row_scales(0)
            copy_row_scales(1)
            copy_qT(2)
            integers(3)
            silu(0)
            copy_qT(3)
            copy_row_scales(2)
            silu(1)
            copy_row_scales(3)
            silu(2)
            silu(3)
            for b in range(B):
                act.wait_ge(Q["atr"], b + 1)
                copy(aT[:, b, :], bank(2 + b % 2, S)).then_inc(Q["aT"], 1)
            for b in range(B):
                act.wait_ge(Xs["tr"], b + 1)
                copy(attT[:, b, :, :].rearrange("p a b -> p (a b)"), bank(4 + b % 2)).then_inc(Xs["attT"], 1)

            def integers2(b):
                act.wait_ge(Q["q32b"], b + 1)
                nc.scalar.activation(q16[:, b % 2, :, 0:CX], q32[:, b % 2, :, 0:CX], ACT.Identity,
                                     bias=unround[:, 0:1]).then_inc(Q["q16b"], 1)

            def copy_qT2(b):
                act.wait_ge(Q["qtr2"], b + 1)
                copy(qT[:, b, :, 0, :], bank16(4 + b % 2, 512).rearrange("p (a b) -> p a b", a=2)).then_inc(Q["qT2"], 1)

            def copy_row_scales2(b):
                act.wait_ge(Q["wtr2"], b + 1)
                if b >= 2:
                    act.wait_ge(y_done, b - 1)
                copy(wbc[:, b % 2, :], bank(b % 2, D)).then_inc(Q["wbc2"], 1)

            for b in range(3):
                integers2(b)
                copy_qT2(b)
                if b == 1:
                    copy_row_scales2(0)
                    copy_row_scales2(1)
            copy_row_scales2(2)
            evac_xT(2, 0, 1)
            integers2(3)
            evac_xT(2, 1, 2)
            copy_qT2(3)
            copy_row_scales2(3)
            act.wait_ge(bias_b1, 16)
            for n in range(2 * FCH):
                if n == AT_XT + 1:
                    evac_xT(2, 2, 4)
                f = n % FCH
                act.wait_ge(Fs["up"], n + 1)
                if n >= 2:
                    act.wait_ge(Fs["parts"], n - 1)
                if n >= 3:
                    act.wait_ge(Fs["down"], n - 2)
                nc.scalar.activation(h32[:, n % 2, :], bank(n % 2), ACT.Gelu, bias=b1[:, f:f + 1])
                nc.scalar.activation(hP[:, n % 3, 0, :], bank(n % 2), ACT.Gelu,
                                     bias=b1[:, f:f + 1]).then_inc(Fs["gelu"], 1)
            evac_xT(3, 0, 2)
            attn_front(1)
            attn_back(1)
            evac_groups(act, copy, NG2, len(G), "act")
            evac_xT(5, 0, 2)

            def router_exp(pair):
                act.wait_ge(Ms["lg"], pair + 1)
                tl = slice(4 * pair, 4 * pair + 4)
                nc.scalar.activation(gp[:, tl, :], gl[:, tl, :], ACT.Exp).then_inc(Ms["exp"], 1)

            router_exp(0)

            def high_part(n):
                act.wait_ge(Ms["am"], n + 1)
                if n >= 3:
                    act.wait_ge(am_read, n - 2)
                copy(amP[:, n % 3, 0, :], am[:, n % 2, :]).then_inc(Ms["high"], 1)

            for n in range(2 * EC):
                act.wait_ge(Ms["gu"], n + 1)
                if n >= 2:
                    act.wait_ge(Ms["am"], n - 1)
                nc.scalar.activation(sgm[:, n % 2, :], bank(2 * (n % 2)), ACT.Silu).then_inc(Ms["sg"], 1)
                if n == 1:
                    evac_xT(4, 2, 4)
                    high_part(0)
                if n >= 1:
                    high_part(n)
                if n == AT_LOGITS - 1:
                    evac_xT(5, 2, 4)
                if n == AT_LOGITS + 1:
                    router_exp(1)

        @block.vector
        def _(dve):
            v = nc.vector
            steps = [0]

            def link(ins):
                steps[0] += 1
                ins.then_inc(v_step, 1)
                dve.wait_ge(v_step, steps[0])

            def rsqrt(y, a, tmp):
                link(v.tensor_scalar(y.bitcast(I32), a.bitcast(I32), 1, None, ALU.logical_shift_right))
                link(v.tensor_scalar(y.bitcast(I32), y.bitcast(I32), -1.0, float(RSQRT_SEED), ALU.mult, ALU.add))
                for _ in range(3):
                    link(v.tensor_tensor(tmp, y, y, ALU.mult))
                    link(v.scalar_tensor_tensor(tmp, tmp, -0.5, a, ALU.mult, ALU.mult))
                    link(v.scalar_tensor_tensor(y, tmp, 1.5, y, ALU.add, ALU.mult))

            def sums_of(stage, b):
                return res4[b // 2] if stage == 4 else res

            def add_residual(stage, b, y, base):
                last = {(5, 0): (3, 3)}.get((stage, b), (stage, 1) if b == 2 else (stage - 1, 3))
                if b % 2 == 0 and stage + b > 0 and stage != 4:
                    dve.wait_ge(x_normed, normed(*last))
                v.tensor_tensor(sums_of(stage, b)[:, b % 2], y, base[:, 2 * b:2 * b + 2, :], ALU.add)\
                    .then_inc(context_read if stage == 4 else out_read, 1)

            def tile_stats(stage, b):
                r = sums_of(stage, b)
                if stage == 4:
                    dve.wait_ge(context_read, b + 1)
                else:
                    dve.wait_ge(out_read, 4 * min(stage, 4) + b + 1)
                for i in range(2):
                    ins = v.bn_stats(stat[:, 2 * (b % 2) + i, :], r[:, b % 2, i, :])
                if b % 2:
                    link(ins)

            def norm_stats(stage, b):
                if (stage, b) != (5, 2):
                    tile_stats(stage, b)
                    tile_stats(stage, b + 1)
                for i in range(4):
                    ins = v.bn_aggr(mv[:, i, :], stat[:, i, :])
                link(ins)

            def norm_factor():
                link(v.tensor_scalar(va[:, :], mv[:, :, 1], LN_EPS, None, ALU.add))
                rsqrt(rstd[:, :], va[:, :], nt[:, :])

            def norm_apply(stage, b):
                r = sums_of(stage, b)
                for i in range(4):
                    ins = v.tensor_scalar(x[:, 2 * b + i, :], r[:, i // 2, i % 2, :], mv[:, i, 0:1], rstd[:, i:i + 1],
                                          ALU.subtract, ALU.mult)
                    if i % 2:
                        ins.then_inc(x_normed, 1)

            def norm_pair(stage, b):
                norm_stats(stage, b)
                norm_factor()
                norm_apply(stage, b)

            def rem_part(L, u):
                a = A[L]
                if u >= 2:
                    dve.wait_ge(a["lo"], u - 1)
                dve.wait_ge(a["hi"], u + 1)
                for which in "qk":
                    hi = stack(L, u, which, "hi")[:, :, 0, :]
                    src = part_source(L, u, which)
                    dst = remainder(L, u, which)
                    if L == 0:
                        nh = H if which == "q" else KVH[0]
                        for half in range(2):
                            ins = v.tensor_tensor(dst[:, half * nh:(half + 1) * nh], src[:, half],
                                                  hi[:, half * nh:(half + 1) * nh], ALU.subtract)
                    else:
                        ins = v.tensor_tensor(dst, src, hi, ALU.subtract)
                ins.then_inc(a["rem"], 1)

            def lo_part(L, u):
                a = A[L]
                dve.wait_ge(a["mid"], u + 1)
                for which in "qk":
                    mid = stack(L, u, which, "mid")[:, :, 0, :]
                    ins = v.tensor_tensor(stack(L, u, which, "lo")[:, :, 0, :], remainder(L, u, which), mid, ALU.subtract)
                ins.then_inc(a["lo"], 1)

            def evac_stacks(L, b):
                a = A[L]
                for g in range(TG[L]):
                    n = b * TG[L] + g
                    if stack_evac(L, n)[0] == "dve":
                        dve.wait_ge(a["stk_tr"], n + 1)
                        v.tensor_copy(tr_groups(L, b)[g][1], bank16(4 + n % 4, 1024, 0, STK)).then_inc(a["ev_dve"], 1)

            def thresholds():
                for k in range(2):
                    dve.wait_ge(abs_tot, 1)
                    link(v.tensor_scalar(tthr[:, k, 0:1], bank(0, 1, k), 1.0 / (FF * D), 1e-8, ALU.mult, ALU.max))
                    link(v.tensor_scalar(tthr[:, k, 0:1], tthr[:, k, 0:1], 0.5, None, ALU.mult))
                    v.tensor_scalar(tthr[:, k, 1:2], tthr[:, k, 0:1], -1.0, None, ALU.mult).then_inc(thr_ready, 1)

            def ternary(k):
                wn, wt = ((w1n, w1t), (w2n, w2t))[k]
                dve.wait_ge(low_ready, k + 1)
                v.scalar_tensor_tensor(wt.rearrange("p a b -> p (a b)"), wn.rearrange("p a b -> p (a b)"),
                                       tthr[:, k, 0:1], tmpw, ALU.is_gt, ALU.subtract).then_inc(tern_ready, 1)

            def read_projections(b):
                a = A[0]
                for k in range(2):
                    tt = 2 * b + k
                    bk = tt % 4
                    dve.wait_ge(a["proj"], tt + 1)
                    v.tensor_tensor(V1[:, tt, 0:KV0, 0:HD],
                                    bank(bk, 64, D + 64).rearrange("p (h d) -> p h d", d=HD),
                                    bqkv[:, D + 64:D + 128].rearrange("p (h d) -> p h d", d=HD),
                                    ALU.add).then_inc(a["v_ready"], 1)
                    v.tensor_tensor(qk[:, b % 2, k, :], bank(bk, D + 64), bqkv[:, 0:D + 64], ALU.add)\
                        .then_inc(a["proj_read"], 1)

            def normed_queries_and_keys(b0):
                a = A[0]
                dve.wait_ge(a["squared"], b0 + 2)
                q2 = qk[:, :, :, :].rearrange("p a t n -> p (a t n)")
                sq = qsq.rearrange("p a t n -> p (a t n)")
                link(v.tensor_reduce(qss[:, :], sq.rearrange("p (h d) -> p h d", d=HD), X, ALU.add))
                link(v.tensor_scalar(qss[:, :], qss[:, :], 1.0 / HD, RMS_EPS, ALU.mult, ALU.add))
                rsqrt(qrs[:, :], qss[:, :], qnt[:, :])
                rq = qrs[:, :].rearrange("p (t h) -> p t h", t=4)[:, :, 0:H]
                link(v.tensor_tensor(rq, rq, gain[:, :].unsqueeze(1).to_broadcast([P, 4, H]), ALU.mult))
                q3 = q2.rearrange("p (h d) -> p h d", d=HD)
                link(v.tensor_tensor(q3, q3, qrs[:, :].unsqueeze(2).to_broadcast([P, 4 * HEADS0, HD]), ALU.mult))

            def rotate(b):
                a = A[0]
                if b >= 2:
                    dve.wait_ge(a["lo"], b - 1)
                hf = HD // 2
                for k in range(2):
                    qi, ri, si = (z[:, b % 2, k, :].rearrange("p (h d) -> p h d", d=HD) for z in (qk, qro, qsq))
                    cos = rope[:, k, 0, :].unsqueeze(1).to_broadcast([P, HEADS0, HD])
                    s1 = rope[:, k, 1, 0:hf].unsqueeze(1).to_broadcast([P, HEADS0, hf])
                    s2 = rope[:, k, 1, hf:HD].unsqueeze(1).to_broadcast([P, HEADS0, hf])
                    v.tensor_tensor(ri, qi, cos, ALU.mult)
                    v.tensor_tensor(si[:, :, 0:hf], qi[:, :, hf:HD], s1, ALU.mult)
                    ins = v.tensor_tensor(si[:, :, hf:HD], qi[:, :, 0:hf], s2, ALU.mult)
                link(ins)
                ro, sq = (z[:, b % 2].rearrange("p t n -> p (t n)") for z in (qro, qsq))
                v.tensor_tensor(ro, ro, sq, ALU.add).then_inc(a["sq"], 1)

            def attn_front(L):
                a = A[L]
                if L == 0:
                    dve.wait_ge(qkv_bias_loaded, 16 * 4)
                    dve.wait_ge(w_loaded["const"], LOADS["const"])
                    read_projections(0)
                    read_projections(1)
                    for b in (0, 2):
                        normed_queries_and_keys(b)
                        rotate(b)
                        rotate(b + 1)
                        rem_part(0, b)
                        rem_part(0, b + 1)
                        if b == 0:
                            read_projections(2)
                            read_projections(3)
                        else:
                            thresholds()
                        lo_part(0, b)
                        lo_part(0, b + 1)
                        evac_stacks(0, b)
                        evac_stacks(0, b + 1)
                else:
                    for b in range(B):
                        for u in (2 * b, 2 * b + 1):
                            rem_part(L, u)
                            v.tensor_copy(V1[:, u, :, 0:HD],
                                          bank(2 * (u % 2) + 1, D).rearrange("p (h d) -> p h d", d=HD))\
                                .then_inc(a["v_ready"], 1)
                        if b >= 1:
                            evac_stacks(L, b - 1)
                        for u in (2 * b, 2 * b + 1):
                            lo_part(L, u)
                    evac_stacks(L, B - 1)

            def row_maxima(L, b, g, m, between):
                a = A[L]
                set_ = score_set(m)
                dve.wait_ge(a["smax"], 2 * m + 1)
                v.tensor_reduce(mx[:, b % 2, 0, HG * g:HG * g + HG],
                                bank(set_).rearrange("p (h s) -> p h s", h=HG), X, ALU.max).then_inc(a["mx"], 1)
                if between is not None:
                    divide_outputs(L, between)
                dve.wait_ge(a["smax"], 2 * m + 2)
                v.tensor_reduce(mx[:, b % 2, 1, HG * g:HG * g + HG],
                                PS[:, set_ + 1:set_ + 3, :].rearrange("p a (h s) -> p (a h) s", h=2), X, ALU.max)\
                    .then_inc(a["mx"], 1)

            def divide_outputs(L, j):
                a = A[L]
                b, g = j // NG, j % NG
                dve.wait_ge(a["ot2"], j + 1)
                o = bank(output_bank(j), S, S).rearrange("p (t h d) -> p t h d", t=2, h=HG)
                link(v.reciprocal(rsum[:, j % 2], o[:, :, :, HD]))
                if b >= 2 and g == 0:
                    dve.wait_ge(a["otr"], b - 1)
                v.tensor_tensor(on[:, b % 2, :, HG * HD * g:HG * HD * (g + 1)]
                                .rearrange("p t (h d) -> p t h d", h=HG), o[:, :, :, 0:HD],
                                rsum[:, j % 2].unsqueeze(3).to_broadcast([P, 2, HG, HD]),
                                ALU.mult).then_inc(a["on"], 1)

            def channel_maxima(b):
                dve.wait_ge(xT_ready, turned(1, b))
                ins = v.tensor_reduce(amx[:, 0, b * DC:(b + 1) * DC], xT[:, :, b * S:(b + 1) * S], X, ALU.max,
                                      apply_absolute_value=True)
                return ins

            def context_residual(b):
                dve.wait_ge(context_ready, b + 1)
                add_residual(4, b, bank(b if b < 2 else 4 + b).rearrange("p (t d) -> p t d", t=2), x)

            def attention_residual(L, b):
                dve.wait_ge(y_ready, 4 * 2 * L + b + 1)
                if L == 0:
                    dve.wait_ge(xb_ready, b + 1)
                add_residual(3 * L, b, bank(7).rearrange("p (t d) -> p t d", t=2), xb if L == 0 else x)

            def evac_parts(lo, hi):
                for k in range(lo, hi):
                    _, (high, low), rows, cols, _, _ = G[k]
                    dve.wait_ge(wt_done, k + 1)
                    src = bank(PLAN[k][0], cols, 0, rows)
                    link(v.tensor_copy(high, src))
                    v.tensor_tensor(low, src, high.bitcast(F32), ALU.subtract).then_inc(wt_dve, 1)

            def low_x(stage, lo, hi):
                for b in range(lo, hi):
                    bs = slice(b * S, (b + 1) * S)
                    dve.wait_ge(xT_ready, turned(stage, b))
                    v.tensor_tensor(xL[stage][:, :, bs], xT[:, :, bs], xH[stage][:, :, bs].bitcast(F32),
                                    ALU.subtract).then_inc(x_low, 1)

            def attn_back(L):
                a = A[L]
                for step in range(STEPS):
                    for g in range(NG):
                        n = (step - LAG) * NG + g
                        if step < B:
                            row_maxima(L, step, g, step * NG + g, n - 1 if n >= 1 else None)
                            if g == NG - 1:
                                k = step % 2
                                if step >= 2:
                                    dve.wait_ge(a["mtr"], step - 1)
                                dve.wait_ge(a["mx"], 2 * NG * (step + 1))
                                link(v.tensor_copy(mst[:, k, :, 0, :], mx[:, k]))
                                link(v.tensor_tensor(mxr[:, k], mx[:, k], mst[:, k, :, 0, :], ALU.subtract))
                                link(v.tensor_copy(mst[:, k, :, 1, :], mxr[:, k]))
                                v.tensor_tensor(mst[:, k, :, 2, :], mxr[:, k], mst[:, k, :, 1, :], ALU.subtract)\
                                    .then_inc(a["mst"], 1)
                        if L == 0:
                            evac_groups(dve, v.tensor_copy, *beside(0, step, g), "dve")
                        else:
                            evac_parts(*beside(1, step, g))
                        if g == 2 and step > LAG:
                            attention_residual(L, step - LAG - 1)
                        if n >= 1 and step >= B:
                            divide_outputs(L, n - 1)
                        if L == 0 and step == B and g in (0, 3):
                            ternary(g // 3)
                        if g == 2 and step == LAG + 2:
                            norm_stats(3 * L, 0)
                        elif g == 3 and step == LAG + 2:
                            norm_factor()
                        elif g == 0 and step == LAG + 3:
                            norm_apply(3 * L, 0)
                if L == 1:
                    context_residual(0)
                divide_outputs(L, B * NG - 1)
                if L == 1:
                    context_residual(1)
                    norm_pair(4, 0)
                if L == 0:
                    copied_out(dve, NGM)
                    v.tensor_reduce(amx[:, 1, :], fT[:, :, :, :].rearrange("p b c s -> p (b c) s"), X, ALU.max,
                                    apply_absolute_value=True)
                    channel_maxima(0)
                    channel_maxima(1)
                attention_residual(L, B - 1)
                if L == 0:
                    norm_pair(0, 2)

            evac_groups(dve, v.tensor_copy, 0, NG0 - 1, "dve")
            dve.wait_ge(ones_set, 3)
            attn_front(0)
            attn_back(0)
            for b in range(B):
                dve.wait_ge(Xs["en"], b + 1)
                v.tensor_reduce(xmx[:, b, :], bank(b).rearrange("p (t s) -> p t s", t=2), X, ALU.max,
                                negate=True).then_inc(Xs["mx"], 1)

            def smooth_scales(n):
                link(v.tensor_scalar(amx[:, :, 0:n], amx[:, :, 0:n], Q_EPS, None, ALU.max))
                link(v.reciprocal(qs[:, 0, 0:n], amx[:, 1, 0:n]))
                link(v.tensor_tensor(qs[:, 0, 0:n], amx[:, 0, 0:n], qs[:, 0, 0:n], ALU.mult))
                rsqrt(qs[:, 1, 0:n], qs[:, 0, 0:n], qs[:, 2, 0:n])
                link(v.tensor_tensor(qs[:, 1, 0:n], qs[:, 1, 0:n], qs[:, 0, 0:n], ALU.mult))
                link(v.tensor_scalar(qs[:, 1, 0:n], qs[:, 1, 0:n], Q_EPS, None, ALU.max))
                link(v.reciprocal(qs[:, 0, 0:n], qs[:, 1, 0:n]))

            def row_scales(b, nat):
                link(v.tensor_reduce(rsc[:, b, :], nat, X, ALU.max, apply_absolute_value=True))
                link(v.tensor_scalar(rsc[:, b, :], rsc[:, b, :], Q_EPS, 1.0 / 127.0, ALU.max, ALU.mult))
                link(v.reciprocal(rrq[:, b, :], rsc[:, b, :]))

            channel_maxima(2)
            link(channel_maxima(3))
            smooth_scales(B * DC)
            for b in range(B):
                for c in range(DC):
                    j = b * DC + c
                    v.tensor_scalar(xw[:, b, 0, c, :], xT[:, c, b * S:(b + 1) * S], qs[:, 0, j:j + 1], None, ALU.mult)
                    ins = v.tensor_scalar(xw[:, b, 1, c, :], fT[:, b, c, :], qs[:, 1, j:j + 1], None, ALU.mult)
                ins.then_inc(Q["xw"], 1)
            for b in range(B):
                dve.wait_ge(Q["nat"], b + 1)
                k = 2 * (b % 2)
                nat = PS[:, k:k + 2, :].rearrange("p a (t d) -> p (a t) d", t=2)
                row_scales(b, nat)
                if b >= 2:
                    dve.wait_ge(Q["q16"], b - 1)
                for i in range(4):
                    ins = v.tensor_scalar(q32[:, b % 2, i, :], nat[:, i, :], rrq[:, b, i:i + 1], MAGIC, ALU.mult, ALU.add)
                ins.then_inc(Q["q32"], 1)

            def context_rows(b):
                for k in range(2):
                    ins = v.tensor_scalar(xP[:, b, k, :], xP[:, b, k, :], xsm[:, b, k:k + 1], None, ALU.mult)
                ins.then_inc(Xs["norm"], 1)

            for b in range(B):
                dve.wait_ge(Q["h"], b + 1)
                dve.wait_ge(Q["wbc"], b + 1)
                if b >= 2:
                    dve.wait_ge(Q["aa"], b - 1)
                for i in range(2):
                    ins = v.scalar_tensor_tensor(hh[:, b % 2, i, :], bank(6 + b % 2, D, i * D), rsc[:, b, i:i + 1],
                                                 wbc[:, b % 2, :], ALU.mult, ALU.mult)
                ins.then_inc(Q["hh"], 1)
                if b == 1:
                    dve.wait_ge(Xs["exp"], B)
                    link(v.reciprocal(xsm[:, :, :], xsm[:, :, :]))
                    context_rows(0)
                    context_rows(1)
                elif b == 2:
                    context_rows(2)
            v.tensor_reduce(amx[:, 1, 0:B], ctxT[:, :, :], X, ALU.max, apply_absolute_value=True)
            context_rows(3)
            dve.wait_ge(Q["aT"], B)
            link(v.tensor_reduce(amx[:, 0, 0:B], aT, X, ALU.max, apply_absolute_value=True))
            smooth_scales(B)
            for b in range(B):
                v.tensor_scalar(xw2[:, b, 0, :], aT[:, b, :], qs[:, 0, b:b + 1], None, ALU.mult)
                v.tensor_scalar(xw2[:, b, 1, :], ctxT[:, b, :], qs[:, 1, b:b + 1], None, ALU.mult).then_inc(Q["xw2"], 1)
            def round2(b):
                dve.wait_ge(Q["nat2"], b + 1)
                nat = bank(b).rearrange("p (t d) -> p t d", t=4)
                row_scales(b, nat)
                if b >= 2:
                    dve.wait_ge(Q["q16b"], b - 1)
                for i in range(4):
                    ins = v.tensor_scalar(q32[:, b % 2, i, 0:CX], nat[:, i, :], rrq[:, b, i:i + 1], MAGIC, ALU.mult, ALU.add)
                ins.then_inc(Q["q32b"], 1)

            def quantised_residual(b):
                dve.wait_ge(y_ready, 4 * 1 + b + 1)
                dve.wait_ge(Q["wbc2"], b + 1)
                for i in range(2):
                    ins = v.scalar_tensor_tensor(y2[:, b % 2, i, :], bank(6 + b if b < 2 else b, D, i * D), rsc[:, b, i:i + 1],
                                                 wbc[:, b % 2, :], ALU.mult, ALU.mult)
                ins.then_inc(y_done, 1)
                dve.wait_ge(y_done, b + 1)
                add_residual(1, b, y2[:, b % 2], x)

            round2(0)
            round2(1)
            round2(2)
            quantised_residual(0)
            quantised_residual(1)
            norm_pair(1, 0)
            round2(3)
            quantised_residual(2)
            low_x(2, 0, 2)
            for n in range(2 * FCH + 1):
                if n < 2 * FCH:
                    dve.wait_ge(Fs["gelu"], n + 1)
                    v.tensor_tensor(hP[:, n % 3, 1, :], h32[:, n % 2, :], hP[:, n % 3, 0, :].bitcast(F32),
                                    ALU.subtract).then_inc(Fs["parts"], 1)
                if n == 0:
                    quantised_residual(3)
                elif n == 1:
                    norm_stats(1, 2)
                elif n == 2:
                    norm_factor()
                elif n == 3:
                    norm_apply(1, 2)
                elif n == AT_XT + 1:
                    low_x(2, 2, 4)
                elif n == FCH + 2:
                    norm_stats(2, 0)
                elif n == FCH + 3:
                    norm_factor()
                elif n == FCH + 4:
                    norm_apply(2, 0)
                if n in (FCH + 1, 2 * FCH):
                    b0 = 0 if n == FCH + 1 else 2
                    for b in (b0, b0 + 1):
                        dve.wait_ge(Fs["down"], FCH * (b // 2 + 1))
                        dve.wait_ge(xb_ready, B + b + 1)
                        add_residual(2, b, bank(2 + b).rearrange("p (t d) -> p t d", t=2), xb)
            norm_pair(2, 2)
            attn_front(1)
            attn_back(1)
            def router(pair, parts=(0, 1, 2)):
                tl = slice(4 * pair, 4 * pair + 4)

                def bc(a):
                    return a.unsqueeze(2).to_broadcast([P, 4, E])

                def flat(a):
                    return a.rearrange("p a b -> p (a b)")

                gl_, gp_, gq_, gr_ = (a[:, tl, :] for a in (gl, gp, gq, gr))
                top1, total, both, largest, first = (g1[:, k, tl] for k in (2, 1, 5, 0, 4))
                picked = [oh[:, j, tl, :] for j in range(2)]
                tops = [g1[:, 2 + j, tl] for j in range(2)]
                ordb = order[:, :].unsqueeze(1).to_broadcast([P, 4, E])
                if 0 in parts:
                    dve.wait_ge(Ms["logit"], pair + 1)
                    lg = bank(4 + 2 * pair, 4 * E).rearrange("p (t e) -> p t e", e=E)
                    link(v.tensor_reduce(largest, lg, X, ALU.max))
                    v.tensor_tensor(gl_, lg, bc(largest), ALU.subtract).then_inc(Ms["lg"], 1)
                    dve.wait_ge(Ms["exp"], pair + 1)
                    link(v.tensor_reduce(total, gp_, X, ALU.add))
                    link(v.reciprocal(total, total))
                    link(v.tensor_tensor(gp_, gp_, bc(total), ALU.mult))
                for j, cur in enumerate((gp_, gq_)):
                    if j in parts:
                        link(v.tensor_reduce(tops[j], cur, X, ALU.max))
                        link(v.tensor_tensor(gr_, cur, bc(tops[j]), ALU.is_equal))
                        link(v.tensor_tensor(gr_, gr_, ordb, ALU.mult))
                        link(v.tensor_reduce(first, gr_, X, ALU.max))
                        link(v.tensor_tensor(picked[j], gr_, bc(first), ALU.is_equal))
                        if j == 0:
                            link(v.scalar_tensor_tensor(flat(gq_), flat(picked[0]), -2.0, flat(gp_), ALU.mult, ALU.add))
                if 2 in parts:
                    link(v.tensor_tensor(picked[0], picked[0], picked[1], ALU.add))
                    link(v.tensor_tensor(both, tops[0], tops[1], ALU.add))
                    link(v.reciprocal(both, both))
                    link(v.tensor_tensor(picked[0], picked[0], gp_, ALU.mult))
                    link(v.tensor_tensor(gq_, picked[0], bc(both), ALU.mult))
                    v.tensor_copy(combw[:, tl].rearrange("p t e i -> p (t e) i"),
                                  flat(gq_).unsqueeze(2).to_broadcast([P, 4 * E, IB])).then_inc(Ms["comb"], 1)

            def copy_combine(pair):
                dve.wait_ge(Ms["ctr"], pair + 1)
                v.tensor_copy(GB[:, pair * 512:(pair + 1) * 512], bank(5 + 2 * pair)).then_inc(Ms["GB"], 1)

            def gated(n):
                blk = n // EC
                dve.wait_ge(Ms["gu"], n + 1)
                dve.wait_ge(Ms["GB"], blk + 1)
                if n >= 2:
                    dve.wait_ge(Ms["parts"], n - 1)
                v.tensor_tensor(um[:, n % 2, :], bank(2 * (n % 2) + 1), GB[:, blk * 512:(blk + 1) * 512],
                                ALU.mult).then_inc(Ms["um"], 1)
                dve.wait_ge(Ms["um"], n + 1)
                dve.wait_ge(Ms["sg"], n + 1)
                v.tensor_tensor(am[:, n % 2, :], sgm[:, n % 2, :], um[:, n % 2, :], ALU.mult).then_inc(Ms["am"], 1)

            def low_part(n):
                dve.wait_ge(Ms["high"], n + 1)
                v.tensor_tensor(amP[:, n % 3, 1, :], am[:, n % 2, :], amP[:, n % 3, 0, :].bitcast(F32),
                                ALU.subtract).then_inc(Ms["parts"], 1)

            def outputs(blk):
                for b in (2 * blk, 2 * blk + 1):
                    if blk == 0:
                        dve.wait_ge(am_read, EC)
                    else:
                        dve.wait_ge(last_outputs, 2 * (b - 2) + 2)
                    add_residual(5, b, bank(4 + b).rearrange("p (t d) -> p t d", t=2), x)
                    if blk == 1:
                        tile_stats(5, b)

            norm_pair(3, 2)
            router(0)
            copy_combine(0)
            for n in range(2 * EC):
                gated(n)
                if n >= 1:
                    low_part(n - 1)
                if n == 1:
                    context_residual(2)
                    context_residual(3)
                elif n == 2:
                    norm_stats(4, 2)
                elif n == 3:
                    norm_factor()
                elif n == 4:
                    norm_apply(4, 2)
                elif n == AT_LOGITS:
                    low_x(5, 2, 4)
                elif AT_LOGITS < n <= AT_LOGITS + 3:
                    router(1, (n - AT_LOGITS - 1,))
                elif n == AT_COMBINE:
                    copy_combine(1)
                elif n == EC + 1:
                    outputs(0)
                elif n == EC + 2:
                    norm_stats(5, 0)
                elif n == EC + 3:
                    norm_factor()
                elif n == EC + 4:
                    norm_apply(5, 0)
            low_part(2 * EC - 1)
            outputs(1)
            norm_pair(5, 2)


        @block.tensor
        def _(pe):
            mm = nc.tensor.matmul

            def transpose_x(stage, lo=0, hi=B):
                for b in range(lo, hi):
                    if stage == 0:
                        pe.wait_ge(x_rest_loaded if b else x_loaded, 16)
                    else:
                        pe.wait_ge(x_normed, normed(stage - 1, b))
                    if stage == 2 and b < 2:
                        pe.wait_ge(y_done, b + 1)
                    elif stage == 3 and b < 2:
                        pe.wait_ge(xT_ready, turned(2, b + 2))
                    elif stage == 4 and b < 2:
                        copied_out(pe, NG2)
                    elif stage == 4:
                        pe.wait_ge(xT_ready, turned(5, b - 2))
                    elif stage == 5 and b < 2:
                        pe.wait_ge(out_read, 16)
                    elif stage == 5:
                        pe.wait_ge(context_read, b + 1)
                    elif b >= 2:
                        pe.wait_ge(xT_ready, turned(stage, b - 2))
                    for c in range(DC):
                        for k in range(2):
                            last = nc.tensor.transpose(bank(xT_bank(stage, b), P, c * S + k * P),
                                                       x[:, 2 * b + k, c * P:(c + 1) * P], ident[:, :])
                    last.then_inc(xtr_done, 1)

            def context(b):
                pe.wait_ge(xT_ready, turned(4, b))
                if b >= 2:
                    pe.wait_ge(xT_ready, turned(4, 3))
                bk = b if b < 2 else 4 + b
                for k in range(2):
                    for c in range(DC):
                        last = mm(bank(bk, S, k * S), xT[:, c, b * S + k * P:b * S + (k + 1) * P], attT[:, b, c, :],
                                  start=(c == 0), stop=(c == DC - 1))
                last.then_inc(context_ready, 1)

            def project(L):
                a = A[L]

                def latents(n):
                    pe.wait_ge(xT_ready, turned(3, 2 * n + 1))
                    pe.wait_ge(out_read, 12 if n else 10)
                    for c in range(DC):
                        last = mm(bank(latent_bank(n), 512, 0, LAT), wdT[:, c, :], xT[:, c, n * 512:(n + 1) * 512],
                                  start=(c == 0), stop=(c == DC - 1))
                    last.then_inc(a["lat"], 1)

                if L == 1:
                    latents(0)
                def project_tile(tt):
                    b = tt // 2
                    ts = slice(tt * P, (tt + 1) * P)
                    if L == 0:
                        pe.wait_ge(xT_ready, b + 1)
                        if tt >= 4:
                            pe.wait_ge(a["proj_read"], tt - 3)
                        for c in range(DC):
                            last = mm(bank(tt % 4, 384), xT[:, c, ts], wqkvT[:, c, :], start=(c == 0), stop=(c == DC - 1))
                    else:
                        k = tt % 2
                        pe.wait_ge(a["lat_ready"], b // 2 + 1)
                        if tt >= 2:
                            pe.wait_ge(a["v_ready"], tt - 1)
                        for c in range(DC):
                            mm(bank(2 * k, D), xT[:, c, ts], wqT1[:, c, :], start=(c == 0), stop=(c == DC - 1))
                        mm(bank(2 * k, D, D), latT[:, ts], wupT[:, 0:D], start=True, stop=True)
                        last = mm(bank(2 * k + 1, D), latT[:, ts], wupT[:, D:2 * D], start=True, stop=True)
                    last.then_inc(a["proj"], 1)

                if L == 0:
                    for tt in range(TT):
                        project_tile(tt)
                    stack_transposes(0, 0)
                    stack_transposes(0, 1)
                    pe.wait_ge(a["proj_read"], 2 * B)
                    pe_groups(pe, NG0 - 1, NG0)
                    pe.wait_ge(ones_set, 1)
                    for k in range(2):
                        pe.wait_ge(abs_sum, k + 1)
                        last = mm(bank(0, 1, k), ones[:, :], tsum[:, k:k + 1], start=True, stop=True)
                    last.then_inc(abs_tot, 1)
                    stack_transposes(0, 2)
                    stack_transposes(0, 3)
                else:
                    project_tile(0)
                    project_tile(1)
                    transpose_x(3, 2, 4)
                    project_tile(2)
                    project_tile(3)
                    latents(1)
                    for b in range(B):
                        for k in range(2):
                            stack_transposes(1, b, k * TG[1] // 2, (k + 1) * TG[1] // 2)
                            if b + 2 < B:
                                project_tile(2 * (b + 2) + k)

            def stack_transposes(L, b, lo=0, hi=None):
                a = A[L]
                pe.wait_ge(a["lo"], b + 1 if L == 0 else 2 * b + 2)
                for g, (srcs, dst) in list(enumerate(tr_groups(L, b)))[lo:hi]:
                    n = b * TG[L] + g
                    if n == 0:
                        pe.wait_ge(xT_ready, 12 * L + B)
                    elif n == 1 and L == 1:
                        pe.wait_ge(a["lat_ready"], 2)
                    if n >= 4:
                        who, count = stack_evac(L, n - 4)
                        pe.wait_ge(a["ev_" + who], count)
                    for i, s_ in enumerate(srcs):
                        last = nc.tensor.transpose(bank16(4 + n % 4, P, i * P, STK), s_, ident16[:, :])
                    last.then_inc(a["stk_tr"], 1)

            def attn_back(L):
                a = A[L]
                mk = masks[:, L, :]
                nkv = KVH[L]
                K_ = Kh0 if L == 0 else Kh
                causal = L == 0
                last_n = B * TG[L] - 1
                for n in range(last_n - 3, last_n + 1):
                    who, count = stack_evac(L, n)
                    pe.wait_ge(a["ev_" + who], count)
                pe.wait_ge(krow_set, L + 1)

                def kv(h):
                    return h * nkv // H

                def mask(out_, cols, n_heads, start):
                    mm(out_, ident16[:, :], mk[:, cols].unsqueeze(1).to_broadcast([P, n_heads, cols.stop - cols.start]),
                       start=start, stop=not start)

                def two_heads(bk):
                    return bank(bk).rearrange("p (h s) -> p h s", h=2)

                def max_scores(b, g, m, between):
                    set_ = score_set(m)
                    if m >= 2 * NG:
                        pe.wait_ge(a["mx"], 2 * m - 1)
                    elif m >= 2:
                        pe.wait_ge(a["mx"], 2 * (m - 1))
                    elif m == 1 and L == 0:
                        pe.wait_ge(thr_ready, 2)
                    mask(bank(set_), slice(0, P), HG, True)
                    for i in range(HG):
                        h = HG * g + i
                        last = mm(bank(set_, P, i * P), Qh[0:STK, b, h, 0:P], K_[0:STK, b, kv(h), 0:P],
                                  start=False, stop=(i == HG - 1))
                    last.then_inc(a["smax"], 1)
                    if between is not None:
                        output_rows(between)
                    if m >= 2 * NG:
                        pe.wait_ge(a["mx"], 2 * m)
                    for j in range(2):
                        bk = set_ + 1 + j
                        if not causal:
                            mask(bank(bk), slice(P, 3 * P), 2, True)
                        for i in range(2):
                            h = HG * g + 2 * j + i
                            last = mm(bank(bk, S, i * S), Qh[0:STK, b, h, P:S], K_[0:STK, b, kv(h), :],
                                      start=(causal and i == 0), stop=(not causal and i == 1))
                        if causal:
                            last = mm(two_heads(bk)[:, :, P:S], ident16[:, :],
                                      mk[:, 2 * P:3 * P].unsqueeze(1).to_broadcast([P, 2, P]), start=False, stop=True)
                    last.then_inc(a["smax"], 1)

                def exp_scores(b, g, n):
                    R = STK + 3
                    if n >= 1:
                        pe.wait_ge(a["pT"], n)
                    else:
                        pe.wait_ge(a["mx"], 2 * (LAG * NG - 1))
                    for j in range(2):
                        bk = 3 + j
                        if not causal:
                            mask(bank(bk), slice(3 * P, 5 * P), 2, True)
                        for i in range(2):
                            h = HG * g + 2 * j + i
                            mm(bank(bk, S, i * S), K_[0:R, b, kv(h), 0:P], Qh[0:R, b, h, :],
                               start=(causal and i == 0), stop=(not causal and i == 1))
                        if causal:
                            mm(two_heads(bk)[:, :, 0:P], ident16[:, :],
                               mk[:, 3 * P:4 * P].unsqueeze(1).to_broadcast([P, 2, P]), start=False, stop=True)
                    mask(bank(5), slice(5 * P, 6 * P), HG, True)
                    for i in range(HG):
                        h = HG * g + i
                        last = mm(bank(5, P, i * P), K_[0:R, b, kv(h), P:S], Qh[0:R, b, h, P:S],
                                  start=False, stop=(i == HG - 1))
                    last.then_inc(a["sT"], 1)

                def values(j):
                    b, g = j // NG, j % NG
                    pe.wait_ge(a["pT"], j + 1)
                    if j > LAG * NG:
                        pe.wait_ge(a["on"], j - 1)
                    elif j == LAG * NG:
                        pe.wait_ge(a["mx"], 2 * B * NG)
                    elif j >= 1:
                        pe.wait_ge(a["on"], j)
                    ob = output_bank(j)
                    p0 = PT[:, j % 2, 0:1024].rearrange("p (h s) -> p h s", h=HG)
                    p1 = PT[:, j % 2, 1024:1536].rearrange("p (h s) -> p h s", h=HG)
                    for i in range(HG):
                        mm(PS[VW * i:VW * (i + 1), ob, 0:S], V1[:, 2 * b, kv(HG * g + i), :], p0[:, i, :],
                           start=True, stop=False)
                    for i in range(HG):
                        last = mm(PS[VW * i:VW * (i + 1), ob, P:S], V1[:, 2 * b + 1, kv(HG * g + i), :], p1[:, i, :],
                                  start=False, stop=True)
                    last.then_inc(a["av"], 1)

                def output_rows(j):
                    pe.wait_ge(a["os"], j + 1)
                    for k in range(2):
                        last = nc.tensor.transpose(bank(output_bank(j), P, S + k * P), OS[:, j % 2, k * P:(k + 1) * P], ident[:, :])
                    last.then_inc(a["ot2"], 1)

                def transpose_maxima(b):
                    pe.wait_ge(a["mst"], b + 1)
                    if b >= LAG + 1:
                        pe.wait_ge(out_read, 12 * L + b - LAG)
                    elif b >= 1:
                        pe.wait_ge(a["mT"], b)
                    for k in range(2):
                        last = nc.tensor.transpose(bank16(7, P, k * P, 3 * H),
                                                   mst[:, b % 2, k].rearrange("p a b -> p (a b)"), ident16[:, :])
                    last.then_inc(a["mtr"], 1)

                def transpose_outputs(b):
                    pe.wait_ge(a["on"], NG * (b + 1))
                    if b + LAG + 1 <= B:
                        pe.wait_ge(a["mT"], b + LAG + 1)
                    elif b >= 1:
                        pe.wait_ge(out_read, 12 * L + b)
                    for c in range(DC):
                        for k in range(2):
                            last = nc.tensor.transpose(bank(7, P, c * S + k * P), on[:, b % 2, k, c * P:(c + 1) * P], ident[:, :])
                    last.then_inc(a["otr"], 1)

                def project_outputs(b):
                    pe.wait_ge(a["OT"], b + 1)
                    for k in range(2):
                        for c in range(DC):
                            last = mm(bank(7, D, k * D), OT[:, b % 2, c, k * P:(k + 1) * P], woT[L][:, c, :],
                                      start=(c == 0), stop=(c == DC - 1))
                    last.then_inc(y_ready, 1)

                for step in range(STEPS):
                    for g in range(NG):
                        n = (step - LAG) * NG + g
                        if n >= 1:
                            values(n - 1)
                        if n >= 0:
                            if g == 0:
                                pe.wait_ge(a["mrow"], 48 * (step - LAG + 1))
                            exp_scores(step - LAG, g, n)
                        if step < B:
                            max_scores(step, g, step * NG + g, n - 1 if n >= 1 else None)
                        lo, hi = beside(L, step, g)
                        if hi > lo and step == B and g == 0:
                            pe.wait_ge(a["mx"], 2 * B * NG)
                        pe_groups(pe, lo, hi)
                        if g == 0 and 1 <= step <= B:
                            transpose_maxima(step - 1)
                        if g == 1 and step > LAG:
                            transpose_outputs(step - LAG - 1)
                        if g == 2 and step > LAG:
                            project_outputs(step - LAG - 1)
                        if n >= 1 and step >= B:
                            output_rows(n - 1)
                if L == 1:
                    transpose_x(4, 0, 2)
                    pe.wait_ge(Xs["attT"], B)
                values(B * NG - 1)
                if L == 1:
                    context(0)
                output_rows(B * NG - 1)
                if L == 1:
                    context(1)
                transpose_outputs(B - 1)
                if L == 0:
                    transpose_x(1, 0, 2)
                project_outputs(B - 1)

            pe.wait_ge(w_loaded["ident"], LOADS["ident"])
            pe_groups(pe, 0, NG0 - 1)
            transpose_x(0)
            copied_out(pe, NG0 - 1)
            pe.wait_ge(w_loaded["const"], LOADS["const"])
            pe.wait_ge(w_loaded["tables"], LOADS["tables"])
            project(0)
            copied_out(pe, NG0)
            attn_back(0)
            copied_out(pe, NG0 + 3)
            for n in range(2):
                for k in range(2):
                    if n >= 1:
                        pe.wait_ge(Xs["qk"], 2 * n + k - 1)
                    mm(bank(4 + k), xwT[:, k, :], ctxT[:, 2 * n:2 * n + 2, :].rearrange("p a b -> p (a b)"),
                       start=True, stop=True).then_inc(Xs["proj"], 1)
            pe.wait_ge(Xs["qk"], 4)
            copied_out(pe, NGM)
            pe.wait_ge(xT_ready, turned(1, 1))
            for b in range(B):
                for k in range(2):
                    last = mm(bank(b, S, k * S), xqk[:, 0, b * S + k * P:b * S + (k + 1) * P],
                              xqk[:, 1, b * S:(b + 1) * S], start=True, stop=True)
                last.then_inc(Xs["en"], 1)
            transpose_x(1, 2, 4)

            def scaled_to_rows(b):
                pe.wait_ge(Q["xw"], b + 1)
                if b < 2:
                    pe.wait_ge(Xs["exp"], 2 * b + 2)
                if b >= 2:
                    pe.wait_ge(Q["q32"], b - 1)
                for w_ in range(2):
                    for k in range(2):
                        for c in range(DC):
                            last = nc.tensor.transpose(bank(2 * (b % 2) + w_, P, k * D + c * P),
                                                       xw[:, b, w_, c, k * P:(k + 1) * P], ident[:, :])
                last.then_inc(Q["nat"], 1)

            def products(b):
                pe.wait_ge(Q["qT"], b + 1)
                if b >= 2:
                    pe.wait_ge(Q["hh"], b - 1)
                elif b == 0:
                    pe.wait_ge(xT_ready, 8)
                for k in range(2):
                    for c in range(DC):
                        last = mm(bank(6 + b % 2, D, k * D), qT[:, b, 0, c, k * P:(k + 1) * P], qT[:, b, 1, c, :],
                                  start=(c == 0), stop=(c == DC - 1))
                last.then_inc(Q["h"], 1)
                if b >= 2:
                    pe.wait_ge(Q["wbc"], b - 1)
                else:
                    pe.wait_ge(Q["q32"], 3)
                for k in range(2):
                    last = nc.tensor.transpose(bank(b % 2, P, k * P), rsc[:, b, 2 + k:3 + k].to_broadcast([P, P]), ident[:, :])
                last.then_inc(Q["wtr"], 1)

            scaled_to_rows(0)
            scaled_to_rows(1)
            scaled_to_rows(2)
            quant_transposes(pe, 0)
            scaled_to_rows(3)
            quant_transposes(pe, 1)
            products(0)
            products(1)
            quant_transposes(pe, 2)
            quant_transposes(pe, 3)
            products(2)
            products(3)
            for b in range(B):
                pe.wait_ge(Q["aa"], b + 1)
                if b >= 2:
                    pe.wait_ge(Q["aT"], b - 1)
                else:
                    pe.wait_ge(Q["q32"], B)
                for k in range(2):
                    last = nc.tensor.transpose(bank(2 + b % 2, P, k * P), aa[:, b, k, :], ident[:, :])
                last.then_inc(Q["atr"], 1)
            for b in range(B):
                pe.wait_ge(Xs["norm"], b + 1)
                if b >= 2:
                    pe.wait_ge(Xs["attT"], b - 1)
                for j in range(2):
                    for k in range(2):
                        last = nc.tensor.transpose(bank(4 + b % 2, P, j * S + k * P),
                                                   xP[:, b, k, j * P:(j + 1) * P], ident[:, :])
                last.then_inc(Xs["tr"], 1)
            for b in range(B):
                pe.wait_ge(Q["xw2"], b + 1)
                for w_ in range(2):
                    for k in range(2):
                        last = nc.tensor.transpose(bank(b, P, (2 * w_ + k) * P), xw2[:, b, w_, k * P:(k + 1) * P], ident[:, :])
                last.then_inc(Q["nat2"], 1)

            def products2(b):
                pe.wait_ge(Q["qT2"], b + 1)
                if b == 0:
                    pe.wait_ge(Q["q32b"], 2)
                elif b >= 2:
                    pe.wait_ge(Q["q32b"], b + 1)
                for k in range(2):
                    last = mm(bank(6 + b if b < 2 else b, D, k * D), qT[:, b, 0, 0, k * P:(k + 1) * P], qT[:, b, 1, 0, :],
                              start=True, stop=True)
                last.then_inc(y_ready, 1)
                if b >= 2:
                    pe.wait_ge(Q["wbc2"], b - 1)
                for k in range(2):
                    last = nc.tensor.transpose(bank(b % 2, P, k * P), rsc[:, b, 2 + k:3 + k].to_broadcast([P, P]), ident[:, :])
                last.then_inc(Q["wtr2"], 1)

            quant_transposes2(pe, 0)
            quant_transposes2(pe, 1)
            products2(0)
            products2(1)
            quant_transposes2(pe, 2)
            products2(2)
            transpose_x(2, 0, 2)
            quant_transposes2(pe, 3)

            def ffn_up(n):
                blk, f = n // FCH, n % FCH
                if f == 0:
                    pe.wait_ge(x_low, 2 * blk + 2)
                if n >= 2:
                    pe.wait_ge(Fs["gelu"], n - 1)
                else:
                    pe.wait_ge(Q["wbc2"], 3 + n)
                for i, part in enumerate((xH[2], xL[2])):
                    for c in range(DC):
                        last = mm(bank(n % 2), w1T[:, c, f * P:(f + 1) * P], part[:, c, blk * 512:(blk + 1) * 512],
                                  start=(i == 0 and c == 0), stop=(i == 1 and c == DC - 1))
                last.then_inc(Fs["up"], 1)

            def ffn_down(n):
                blk, f = n // FCH, n % FCH
                pe.wait_ge(Fs["parts"], n + 1)
                if n == 0:
                    pe.wait_ge(y_done, B)
                for k in range(4):
                    for i in range(2):
                        last = mm(bank(2 + 2 * blk + k // 2, D, (k % 2) * D), hP[:, n % 3, i, k * P:(k + 1) * P],
                                  w2T[:, f, :], start=(f == 0 and k % 2 == 0 and i == 0),
                                  stop=(f == FCH - 1 and k % 2 == 1 and i == 1))
                    if k == 3:
                        last.then_inc(Fs["down"], 1)

            for n in range(2 * FCH + 2):
                if n < 2 * FCH:
                    ffn_up(n)
                if n == 0:
                    products2(3)
                if n >= 2:
                    ffn_down(n - 2)
                if n == AT_XT:
                    transpose_x(2, 2, 4)
                if n == 2 * FCH:
                    transpose_x(3, 0, 2)
            project(1)
            attn_back(1)

            def logits(pair):
                pe.wait_ge(xT_ready, turned(5, 2 * pair + 1))
                for i in range(4):
                    tt = 4 * pair + i
                    for c in range(DC):
                        last = mm(bank(4 + 2 * pair, E, i * E), xT[:, c, tt * P:(tt + 1) * P], gwT[:, c, :],
                                  start=(c == 0), stop=(c == DC - 1))
                last.then_inc(Ms["logit"], 1)

            def combine(pair):
                pe.wait_ge(Ms["comb"], pair + 1)
                for i in range(4):
                    last = nc.tensor.transpose(bank(5 + 2 * pair, P, i * P),
                                               combw[:, 4 * pair + i].rearrange("p e i -> p (e i)"), ident[:, :])
                last.then_inc(Ms["ctr"], 1)

            def up(n):
                blk, c_ = n // EC, n % EC
                if n == 0:
                    pe.wait_ge(context_read, 2)
                elif n == 1:
                    copied_out(pe, len(G))
                if n >= 2:
                    pe.wait_ge(Ms["sg"], n - 1)
                    pe.wait_ge(Ms["um"], n - 1)
                pe.wait_ge(xT_ready, turned(5, 2 * blk + 1))
                for step in range(2):
                    if step == 1 and c_ == 0:
                        pe.wait_ge(x_low if blk else x_low0, B + 2 if blk else 2)
                    for gu in range(2):
                        for c in range(DC):
                            for i, (wp, xp) in enumerate(((mw1H, xH), (mw1L, xH)) if step == 0 else ((mw1H, xL),)):
                                last = mm(bank(2 * (n % 2) + gu), wp[c][:, gu, c_ * P:(c_ + 1) * P],
                                          xp[5][:, c, blk * 512:(blk + 1) * 512],
                                          start=(step == 0 and c == 0 and i == 0), stop=(step == 1 and c == DC - 1))
                last.then_inc(Ms["gu"], 1)

            def down(n, tiles=range(4)):
                blk, c_ = n // EC, n % EC
                pe.wait_ge(Ms["parts"], n + 1)
                if n == 0:
                    copied_out(pe, len(G))
                    pe.wait_ge(mw2_low, len(G) - NG2)
                if c_ == 0:
                    pe.wait_ge(Ms["GB"], blk + 1)
                for k in tiles:
                    for i, (part, wp) in enumerate(((0, mw2H), (0, mw2L), (1, mw2H))):
                        last = mm(bank(4 + 2 * blk + k // 2, D, (k % 2) * D), amP[:, n % 3, part, k * P:(k + 1) * P],
                                  wp[:, c_, :], start=(c_ == 0 and k % 2 == 0 and i == 0),
                                  stop=(c_ == EC - 1 and k % 2 == 1 and i == 2))
                last.then_inc(am_read if len(tiles) == 4 else last_outputs, 1)

            pe_groups(pe, NG2, len(G))
            transpose_x(5, 0, 2)
            up(0)
            logits(0)
            up(1)
            transpose_x(4, 2, 4)
            context(2)
            combine(0)
            context(3)
            for n in range(2, 2 * EC):
                up(n)
                down(n - 2)
                if n == AT_LOGITS - 1:
                    transpose_x(5, 2, 4)
                elif n == AT_LOGITS:
                    logits(1)
                if n == AT_COMBINE:
                    combine(1)
            for tiles in (range(0, 2), range(2, 4)):
                down(2 * EC - 2, tiles)
                down(2 * EC - 1, tiles)


def shape_constants():
    import numpy as np

    def bf16_bits(a):
        return (np.ascontiguousarray(a, np.float32).view(np.uint32) >> 16).astype(np.uint16)

    s, hd = 256, 16
    i = np.arange(s)[:, None]
    j = np.arange(s)[None, :]
    causal = j <= i
    window = (causal & (j >= i - 63)) | ((j < 4) & causal)
    m = np.zeros((128, 2, 768), np.float32)
    for n, ok in enumerate((causal, window)):
        f = np.where(ok, 0.0, -1e30).astype(np.float32)
        m[:, n, 0:128] = f[0:128, 0:128]
        m[:, n, 128:384] = f[128:256, :]
        m[:, n, 384:640] = f[:, 0:128].T
        m[:, n, 640:768] = f[128:256, 128:256].T
    inv = 1.0 / 10000.0 ** (np.arange(0, hd, 2, dtype=np.float32) / hd)
    fr = np.outer(np.arange(s, dtype=np.float32), inv.astype(np.float32)).astype(np.float32)
    c, sn = np.cos(fr).astype(np.float32), np.sin(fr).astype(np.float32)
    r = np.stack([np.concatenate([c, c], 1), np.concatenate([sn, -sn], 1)], 1)
    r = np.ascontiguousarray(r.reshape(2, 128, 2, hd).transpose(1, 0, 2, 3))
    return {
        "ident": np.eye(128, dtype=np.float32),
        "ident16": bf16_bits(np.eye(128)),
        "masks": bf16_bits(m),
        "rope": r,
        "order": np.tile(np.arange(8, 0, -1, dtype=np.float32), (128, 1)),
    }


def kernel(**inputs):
    import numpy as np
    import concourse.bacc as bacc
    from concourse import mybir as mb
    from concourse.bass_utils import run_bass_kernel_spmd

    nc = bacc.Bacc("TRN2", target_bir_lowering=False, num_devices=1)
    arrays, args = {}, {}
    named = {k: np.asarray(v) for k, v in inputs.items()}
    named["b1_cols"] = np.ascontiguousarray(named.pop("L0_ffn_b1").reshape(8, 128).T)
    named.update(shape_constants())
    for name, a in named.items():
        a = np.ascontiguousarray(a)
        arrays[f"in_{name}"] = a
        args[name] = nc.dram_tensor(f"in_{name}", a.shape, mb.dt.from_np(a.dtype), kind="ExternalInput").ap()
    out = nc.dram_tensor("out_0", (4, 256, 256), mb.dt.float32, kind="ExternalOutput").ap()
    post_ln_decoder_two_layers(nc, args, out)
    r = run_bass_kernel_spmd(nc, [arrays], core_ids=[0])
    return r.results[0]["out_0"]
```
